# Optimizing a Trainium2 kernel written in Bass

```python
import numpy as np
import jax
import jax.numpy as jnp

def _softmax(x, axis=-1):
    return jax.nn.softmax(x, axis=axis)

def _gelu(x):
    return jax.nn.gelu(x, approximate=True)

def _silu(x):
    return jax.nn.silu(x)

def _sigmoid(x):
    return jax.nn.sigmoid(x)

def _layernorm(x, axis=-1, eps=1e-05):
    m = jnp.mean(x, axis=axis, keepdims=True)
    v = jnp.var(x, axis=axis, keepdims=True)
    return (x - m) / jnp.sqrt(v + eps)

def _scatter_add(tgt, idx, src, axis=0):
    return tgt.at[idx].add(src)

def _segment_sum(src, seg, n):
    return jax.ops.segment_sum(src, seg, n)
kernel_name = 'mk_xattn_ffn_d4_seqx_r8_607daa'

def setup_inputs(seed: int=0):
    np.random.seed(seed)
    _w = jnp.asarray

    def _rec_inputs():
        import jax
        import jax.numpy as jnp
        _rk = jax.random.key(seed)
        x = 7.22e-05 + 1 * jax.random.normal(jax.random.fold_in(_rk, 1), (4, 256, 256), jnp.float32)
        _lenS = 256 - jax.random.randint(jax.random.fold_in(_rk, 7), (4,), 0, max(1, 256 // 4) + 1, jnp.int32)
        _lenS2 = 64 - jax.random.randint(jax.random.fold_in(_rk, 8), (4,), 0, max(1, 64 // 4) + 1, jnp.int32)
        _ctx_512P = jax.random.normal(jax.random.fold_in(_rk, 11), (4, 16, 64), jnp.float32)
        _ctx_512c = jax.random.dirichlet(jax.random.fold_in(_rk, 511), 0.3 * jnp.ones((16,), jnp.float32), (4, 64))
        _ctx_512t = jnp.einsum('bsk,bkd->bsd', _ctx_512c, _ctx_512P)
        _ctx_512t = _ctx_512t * jax.lax.rsqrt(jnp.mean(jnp.square(_ctx_512t)) + 1e-12) * 0.953939
        ctx_512 = -0.000514642 + 1.00011 * (_ctx_512t + 0.3 * jax.random.normal(jax.random.fold_in(_rk, 611), (4, 64, 64), jnp.float32))
        return (x, ctx_512)
    x, ctx_512 = _rec_inputs()

    def _L0_xattn_setup():
        import jax, jax.numpy as jnp
        import numpy as np
        B, S, H, NH, L = (2, 256, 256, 16, 64)
        HD = H // NH
        key = jax.random.key(seed)
        k1, k2, k3, k4, k5 = jax.random.split(key, 5)
        scale = 0.02
        return {'q': jax.random.normal(k1, (B, S, H), dtype=jnp.float32), 'latent_kv': jax.random.normal(k2, (B, S, L), dtype=jnp.float32), 'Wq': jax.random.normal(k3, (H, H), dtype=jnp.float32) * scale, 'Wkv_expand': jax.random.normal(k4, (2 * H, L), dtype=jnp.float32) * scale, 'Wout': jax.random.normal(k5, (H, H), dtype=jnp.float32) * scale}
    _L0_xattn_all = _L0_xattn_setup()
    _L0_xattn_in = {k: v for k, v in _L0_xattn_all.items() if k in ('Wq', 'Wkv_expand', 'Wout')}
    del _L0_xattn_all

    def _L0_ffn_setup():
        import jax, jax.numpy as jnp
        import numpy as np
        B, T, D, FF = (4, 256, 256, 704)
        EPS = 1e-06

        def rmsnorm(x, w):
            var = jnp.mean(jnp.square(x), axis=-1, keepdims=True)
            return x * jax.lax.rsqrt(var + EPS) * w
        key = jax.random.key(seed)
        ks = jax.random.split(key, 9)
        s = 0.02
        return {'hidden_states': jax.random.normal(ks[0], (B, T, D), jnp.float32), 'w_router': jax.random.normal(ks[1], (D,), jnp.float32) * s, 'b_router': jnp.zeros((), jnp.float32), 'norm1_w': jnp.ones((D,), jnp.float32), 'wv': jax.random.normal(ks[2], (D, D), jnp.float32) * s, 'bv': jnp.zeros((D,), jnp.float32), 'wo': jax.random.normal(ks[3], (D, D), jnp.float32) * s, 'norm2_w': jnp.ones((D,), jnp.float32), 'w_gate': jax.random.normal(ks[4], (D, FF), jnp.float32) * s, 'w_up': jax.random.normal(ks[5], (D, FF), jnp.float32) * s, 'w_down': jax.random.normal(ks[6], (FF, D), jnp.float32) * s}
    _L0_ffn_all = _L0_ffn_setup()
    _L0_ffn_in = {k: v for k, v in _L0_ffn_all.items() if k in ('w_router', 'b_router', 'norm1_w', 'wv', 'bv', 'wo', 'norm2_w', 'w_gate', 'w_up', 'w_down')}
    del _L0_ffn_all

    def _L1_xattn_setup():
        import jax, jax.numpy as jnp
        import numpy as np
        B, S, L = (2, 128, 128)
        DIM_Q, H, K, D_C, D_CQ, R = (256, 16, 128, 64, 192, 64)

        def _rope_tables(length, dim):
            inv = 1.0 / 10000.0 ** (jnp.arange(0, dim, 2, dtype=jnp.float32) / dim)
            f = jnp.arange(length, dtype=jnp.float32)[:, None] * inv[None, :]
            sin = jnp.repeat(jnp.sin(f), 2, axis=-1)
            cos = jnp.repeat(jnp.cos(f), 2, axis=-1)
            return (sin, cos)

        def _rotate_half(x):
            half = x.shape[-1] // 2
            return jnp.concatenate([-x[..., half:], x[..., :half]], axis=-1)

        def _apply_rope(x, sin, cos):
            return x * cos + _rotate_half(x) * sin
        key = jax.random.key(seed)
        ks = jax.random.split(key, 8)
        return {'hidden_q': jax.random.normal(ks[0], (B, S, DIM_Q), jnp.float32), 'kv_c': jax.random.normal(ks[1], (B, L, D_C), jnp.float32), 'Wq': jax.random.normal(ks[2], (H * K, DIM_Q), jnp.float32) / np.sqrt(DIM_Q).astype(np.float32), 'w_kc_q': jax.random.normal(ks[3], (H, K, D_CQ), jnp.float32) / np.sqrt(K).astype(np.float32), 'w_kc_kv': jax.random.normal(ks[4], (H, K, D_C), jnp.float32) / np.sqrt(K).astype(np.float32), 'W_qr': jax.random.normal(ks[5], (H, D_CQ, R), jnp.float32) / np.float32(np.sqrt(D_CQ) * np.sqrt(R)), 'W_kr': jax.random.normal(ks[6], (H, D_C, R), jnp.float32) / np.sqrt(D_C).astype(np.float32), 'Wo': jax.random.normal(ks[7], (DIM_Q, H * K), jnp.float32) / np.sqrt(H * K).astype(np.float32)}
    _L1_xattn_all = _L1_xattn_setup()
    _L1_xattn_in = {k: v for k, v in _L1_xattn_all.items() if k in ('Wq', 'w_kc_q', 'w_kc_kv', 'W_qr', 'W_kr', 'Wo')}
    del _L1_xattn_all

    def _L1_ffn_setup():
        import jax, jax.numpy as jnp
        import numpy as np
        from jax import lax
        B, S, H = (1, 256, 256)
        E, I, TOP_K = (64, 64, 8)
        SHARED_I = 64
        key = jax.random.key(seed)
        ks = jax.random.split(key, 8)
        sc = 0.02
        return {'hidden_states': jax.random.normal(ks[0], (B, S, H), jnp.float32), 'router_w': jax.random.normal(ks[1], (E, H), jnp.float32) * sc, 'gate_up_proj': jax.random.normal(ks[2], (E, 2 * I, H), jnp.float32) * sc, 'down_proj': jax.random.normal(ks[3], (E, H, I), jnp.float32) * sc, 'shared_gate_w': jax.random.normal(ks[4], (SHARED_I, H), jnp.float32) * sc, 'shared_up_w': jax.random.normal(ks[5], (SHARED_I, H), jnp.float32) * sc, 'shared_down_w': jax.random.normal(ks[6], (H, SHARED_I), jnp.float32) * sc, 'shared_expert_gate_w': jax.random.normal(ks[7], (1, H), jnp.float32) * sc}
    _L1_ffn_all = _L1_ffn_setup()
    _L1_ffn_in = {k: v for k, v in _L1_ffn_all.items() if k in ('router_w', 'gate_up_proj', 'down_proj', 'shared_gate_w', 'shared_up_w', 'shared_down_w', 'shared_expert_gate_w')}
    del _L1_ffn_all

    def _L2_xattn_setup():
        import jax, jax.numpy as jnp
        import numpy as np
        B, S, L = (2, 128, 128)
        DIM_Q, H, K, D_C, D_CQ, R = (256, 16, 128, 64, 192, 64)

        def _rope_tables(seq_len, dim, dtype):
            inv_freq = 1.0 / 10000.0 ** (jnp.arange(0, dim, 2, dtype=dtype) / dim)
            t = jnp.arange(seq_len, dtype=dtype)
            freqs = t[:, None] * inv_freq[None, :]
            sin = jnp.repeat(jnp.sin(freqs), 2, axis=-1)
            cos = jnp.repeat(jnp.cos(freqs), 2, axis=-1)
            return (sin, cos)

        def _rotate_half(x):
            h = x.shape[-1] // 2
            return jnp.concatenate([-x[..., h:], x[..., :h]], axis=-1)
        key = jax.random.key(seed)
        ks = jax.random.split(key, 8)
        s_in = 1.0 / np.sqrt(DIM_Q)
        s_k = 1.0 / np.sqrt(K)
        s_cq = 1.0 / np.sqrt(D_CQ)
        s_c = 1.0 / np.sqrt(D_C)
        return {'hidden_q': jax.random.normal(ks[0], (B, S, DIM_Q), jnp.float32), 'kv_c': jax.random.normal(ks[1], (B, L, D_C), jnp.float32), 'Wq': jax.random.normal(ks[2], (H * K, DIM_Q), jnp.float32) * s_in, 'w_kc_q': jax.random.normal(ks[3], (H, K, D_CQ), jnp.float32) * s_k, 'w_kc_kv': jax.random.normal(ks[4], (H, K, D_C), jnp.float32) * s_k, 'W_qr': jax.random.normal(ks[5], (H, D_CQ, R), jnp.float32) * s_cq / np.sqrt(R), 'W_kr': jax.random.normal(ks[6], (H, D_C, R), jnp.float32) * s_c, 'Wo': jax.random.normal(ks[7], (DIM_Q, H * K), jnp.float32) * s_k}
    _L2_xattn_all = _L2_xattn_setup()
    _L2_xattn_in = {k: v for k, v in _L2_xattn_all.items() if k in ('Wq', 'w_kc_q', 'w_kc_kv', 'W_qr', 'W_kr', 'Wo')}
    del _L2_xattn_all

    def _L2_ffn_setup():
        import jax, jax.numpy as jnp
        import numpy as np
        HID = 256
        N_HEADS = 16
        N_KV = 16
        HEAD_DIM = HID // N_HEADS
        N_EXP = 8
        TOP_K = 2
        MOE_I = 176
        SH_I = 704
        EPS = 1e-06
        ROPE_THETA = 1000000.0

        def _rms(x, w):
            v = jnp.mean(jnp.square(x), axis=-1, keepdims=True)
            return x * jax.lax.rsqrt(v + EPS) * w

        def _rope(q, k):
            S, D = (q.shape[1], q.shape[-1])
            inv = 1.0 / ROPE_THETA ** (jnp.arange(0, D, 2, dtype=jnp.float32) / D)
            freqs = jnp.arange(S, dtype=jnp.float32)[:, None] * inv[None, :]
            emb = jnp.concatenate([freqs, freqs], axis=-1)
            cos = jnp.cos(emb)[None, :, None, :]
            sin = jnp.sin(emb)[None, :, None, :]

            def rot(t):
                t1, t2 = (t[..., :D // 2], t[..., D // 2:])
                return jnp.concatenate([-t2, t1], axis=-1)
            return (q * cos + rot(q) * sin, k * cos + rot(k) * sin)
        key = jax.random.key(seed)
        ks = jax.random.split(key, 20)
        s = 0.02
        d = {'x': jax.random.normal(ks[0], (2, 128, HID), jnp.float32), 'w_ln1': jnp.ones((HID,), jnp.float32), 'wq': jax.random.normal(ks[1], (HID, N_HEADS * HEAD_DIM), jnp.float32) * s, 'bq': jnp.zeros((N_HEADS * HEAD_DIM,), jnp.float32), 'wk': jax.random.normal(ks[2], (HID, N_KV * HEAD_DIM), jnp.float32) * s, 'bk': jnp.zeros((N_KV * HEAD_DIM,), jnp.float32), 'wv': jax.random.normal(ks[3], (HID, N_KV * HEAD_DIM), jnp.float32) * s, 'bv': jnp.zeros((N_KV * HEAD_DIM,), jnp.float32), 'wo': jax.random.normal(ks[4], (N_HEADS * HEAD_DIM, HID), jnp.float32) * s, 'w_ln2': jnp.ones((HID,), jnp.float32), 'w_router': jax.random.normal(ks[5], (HID, N_EXP), jnp.float32) * s, 'w_gate_e': jax.random.normal(ks[6], (N_EXP, HID, MOE_I), jnp.float32) * s, 'w_up_e': jax.random.normal(ks[7], (N_EXP, HID, MOE_I), jnp.float32) * s, 'w_down_e': jax.random.normal(ks[8], (N_EXP, MOE_I, HID), jnp.float32) * s, 'w_sh_gate': jax.random.normal(ks[9], (HID, SH_I), jnp.float32) * s, 'w_sh_up': jax.random.normal(ks[10], (HID, SH_I), jnp.float32) * s, 'w_sh_down': jax.random.normal(ks[11], (SH_I, HID), jnp.float32) * s, 'w_sh_eg': jax.random.normal(ks[12], (HID, 1), jnp.float32) * s}
        return d
    _L2_ffn_all = _L2_ffn_setup()
    _L2_ffn_in = {k: v for k, v in _L2_ffn_all.items() if k in ('w_ln1', 'wq', 'bq', 'wk', 'bk', 'wv', 'bv', 'wo', 'w_ln2', 'w_router', 'w_gate_e', 'w_up_e', 'w_down_e', 'w_sh_gate', 'w_sh_up', 'w_sh_down', 'w_sh_eg')}
    del _L2_ffn_all

    def _L3_xattn_setup():
        import jax, jax.numpy as jnp
        import numpy as np
        B, S, H, NH, L = (2, 256, 256, 16, 64)
        HD = H // NH
        key = jax.random.key(seed)
        k1, k2, k3, k4, k5 = jax.random.split(key, 5)
        scale = 0.02
        return {'q': jax.random.normal(k1, (B, S, H), dtype=jnp.float32), 'latent_kv': jax.random.normal(k2, (B, S, L), dtype=jnp.float32), 'Wq': jax.random.normal(k3, (H, H), dtype=jnp.float32) * scale, 'Wkv_expand': jax.random.normal(k4, (2 * H, L), dtype=jnp.float32) * scale, 'Wout': jax.random.normal(k5, (H, H), dtype=jnp.float32) * scale}
    _L3_xattn_all = _L3_xattn_setup()
    _L3_xattn_in = {k: v for k, v in _L3_xattn_all.items() if k in ('Wq', 'Wkv_expand', 'Wout')}
    del _L3_xattn_all

    def _L3_ffn_setup():
        import jax, jax.numpy as jnp
        import numpy as np
        TOP_K = 4
        key = jax.random.key(seed)
        ks = jax.random.split(key, 9)
        B, T, D, H, NE = (2, 128, 256, 176, 16)
        s = 0.02
        return {'x': jax.random.normal(ks[0], (B, T, D), jnp.float32), 'gate_w': jax.random.normal(ks[1], (NE, D), jnp.float32) * s, 'gate_b': jax.random.normal(ks[2], (NE,), jnp.float32) * s, 'w1_shared': jax.random.normal(ks[3], (D, H), jnp.float32) * s, 'w2_shared': jax.random.normal(ks[4], (H, D), jnp.float32) * s, 'w3_shared': jax.random.normal(ks[5], (D, H), jnp.float32) * s, 'w1_routed': jax.random.normal(ks[6], (NE, D, H), jnp.float32) * s, 'w2_routed': jax.random.normal(ks[7], (NE, H, D), jnp.float32) * s, 'w3_routed': jax.random.normal(ks[8], (NE, D, H), jnp.float32) * s}
    _L3_ffn_all = _L3_ffn_setup()
    _L3_ffn_in = {k: v for k, v in _L3_ffn_all.items() if k in ('gate_w', 'gate_b', 'w1_shared', 'w2_shared', 'w3_shared', 'w1_routed', 'w2_routed', 'w3_routed')}
    del _L3_ffn_all
    return {'x': x, 'ctx_512': ctx_512, 'L0_xattn_Wq': _L0_xattn_in['Wq'], 'L0_xattn_Wkv_expand': _L0_xattn_in['Wkv_expand'], 'L0_xattn_Wout': _L0_xattn_in['Wout'], 'L0_ffn_w_router': _L0_ffn_in['w_router'], 'L0_ffn_b_router': _L0_ffn_in['b_router'], 'L0_ffn_norm1_w': _L0_ffn_in['norm1_w'], 'L0_ffn_wv': _L0_ffn_in['wv'], 'L0_ffn_bv': _L0_ffn_in['bv'], 'L0_ffn_wo': _L0_ffn_in['wo'], 'L0_ffn_norm2_w': _L0_ffn_in['norm2_w'], 'L0_ffn_w_gate': _L0_ffn_in['w_gate'], 'L0_ffn_w_up': _L0_ffn_in['w_up'], 'L0_ffn_w_down': _L0_ffn_in['w_down'], 'L1_xattn_Wq': _L1_xattn_in['Wq'], 'L1_xattn_w_kc_q': _L1_xattn_in['w_kc_q'], 'L1_xattn_w_kc_kv': _L1_xattn_in['w_kc_kv'], 'L1_xattn_W_qr': _L1_xattn_in['W_qr'], 'L1_xattn_W_kr': _L1_xattn_in['W_kr'], 'L1_xattn_Wo': _L1_xattn_in['Wo'], 'L1_ffn_router_w': _L1_ffn_in['router_w'], 'L1_ffn_gate_up_proj': _L1_ffn_in['gate_up_proj'], 'L1_ffn_down_proj': _L1_ffn_in['down_proj'], 'L1_ffn_shared_gate_w': _L1_ffn_in['shared_gate_w'], 'L1_ffn_shared_up_w': _L1_ffn_in['shared_up_w'], 'L1_ffn_shared_down_w': _L1_ffn_in['shared_down_w'], 'L1_ffn_shared_expert_gate_w': _L1_ffn_in['shared_expert_gate_w'], 'L2_xattn_Wq': _L2_xattn_in['Wq'], 'L2_xattn_w_kc_q': _L2_xattn_in['w_kc_q'], 'L2_xattn_w_kc_kv': _L2_xattn_in['w_kc_kv'], 'L2_xattn_W_qr': _L2_xattn_in['W_qr'], 'L2_xattn_W_kr': _L2_xattn_in['W_kr'], 'L2_xattn_Wo': _L2_xattn_in['Wo'], 'L2_ffn_w_ln1': _L2_ffn_in['w_ln1'], 'L2_ffn_wq': _L2_ffn_in['wq'], 'L2_ffn_bq': _L2_ffn_in['bq'], 'L2_ffn_wk': _L2_ffn_in['wk'], 'L2_ffn_bk': _L2_ffn_in['bk'], 'L2_ffn_wv': _L2_ffn_in['wv'], 'L2_ffn_bv': _L2_ffn_in['bv'], 'L2_ffn_wo': _L2_ffn_in['wo'], 'L2_ffn_w_ln2': _L2_ffn_in['w_ln2'], 'L2_ffn_w_router': _L2_ffn_in['w_router'], 'L2_ffn_w_gate_e': _L2_ffn_in['w_gate_e'], 'L2_ffn_w_up_e': _L2_ffn_in['w_up_e'], 'L2_ffn_w_down_e': _L2_ffn_in['w_down_e'], 'L2_ffn_w_sh_gate': _L2_ffn_in['w_sh_gate'], 'L2_ffn_w_sh_up': _L2_ffn_in['w_sh_up'], 'L2_ffn_w_sh_down': _L2_ffn_in['w_sh_down'], 'L2_ffn_w_sh_eg': _L2_ffn_in['w_sh_eg'], 'L3_xattn_Wq': _L3_xattn_in['Wq'], 'L3_xattn_Wkv_expand': _L3_xattn_in['Wkv_expand'], 'L3_xattn_Wout': _L3_xattn_in['Wout'], 'L3_ffn_gate_w': _L3_ffn_in['gate_w'], 'L3_ffn_gate_b': _L3_ffn_in['gate_b'], 'L3_ffn_w1_shared': _L3_ffn_in['w1_shared'], 'L3_ffn_w2_shared': _L3_ffn_in['w2_shared'], 'L3_ffn_w3_shared': _L3_ffn_in['w3_shared'], 'L3_ffn_w1_routed': _L3_ffn_in['w1_routed'], 'L3_ffn_w2_routed': _L3_ffn_in['w2_routed'], 'L3_ffn_w3_routed': _L3_ffn_in['w3_routed']}

def reference(x, ctx_512, L0_xattn_Wq, L0_xattn_Wkv_expand, L0_xattn_Wout, L0_ffn_w_router, L0_ffn_b_router, L0_ffn_norm1_w, L0_ffn_wv, L0_ffn_bv, L0_ffn_wo, L0_ffn_norm2_w, L0_ffn_w_gate, L0_ffn_w_up, L0_ffn_w_down, L1_xattn_Wq, L1_xattn_w_kc_q, L1_xattn_w_kc_kv, L1_xattn_W_qr, L1_xattn_W_kr, L1_xattn_Wo, L1_ffn_router_w, L1_ffn_gate_up_proj, L1_ffn_down_proj, L1_ffn_shared_gate_w, L1_ffn_shared_up_w, L1_ffn_shared_down_w, L1_ffn_shared_expert_gate_w, L2_xattn_Wq, L2_xattn_w_kc_q, L2_xattn_w_kc_kv, L2_xattn_W_qr, L2_xattn_W_kr, L2_xattn_Wo, L2_ffn_w_ln1, L2_ffn_wq, L2_ffn_bq, L2_ffn_wk, L2_ffn_bk, L2_ffn_wv, L2_ffn_bv, L2_ffn_wo, L2_ffn_w_ln2, L2_ffn_w_router, L2_ffn_w_gate_e, L2_ffn_w_up_e, L2_ffn_w_down_e, L2_ffn_w_sh_gate, L2_ffn_w_sh_up, L2_ffn_w_sh_down, L2_ffn_w_sh_eg, L3_xattn_Wq, L3_xattn_Wkv_expand, L3_xattn_Wout, L3_ffn_gate_w, L3_ffn_gate_b, L3_ffn_w1_shared, L3_ffn_w2_shared, L3_ffn_w3_shared, L3_ffn_w1_routed, L3_ffn_w2_routed, L3_ffn_w3_routed):
    import jax
    import jax.numpy as jnp

    def _L0_xattn_ref(q, latent_kv, Wq, Wkv_expand, Wout):
        import jax, jax.numpy as jnp
        import numpy as np
        B, S, H, NH, L = (2, 256, 256, 16, 64)
        HD = H // NH
        b, sq, _ = q.shape
        sk = latent_kv.shape[1]
        qp = q @ Wq.T
        kv = latent_kv @ Wkv_expand.T
        k, v = jnp.split(kv, 2, axis=-1)
        qh = qp.reshape(b, sq, NH, HD).transpose(0, 2, 1, 3)
        kh = k.reshape(b, sk, NH, HD).transpose(0, 2, 1, 3)
        vh = v.reshape(b, sk, NH, HD).transpose(0, 2, 1, 3)
        inv_sqrt_d = 1.0 / jnp.sqrt(jnp.float32(HD))
        scores = jnp.einsum('bhqd,bhkd->bhqk', qh, kh) * inv_sqrt_d
        causal = jnp.tril(jnp.ones((sq, sk), dtype=bool))
        scores = jnp.where(causal, scores, jnp.finfo(scores.dtype).min)
        attn = jax.nn.softmax(scores, axis=-1)
        out = jnp.einsum('bhqk,bhkd->bhqd', attn, vh)
        out = out.transpose(0, 2, 1, 3).reshape(b, sq, H)
        return out @ Wout.T

    def _L0_ffn_ref(hidden_states, w_router, b_router, norm1_w, wv, bv, wo, norm2_w, w_gate, w_up, w_down):
        import jax, jax.numpy as jnp
        import numpy as np
        B, T, D, FF = (4, 256, 256, 704)
        EPS = 1e-06

        def rmsnorm(x, w):
            var = jnp.mean(jnp.square(x), axis=-1, keepdims=True)
            return x * jax.lax.rsqrt(var + EPS) * w
        x = hidden_states
        scores = jnp.einsum('btd,d->bt', x, w_router) + b_router
        routed = jax.nn.sigmoid(scores) > 0.5
        h1 = rmsnorm(x, norm1_w)
        v = jnp.einsum('btd,de->bte', h1, wv) + bv
        attn = jnp.einsum('bte,ed->btd', v, wo)
        h = x + attn
        h2 = rmsnorm(h, norm2_w)
        mlp = jnp.einsum('btf,fd->btd', jax.nn.silu(h2 @ w_gate) * (h2 @ w_up), w_down)
        processed = h + mlp
        return jnp.where(routed[..., None], processed, x)

    def _L1_xattn_ref(hidden_q, kv_c, Wq, w_kc_q, w_kc_kv, W_qr, W_kr, Wo):
        import jax, jax.numpy as jnp
        import numpy as np
        B, S, L = (2, 128, 128)
        DIM_Q, H, K, D_C, D_CQ, R = (256, 16, 128, 64, 192, 64)

        def _rope_tables(length, dim):
            inv = 1.0 / 10000.0 ** (jnp.arange(0, dim, 2, dtype=jnp.float32) / dim)
            f = jnp.arange(length, dtype=jnp.float32)[:, None] * inv[None, :]
            sin = jnp.repeat(jnp.sin(f), 2, axis=-1)
            cos = jnp.repeat(jnp.cos(f), 2, axis=-1)
            return (sin, cos)

        def _rotate_half(x):
            half = x.shape[-1] // 2
            return jnp.concatenate([-x[..., half:], x[..., :half]], axis=-1)

        def _apply_rope(x, sin, cos):
            return x * cos + _rotate_half(x) * sin
        Bv, Sv, _ = hidden_q.shape
        _, Lv, _ = kv_c.shape
        q_hk = (hidden_q @ Wq.T).reshape(Bv, Sv, H, K)
        q_big = jnp.einsum('bshk,hkq->bshq', q_hk, w_kc_q)
        sin_q, cos_q = _rope_tables(Sv, D_CQ)
        q_big = _apply_rope(q_big, sin_q[None, :, None, :], cos_q[None, :, None, :])
        sin_k, cos_k = _rope_tables(Lv, D_C)
        kv_r = _apply_rope(kv_c, sin_k[None], cos_k[None])
        q_r = jnp.einsum('bshq,hqr->bhsr', q_big, W_qr)
        k_r = jnp.einsum('bld,hdr->bhlr', kv_r, W_kr)
        scores = jnp.einsum('bhsr,bhlr->bhsl', q_r, k_r)
        attn = jax.nn.softmax(scores, axis=-1)
        ctx_c = jnp.einsum('bhsl,bld->bhsd', attn, kv_r)
        ctx_lat = jnp.einsum('bhsd,hkd->bhsk', ctx_c, w_kc_kv)
        ctx = ctx_lat.transpose(0, 2, 1, 3).reshape(Bv, Sv, H * K)
        return ctx @ Wo.T

    def _L1_ffn_ref(hidden_states, router_w, gate_up_proj, down_proj, shared_gate_w, shared_up_w, shared_down_w, shared_expert_gate_w):
        import jax, jax.numpy as jnp
        import numpy as np
        from jax import lax
        B, S, H = (1, 256, 256)
        E, I, TOP_K = (64, 64, 8)
        SHARED_I = 64
        b, s, h_dim = hidden_states.shape
        h = hidden_states.reshape(-1, h_dim)
        T = h.shape[0]
        shared = jnp.dot(jax.nn.silu(jnp.dot(h, shared_gate_w.T)) * jnp.dot(h, shared_up_w.T), shared_down_w.T)
        shared = jax.nn.sigmoid(jnp.dot(h, shared_expert_gate_w.T)) * shared
        logits = jnp.dot(h, router_w.T)
        probs = jax.nn.softmax(logits.astype(jnp.float32), axis=-1)
        top_vals, top_idx = lax.top_k(probs, TOP_K)
        top_vals = top_vals / jnp.sum(top_vals, axis=-1, keepdims=True)
        top_vals = top_vals.astype(h.dtype)
        comb = jnp.zeros((T, E), h.dtype).at[jnp.arange(T)[:, None], top_idx].add(top_vals)

        def body(acc, xs):
            wgu, wd, w_e = xs
            g, u = jnp.split(jnp.dot(h, wgu.T), 2, axis=-1)
            eo = jnp.dot(jax.nn.silu(g) * u, wd.T)
            return (acc + eo * w_e[:, None], None)
        expert_out, _ = lax.scan(body, jnp.zeros_like(h), (gate_up_proj, down_proj, comb.T))
        return (expert_out + shared).reshape(b, s, h_dim)

    def _L2_xattn_ref(hidden_q, kv_c, Wq, w_kc_q, w_kc_kv, W_qr, W_kr, Wo):
        import jax, jax.numpy as jnp
        import numpy as np
        B, S, L = (2, 128, 128)
        DIM_Q, H, K, D_C, D_CQ, R = (256, 16, 128, 64, 192, 64)

        def _rope_tables(seq_len, dim, dtype):
            inv_freq = 1.0 / 10000.0 ** (jnp.arange(0, dim, 2, dtype=dtype) / dim)
            t = jnp.arange(seq_len, dtype=dtype)
            freqs = t[:, None] * inv_freq[None, :]
            sin = jnp.repeat(jnp.sin(freqs), 2, axis=-1)
            cos = jnp.repeat(jnp.cos(freqs), 2, axis=-1)
            return (sin, cos)

        def _rotate_half(x):
            h = x.shape[-1] // 2
            return jnp.concatenate([-x[..., h:], x[..., :h]], axis=-1)
        b, s, _ = hidden_q.shape
        l = kv_c.shape[1]
        q_hk = (hidden_q @ Wq.T).reshape(b, s, H, K)
        q_big = jnp.einsum('bshk,hkq->bshq', q_hk, w_kc_q)
        sin, cos = _rope_tables(l, D_C, kv_c.dtype)
        kv_rope = kv_c * cos[None] + _rotate_half(kv_c) * sin[None]
        q_r = jnp.einsum('bshq,hqr->bhsr', q_big, W_qr)
        k_r = jnp.einsum('bld,hdr->bhlr', kv_rope, W_kr)
        scores = jnp.einsum('bhsr,bhlr->bhsl', q_r, k_r)
        attn = jax.nn.softmax(scores, axis=-1)
        ctx_c = jnp.einsum('bhsl,bld->bhsd', attn, kv_rope)
        ctx_lat = jnp.einsum('bhsd,hkd->bshk', ctx_c, w_kc_kv)
        out = ctx_lat.reshape(b, s, H * K) @ Wo.T
        return out

    def _L2_ffn_ref(x, w_ln1, wq, bq, wk, bk, wv, bv, wo, w_ln2, w_router, w_gate_e, w_up_e, w_down_e, w_sh_gate, w_sh_up, w_sh_down, w_sh_eg):
        import jax, jax.numpy as jnp
        import numpy as np
        HID = 256
        N_HEADS = 16
        N_KV = 16
        HEAD_DIM = HID // N_HEADS
        N_EXP = 8
        TOP_K = 2
        MOE_I = 176
        SH_I = 704
        EPS = 1e-06
        ROPE_THETA = 1000000.0

        def _rms(x, w):
            v = jnp.mean(jnp.square(x), axis=-1, keepdims=True)
            return x * jax.lax.rsqrt(v + EPS) * w

        def _rope(q, k):
            S, D = (q.shape[1], q.shape[-1])
            inv = 1.0 / ROPE_THETA ** (jnp.arange(0, D, 2, dtype=jnp.float32) / D)
            freqs = jnp.arange(S, dtype=jnp.float32)[:, None] * inv[None, :]
            emb = jnp.concatenate([freqs, freqs], axis=-1)
            cos = jnp.cos(emb)[None, :, None, :]
            sin = jnp.sin(emb)[None, :, None, :]

            def rot(t):
                t1, t2 = (t[..., :D // 2], t[..., D // 2:])
                return jnp.concatenate([-t2, t1], axis=-1)
            return (q * cos + rot(q) * sin, k * cos + rot(k) * sin)
        B, S, H = x.shape
        h = _rms(x, w_ln1)
        q = (h @ wq + bq).reshape(B, S, N_HEADS, HEAD_DIM)
        k = (h @ wk + bk).reshape(B, S, N_KV, HEAD_DIM)
        v = (h @ wv + bv).reshape(B, S, N_KV, HEAD_DIM)
        q, k = _rope(q, k)
        rep = N_HEADS // N_KV
        if rep > 1:
            k = jnp.repeat(k, rep, axis=2)
            v = jnp.repeat(v, rep, axis=2)
        scores = jnp.einsum('bqhd,bkhd->bhqk', q, k) * HEAD_DIM ** (-0.5)
        causal = jnp.tril(jnp.ones((S, S), bool))
        scores = jnp.where(causal[None, None], scores, jnp.finfo(scores.dtype).min)
        attn = jax.nn.softmax(scores, axis=-1)
        ctx = jnp.einsum('bhqk,bkhd->bqhd', attn, v).reshape(B, S, N_HEADS * HEAD_DIM)
        x = x + ctx @ wo
        h = _rms(x, w_ln2).reshape(B * S, H)
        logits = h @ w_router
        probs = jax.nn.softmax(logits, axis=-1)
        top_w, top_i = jax.lax.top_k(probs, TOP_K)
        combine = jnp.sum(jax.nn.one_hot(top_i, N_EXP, dtype=h.dtype) * top_w[..., None], axis=1)
        g = jnp.einsum('th,ehi->eti', h, w_gate_e)
        u = jnp.einsum('th,ehi->eti', h, w_up_e)
        y = jnp.einsum('eti,eih->eth', jax.nn.silu(g) * u, w_down_e)
        routed = jnp.einsum('eth,te->th', y, combine)
        sh = jax.nn.silu(h @ w_sh_gate) * (h @ w_sh_up) @ w_sh_down
        sh = sh * jax.nn.sigmoid(h @ w_sh_eg)
        x = x + (routed + sh).reshape(B, S, H)
        return x

    def _L3_xattn_ref(q, latent_kv, Wq, Wkv_expand, Wout):
        import jax, jax.numpy as jnp
        import numpy as np
        B, S, H, NH, L = (2, 256, 256, 16, 64)
        HD = H // NH
        b, sq, _ = q.shape
        sk = latent_kv.shape[1]
        qp = q @ Wq.T
        kv = latent_kv @ Wkv_expand.T
        k, v = jnp.split(kv, 2, axis=-1)
        qh = qp.reshape(b, sq, NH, HD).transpose(0, 2, 1, 3)
        kh = k.reshape(b, sk, NH, HD).transpose(0, 2, 1, 3)
        vh = v.reshape(b, sk, NH, HD).transpose(0, 2, 1, 3)
        inv_sqrt_d = 1.0 / jnp.sqrt(jnp.float32(HD))
        scores = jnp.einsum('bhqd,bhkd->bhqk', qh, kh) * inv_sqrt_d
        causal = jnp.tril(jnp.ones((sq, sk), dtype=bool))
        scores = jnp.where(causal, scores, jnp.finfo(scores.dtype).min)
        attn = jax.nn.softmax(scores, axis=-1)
        out = jnp.einsum('bhqk,bhkd->bhqd', attn, vh)
        out = out.transpose(0, 2, 1, 3).reshape(b, sq, H)
        return out @ Wout.T

    def _L3_ffn_ref(x, gate_w, gate_b, w1_shared, w2_shared, w3_shared, w1_routed, w2_routed, w3_routed):
        import jax, jax.numpy as jnp
        import numpy as np
        TOP_K = 4
        n_experts = w1_routed.shape[0]
        logits = jnp.einsum('ed,btd->bte', gate_w, x)
        scores = jax.nn.sigmoid(logits) + gate_b
        weights, indices = jax.lax.top_k(scores, TOP_K)
        weights = weights / weights.sum(-1, keepdims=True)
        shared_out = jax.nn.silu(x @ w1_shared) * (x @ w3_shared) @ w2_shared
        one_hot = jax.nn.one_hot(indices, n_experts, dtype=x.dtype)
        router_probs = (weights[..., None] * one_hot).sum(-2)
        h1 = jnp.einsum('btd,edc->btec', x, w1_routed)
        h2 = jnp.einsum('btd,edc->btec', x, w3_routed)
        h3 = jax.nn.silu(h1 * h2)
        experts_out = jnp.einsum('btec,ecd->bted', h3, w2_routed)
        routed_out = jnp.einsum('bted,bte->btd', experts_out, router_probs)
        return shared_out + routed_out
    x = x + _L0_xattn_ref(_layernorm(x, axis=-1), ctx_512, L0_xattn_Wq, L0_xattn_Wkv_expand, L0_xattn_Wout)
    x = x + _L0_ffn_ref(_layernorm(x, axis=-1), L0_ffn_w_router, L0_ffn_b_router, L0_ffn_norm1_w, L0_ffn_wv, L0_ffn_bv, L0_ffn_wo, L0_ffn_norm2_w, L0_ffn_w_gate, L0_ffn_w_up, L0_ffn_w_down)
    x = x + _L1_xattn_ref(_layernorm(x, axis=-1), ctx_512, L1_xattn_Wq, L1_xattn_w_kc_q, L1_xattn_w_kc_kv, L1_xattn_W_qr, L1_xattn_W_kr, L1_xattn_Wo)
    x = x + _L1_ffn_ref(_layernorm(x, axis=-1), L1_ffn_router_w, L1_ffn_gate_up_proj, L1_ffn_down_proj, L1_ffn_shared_gate_w, L1_ffn_shared_up_w, L1_ffn_shared_down_w, L1_ffn_shared_expert_gate_w)
    x = x + _L2_xattn_ref(_layernorm(x, axis=-1), ctx_512, L2_xattn_Wq, L2_xattn_w_kc_q, L2_xattn_w_kc_kv, L2_xattn_W_qr, L2_xattn_W_kr, L2_xattn_Wo)
    x = x + _L2_ffn_ref(_layernorm(x, axis=-1), L2_ffn_w_ln1, L2_ffn_wq, L2_ffn_bq, L2_ffn_wk, L2_ffn_bk, L2_ffn_wv, L2_ffn_bv, L2_ffn_wo, L2_ffn_w_ln2, L2_ffn_w_router, L2_ffn_w_gate_e, L2_ffn_w_up_e, L2_ffn_w_down_e, L2_ffn_w_sh_gate, L2_ffn_w_sh_up, L2_ffn_w_sh_down, L2_ffn_w_sh_eg)
    x = x + _L3_xattn_ref(_layernorm(x, axis=-1), ctx_512, L3_xattn_Wq, L3_xattn_Wkv_expand, L3_xattn_Wout)
    x = x + _L3_ffn_ref(_layernorm(x, axis=-1), L3_ffn_gate_w, L3_ffn_gate_b, L3_ffn_w1_shared, L3_ffn_w2_shared, L3_ffn_w3_shared, L3_ffn_w1_routed, L3_ffn_w2_routed, L3_ffn_w3_routed)
    return x

_drawn_inputs = setup_inputs


def setup_inputs(seed=0):
    import zlib

    import numpy as np

    out = dict(_drawn_inputs(seed))
    spreads = {'L0_ffn_norm1_w': (1.0, 0.6),
     'L0_ffn_bv': (0.0, 0.8),
     'L0_ffn_norm2_w': (1.0, 0.6),
     'L2_ffn_w_ln1': (1.0, 0.6),
     'L2_ffn_bq': (0.0, 0.8),
     'L2_ffn_bk': (0.0, 0.8),
     'L2_ffn_bv': (0.0, 0.8),
     'L2_ffn_w_ln2': (1.0, 0.6)}
    factors = {'L0_xattn_Wq': 8.0,
     'L0_ffn_w_gate': 6.185,
     'L0_ffn_w_up': 6.067,
     'L0_ffn_w_down': 6.11,
     'L1_ffn_router_w': 8.0,
     'L1_ffn_gate_up_proj': 8.0,
     'L1_ffn_down_proj': 8.0,
     'L1_ffn_shared_gate_w': 8.0,
     'L1_ffn_shared_up_w': 8.0,
     'L1_ffn_shared_down_w': 8.0,
     'L1_ffn_shared_expert_gate_w': 8.0,
     'L2_ffn_wq': 8.0,
     'L2_ffn_wk': 8.0,
     'L2_ffn_wv': 3.256,
     'L2_ffn_wo': 2.849,
     'L2_ffn_w_router': 8.0,
     'L2_ffn_w_gate_e': 8.0,
     'L2_ffn_w_up_e': 8.0,
     'L2_ffn_w_down_e': 8.0,
     'L2_ffn_w_sh_gate': 8.0,
     'L2_ffn_w_sh_up': 8.0,
     'L2_ffn_w_sh_down': 8.0,
     'L2_ffn_w_sh_eg': 8.0,
     'L3_xattn_Wq': 8.0,
     'L3_xattn_Wkv_expand': 7.191,
     'L3_xattn_Wout': 7.314,
     'L3_ffn_gate_w': 8.0,
     'L3_ffn_gate_b': 8.0,
     'L3_ffn_w1_shared': 8.0,
     'L3_ffn_w2_shared': 8.0,
     'L3_ffn_w3_shared': 8.0,
     'L3_ffn_w1_routed': 8.0,
     'L3_ffn_w2_routed': 8.0,
     'L3_ffn_w3_routed': 8.0}
    for name, (base, spread) in spreads.items():
        noise = np.random.default_rng([zlib.crc32(name.encode()), seed]).standard_normal(out[name].shape)
        drawn = base * np.exp(spread * noise) if base else spread * noise
        out[name] = jnp.asarray(drawn.astype(out[name].dtype))
    for name, factor in factors.items():
        out[name] = (out[name] * factor).astype(out[name].dtype)
    return out
```

```python
import concourse.bass as bass
from concourse import mybir
from collections import namedtuple
from contextlib import ExitStack
import numpy as np

F32, F16, BF16 = mybir.dt.float32, mybir.dt.float16, mybir.dt.bfloat16
ALU, ACT, AX = mybir.AluOpType, mybir.ActivationFunctionType, mybir.AxisListType

P = 128
D = 256
KT = D // P
B, S, L = 4, 256, 64
NT = B * S // P
QT = S // P
H = 16
HD = 16
PAIRS = H // 2
G = H * HD // P
HG = H // G
DC, DCQ, R = 64, 192, 64
HEAD_W = 1088
SPLIT = 64.0
UNSPLIT = 1.0 / (SPLIT * SPLIT)
LN_EPS, RMS_EPS = 1e-5, 1e-6
STAGES = 8


class Count:

    def __init__(self, sem):
        self.sem, self.done, self.turn, self.steps = sem, 0, 0, 0

    def open(self, turn, steps):
        self.turn, self.steps, self.begun = turn, steps, self.done

    def close(self, turns):
        assert self.done - self.begun == self.steps, (self.sem, self.done - self.begun)
        self.done, self.turn, self.steps = self.begun + turns * self.steps, 0, 0

    def link(self, engine, instruction):
        instruction.then_inc(self.sem, 1)
        self.done += 1
        engine.wait_ge(self.sem, self.done + (self.turn * self.steps if self.steps else 0))


class Ffn:

    def __init__(self, name, chunks, experts, width, last=None, both=False):
        self.name, self.chunks, self.experts, self.width = name, chunks, experts, width
        self.last_experts = last or experts
        self.both = both
        self.steps = chunks * NT

    def cols(self, c):
        last = isinstance(c, int) and c == self.chunks - 1
        return (self.last_experts if last else self.experts) * self.width


FFNS = [Ffn("ffn0", 2, 2, 352 // 2), Ffn("ffn1", 9, 8, 64, last=1),
        Ffn("ffn2", 6, 2, 352 // 2), Ffn("ffn3", 9, 2, 352 // 2, last=1, both=True)]


def k_tiles(cols):
    return [(k, min(P, cols - k * P)) for k in range((cols + P - 1) // P)]


def build(nc, d, out):
    ctx = ExitStack()
    with ctx:
        def sb(name, shape, dt=F32):
            return ctx.enter_context(nc.sbuf_tensor(name, shape, dt))

        def Sems(part, names):
            return namedtuple(part, names)(*(ctx.enter_context(nc.semaphore(f"{part}_{n}")) for n in names.split()))

        x = sb("x", [P, NT, D])
        xn = sb("xn", [P, NT, D])
        xT = sb("xT", [P, KT, NT, P])
        ident = sb("ident", [P, P])
        ident_b = sb("ident_b", [P, P], BF16)
        causal_b = sb("causal_b", [P, 8 * L + 2 * P], BF16)
        mask_lat = causal_b[:, 0:8 * L]
        mask_self = causal_b[:, 8 * L:]
        heads_c = sb("heads_c", [P, HG + D + 2])
        own_head = heads_c[:, 0:HG]
        own_half = heads_c[:, HG:HG + D]
        parity = heads_c[:, HG + D:HG + D + 2]
        primer = sb("primer", [P, 8])
        half_neg = sb("half_neg", [P, NT])
        ctx_t = sb("ctx_t", [P, B * L])
        ctx_d = sb("ctx_d", [L, B, 2, L])
        kvr = sb("kvr", [P, B * L])
        stats = sb("stats", [P, NT, 6])
        meanvar = sb("meanvar", [P, NT, 2])
        var_e = sb("var_e", [P, NT])
        rstd = sb("rstd", [P, NT])
        rms_e = sb("rms_e", [P, NT])
        rms_r = sb("rms_r", [P, NT])
        gates = sb("gates", [P, 9, NT, 8])
        w_stage = sb("w_stage", [P, 2048])
        w_down = sb("w_down", [P, 2, 1024])
        arena = sb("arena", [P, 39424])

        def take(at, shape, dt=F32):
            n = int(np.prod(shape)) // (1 if dt == F32 else 2)
            a = arena[:, at:at + n]
            if dt != F32:
                a = a.bitcast(dt)
            if len(shape) > 1:
                names = " ".join("abcdefg"[:len(shape)])
                kw = {"abcdefg"[i]: shape[i] for i in range(1, len(shape))}
                a = a.rearrange(f"p ({names}) -> p {names}", **kw)
            return a, at + n

        at = 0
        w_split, at = take(at, [2, 2, 2048], F16)
        xh, at = take(at, [KT, NT, P], F16)
        xl, at = take(at, [KT, NT, P], F16)
        m_t, at = take(at, [2, 512])
        m_a, at = take(at, [2, 512])
        m_b, at = take(at, [2, 512])
        m_c, at = take(at, [2, 512])
        hidT, at = take(at, [2, 4, P])
        ffn_w, at = take(at, [4096])
        ffn_v, at = take(at, [2048])
        ffn_s, at = take(at, [6144])
        qkv_w, at = take(at, [KT, 768])

        at = 0
        at_w, at = take(at, [6144])
        at_m, at = take(at, [16384])
        at_f, at = take(at, [8192])
        at_p, at = take(at, [2, 1024])
        at_pt, at = take(at, [2, 1024])
        tables, _ = take(at, [2, 3, 256])
        at_o, _ = take(at, [2, 512])
        at_r, at = take(at + 1536, [2, 2, 3, 256])
        heads = arena[:, 30720:30720 + 4 * HEAD_W].rearrange("p (s h c) -> p s h c", s=2, h=2)
        at = 30720 + 4 * HEAD_W
        kv_diag, at = take(at, [B, P])
        bt, at = take(at, [2, 2, DCQ])
        e_pair, at = take(at, [D])
        bb, at = take(at, [2, 2, DC])
        cc, at = take(at, [2, DC])
        dt_, at = take(at, [2, D])
        small = sb("small", [P, 2, 4, H])
        causal_f = w_stage[:, 1024:1024 + 8 * L + 2 * P]
        rot_in = w_stage

        PS = ctx.enter_context(nc.psum_tensor("PS", [P, 8, 512], F32))

        def bank(n, k=1):
            return PS[:, n:n + k, :].rearrange("p b c -> p (b c)")


        load = Sems("load", "x const ctx rot out")
        kvs = Sems("kv", "rot")
        kv_diag_done = {n: ctx.enter_context(nc.semaphore(f"kv_diag{n}")) for n in (1, 2)}
        own = {n: Count(ctx.enter_context(nc.semaphore(f"own_{n}"))) for n in ("dve", "pool")}
        ln = Sems("ln", "var rstd xn xT_ps xT")
        ln_T_before = {0: 0, 2: 8, 3: 16, 4: 24, 6: 32, 7: 40}
        ln_xT_before = {0: 0, 2: 4, 3: 8, 4: 16, 6: 20, 7: 24}
        soft = Sems("soft", "sub p sums t_ps t y_ps x")
        norm = Sems("norm", "pn")
        lat = Sems("lat", "w kv_ps kv q_ps q s o_ps o ot_ps ot")
        att = {1: Sems("att1", "w0 w1 zero a_ps a bt_ps bt e_ps e m_ps m f_ps f tab q_ps roped s"),
               2: Sems("att2", "w0 w1 zero bt_ps bt e_ps e m_ps m f_ps f c_ps c dt_ps dt q s")}
        pre = [Sems("pre0", "w fold_ps fold ms r z zT_ps zT y_ps ssq rr z2 z2T_ps h gates"),
               Sems("pre1", "w h logit lg e t gates"),
               Sems("pre2", "w hT z zT_ps ms r stage qkv qr qrT_ps qT kT s mx p pt_ps pt o_ps o ot_ps ot y_ps x2 "
                    "ssq rr z2 z2T_ps h f logit lg e t gates"),
               Sems("pre3", "w h logit lg t gates")]
        ffn = Sems("ffn", "w_in w_hi w_lo dn_in gu g act t prod hid hidT_ps hidT down x")
        chunks_before = [sum(f.chunks for f in FFNS[:n]) for n in range(5)]
        steps_before = [sum(f.steps for f in FFNS[:n]) for n in range(5)]

        def x_ready(engine, m, i=NT - 1):
            n = (m - 1) // 2
            if m == 0:
                engine.wait_ge(load.x, 16)
            elif m % 2:
                engine.wait_ge(soft.x, NT * n + i + 1)
            else:
                engine.wait_ge(ffn.x, steps_before[n + 1] - NT + i + 1)

        def hold(engine, sem, value):
            engine.wait_ge(load.const, 48)
            engine.wait_ge(sem, value)

        primed = [0]

        def prime(*sems):
            for sem in sems:
                nc.gpsimd.memset(primer[:, primed[0]:primed[0] + 1], 0.0).then_inc(sem, 1)
                primed[0] += 1

        def over(ap, axis, n):
            a = ap.unsqueeze(axis)
            shape = list(a.shape)
            shape[axis] = n
            return a.broadcast_to(shape)

        block = ctx.enter_context(nc.Block())


        def dve_ln(m):
            s, me = ln, own["dve"]
            for i in range(NT):
                x_ready(nc.vector, m, i)
                me.link(nc.vector, nc.vector.bn_stats(stats[:, i, :], x[:, i, :]))
                ins = nc.vector.bn_aggr(meanvar[:, i, :], stats[:, i, :])
            me.link(nc.vector, ins)
            nc.vector.tensor_scalar(var_e[:], meanvar[:, :, 1], LN_EPS, None, ALU.add).then_inc(s.var, 1)
            nc.vector.wait_ge(s.rstd, m + 1)
            for i in range(NT):
                nc.vector.tensor_scalar(xn[:, i, :], x[:, i, :], meanvar[:, i, 0:1], rstd[:, i:i + 1],
                                        ALU.subtract, ALU.mult).then_inc(s.xn, 1)

        def pool_ln(m):
            nc.gpsimd.wait_ge(ln.var, m + 1)
            nc.gpsimd.tensor_tensor(rstd[:], var_e[:], half_neg[:], ALU.pow).then_inc(ln.rstd, 1)

        def pe_transpose_tiles(src, ready, before, done):
            for i in range(NT):
                nc.tensor.wait_ge(ready, before + i + 1)
                for k in range(KT):
                    ins = nc.tensor.transpose(PS[:, i // 2, (i % 2) * D + k * P:(i % 2) * D + (k + 1) * P],
                                              src[:, i, k * P:(k + 1) * P], ident[:])
                ins.then_inc(done, 1)

        def pair_ps(j):
            return PS[:, j, :].rearrange("p (t k c) -> p k t c", t=2, k=KT)

        def act_ln(m):
            for j in range(NT // 2):
                nc.scalar.wait_ge(ln.xT_ps, ln_T_before[m] + 2 * j + 2)
                nc.scalar.activation(xT[:, :, 2 * j:2 * j + 2, :], pair_ps(j), ACT.Copy).then_inc(ln.xT, 1)

        lat_wq = at_w[:, 0:KT * D].rearrange("p (k c) -> p k c", k=KT)
        lat_wo = at_w[:, 512:512 + G * D].rearrange("p (k c) -> p k c", k=G)
        lat_wkv = at_w[0:L, 1024:1536]
        lat_k = at_m[:, 0:B * G * HG * L].rearrange("p (b g h l) -> p b g h l", b=B, g=G, h=HG)
        lat_v = at_f[:, 0:B * D].rearrange("p (b c) -> p b c", b=B)
        lat_q = at_o[:, 0, :].rearrange("p (g c) -> p g c", g=G)
        lat_o = at_o[:, 1, :].rearrange("p (q c) -> p q c", q=QT)
        lat_oT = at_r[:, 0, 0, 0:2, :].rearrange("p q (g c) -> p q g c", g=G)

        def heads_of(ap):
            return ap.rearrange("p (h l) -> p h l", h=H)

        def sp_latent(n):
            x_ready(nc.sync, 2 * n)
            nc.sync.dma_start(at_w[:, 0:1536], d[f"lat{n}"]).then_inc(lat.w, 16)

        def pe_latent(n):
            pe, s, again = nc.tensor, lat, n // 3
            x_ready(pe, 2 * n)
            pe.wait_ge(load.ctx, 32)
            pe.wait_ge(s.w, 16 * again + 16)
            for g in range(G):
                ins = pe.matmul(PS[:, 4, g * B * L:(g + 1) * B * L], lat_wkv[:, g * P:(g + 1) * P], ctx_t[0:L, :],
                                start=True, stop=True)
            ins.then_inc(s.kv_ps, 1)
            for b in range(B):
                ins = pe.matmul(PS[:, 5 + b // 2, (b % 2) * D:(b % 2 + 1) * D],
                                ctx_d[:, b, :, :].rearrange("p a l -> p (a l)"), lat_wkv[:, D:2 * D],
                                start=True, stop=True)
            ins.then_inc(s.kv_ps, 1)
            pe_transpose_tiles(xn, ln.xn, 2 * n * NT, ln.xT_ps)
            pe.wait_ge(ln.xT, ln_xT_before[2 * n] + NT // 2)
            pe.wait_ge(s.kv, 4 * again + 4)
            with pe.Fori(0, B) as b:
                for g in range(G):
                    for k in range(KT):
                        ins = pe.matmul(PS[:, 0, g * S:(g + 1) * S], lat_wq[:, k, g * P:(g + 1) * P],
                                        xT[:, k, bass.ds(QT * b, QT), :].rearrange("p t c -> p (t c)"),
                                        start=(k == 0), stop=(k == KT - 1))
                ins.then_inc(s.q_ps, 1)
                pe.wait_ge(s.q, B * again + b + 1)
                for q in range(QT):
                    for g in range(G):
                        ins = pe.matmul(PS[:, 1 + 2 * q + g, :], lat_q[:, g, q * P:(q + 1) * P],
                                        lat_k[:, bass.ds(b, 1), g, :, :].rearrange("p b h l -> p (b h l)"),
                                        start=True, stop=(q > 0))
                        if q == 0:
                            ins = pe.matmul(PS[:, 1 + g, :], ident_b[:], mask_lat, start=False, stop=True)
                    ins.then_inc(s.s, 1)

                def transposed(q):
                    pe.wait_ge(soft.p, NT * n + 2 * b + q + 1)
                    for j in range(PAIRS):
                        ins = pe.transpose(PS[:, 5 + j // 4, (j % 4) * P:(j % 4 + 1) * P],
                                           at_p[:, q, j * P:(j + 1) * P], ident[:])
                    ins.then_inc(soft.t_ps, 1)

                def times_values(q):
                    pe.wait_ge(soft.t, NT * n + 2 * b + q + 1)
                    for j in range(PAIRS):
                        ins = pe.matmul(PS[:, 7, j * 2 * HD:(j + 1) * 2 * HD], at_pt[:, q, j * P:(j + 1) * P],
                                        lat_v[:, bass.ds(b, 1), j * 2 * HD:(j + 1) * 2 * HD]
                                        .rearrange("p b c -> p (b c)"), start=True, stop=True)
                    ins.then_inc(s.o_ps, 1)

                def project(q):
                    pe.wait_ge(s.o, NT * again + 2 * b + q + 1)
                    if q:
                        pe.wait_ge(soft.x, NT * n + 2 * b + q)
                    for g in range(G):
                        ins = pe.transpose(PS[:, 0, g * P:(g + 1) * P], lat_o[:, q, g * P:(g + 1) * P], ident[:])
                    ins.then_inc(s.ot_ps, 1)
                    pe.wait_ge(s.ot, NT * again + 2 * b + q + 1)
                    for g in range(G):
                        ins = pe.matmul(PS[:, 0, D:2 * D], lat_oT[:, q, g, :], lat_wo[:, g, :],
                                        start=(g == 0), stop=(g == G - 1))
                    ins.then_inc(soft.y_ps, 1)

                transposed(0)
                times_values(0)
                transposed(1)
                project(0)
                times_values(1)
                project(1)
                pe.wait_ge(soft.x, NT * n + 2 * b + 2)

        def act_latent(n):
            act, s, again = nc.scalar, lat, n // 3
            act_ln(2 * n)
            with act.Fori(0, B) as b:
                act.wait_ge(s.q_ps, B * again + b + 1)
                act.activation(lat_q, PS[:, 0, :].rearrange("p (g c) -> p g c", g=G), ACT.Copy).then_inc(s.q, 1)
                for q in range(QT):
                    act.wait_ge(soft.sub, NT * n + 2 * b + q + 1)
                    act.activation(at_p[:, q, :], at_p[:, q, :], ACT.Exp).then_inc(soft.p, 1)
                for q in range(QT):
                    act.wait_ge(soft.t_ps, NT * n + 2 * b + q + 1)
                    act.activation(at_pt[:, q, :], bank(5, 2), ACT.Copy).then_inc(soft.t, 1)
                for q in range(QT):
                    act.wait_ge(s.ot_ps, NT * again + 2 * b + q + 1)
                    act.activation(lat_oT[:, q, :, :], PS[:, 0, 0:D].rearrange("p (g c) -> p g c", g=G),
                                   ACT.Copy).then_inc(s.ot, 1)

        def dve_scores(ready, me, q, count, first_bank):
            scores = heads_of(bank(first_bank, 2))
            nc.vector.wait_ge(ready, count)
            me.link(nc.vector, nc.vector.tensor_reduce(small[:, q, 0, :], scores, AX.X, ALU.max))
            nc.vector.tensor_tensor(heads_of(at_p[:, q, :]), scores, over(small[:, q, 0, :], 2, L),
                                    ALU.subtract).then_inc(soft.sub, 1)

        def dve_sums(me, q, count):
            nc.vector.wait_ge(soft.p, count)
            me.link(nc.vector, nc.vector.tensor_reduce(small[:, q, 1, :], heads_of(at_p[:, q, :]), AX.X, ALU.add))
            nc.vector.reciprocal(small[:, q, 2, :], small[:, q, 1, :]).then_inc(soft.sums, 1)

        def dve_latent(n):
            dve, s, again, me = nc.vector, lat, n // 3, own["dve"]
            x_ready(dve, 2 * n)
            dve.wait_ge(load.const, 48)
            dve.wait_ge(s.kv_ps, 2 * again + 1)
            for g in range(G):
                dve.tensor_tensor(lat_k[:, :, g, :, :],
                                  over(PS[:, 4, g * B * L:(g + 1) * B * L].rearrange("p (b l) -> p b l", b=B), 2, HG),
                                  over(over(own_head, 1, B), 3, L), ALU.mult).then_inc(s.kv, 1)
            dve.wait_ge(s.kv_ps, 2 * again + 2)
            for j in range(2):
                dve.tensor_tensor(lat_v[:, 2 * j:2 * j + 2, :], PS[:, 5 + j, :].rearrange("p (b c) -> p b c", b=2),
                                  over(own_half, 1, 2), ALU.mult).then_inc(s.kv, 1)
            dve_ln(2 * n)
            steps = 4
            with dve.Fori(0, B) as b:
                me.open(b, steps)
                for q in range(QT):
                    dve_scores(s.s, me, q, NT * again + 2 * b + q + 1, 1 + 2 * q)
                for q in range(QT):
                    dve_sums(me, q, NT * n + 2 * b + q + 1)
                for q in range(QT):
                    if q == 0:
                        dve.wait_ge(soft.sums, NT * n + 2 * b + 2)
                    dve.wait_ge(s.o_ps, NT * again + 2 * b + q + 1)
                    dve.tensor_tensor(lat_o[:, q, :].rearrange("p (h c) -> p h c", h=H),
                                      PS[:, 7, 0:D].rearrange("p (h c) -> p h c", h=H),
                                      over(small[:, q, 2, :], 2, HD), ALU.mult).then_inc(s.o, 1)
                    dve.wait_ge(soft.y_ps, NT * n + 2 * b + q + 1)
                    tile = x[:, bass.ds(2 * b + q, 1), :]
                    dve.tensor_tensor(tile, tile, PS[:, 0:1, D:2 * D], ALU.add).then_inc(soft.x, 1)
            me.close(B)

        fold_a = at_w.rearrange("p (k c) -> p k c", k=KT)
        fold_m = at_m.rearrange("p (b j s c) -> p b j s c", b=B, j=PAIRS, s=2)
        fold_n = at_m[:, 0:B * KT * H * L].rearrange("p (b k c) -> p b k c", b=B, k=KT)
        fold_f = at_f.rearrange("p (b j c) -> p b j c", b=B, j=PAIRS)
        fold_x = at_o[:, 0, :].rearrange("p (k q c) -> p k q c", k=KT, q=QT)
        W_KCQ, W_Q, W_KV, W_O, W_KR, W_QR = 0, 256, 512, 576, 832, 896

        def head_w(slot, h, at, cols, rows=P):
            return heads[0:rows, slot, h, at:at + cols]

        def sp_folded(n):
            sp, s = nc.sync, att[n]
            x_ready(sp, 2 * n)
            for j in range(2):
                sp.dma_start(heads[:, j, :, :], d[f"heads{n}"][j]).then_inc((s.w0, s.w1)[j], 16)
            with sp.Fori(1, PAIRS // 2) as i:
                for j in range(2):
                    sp.wait_ge(s.e_ps if n == 1 else s.dt_ps, 2 * i + j - 1)
                    sp.dma_start(heads[:, j, :, :], d[f"heads{n}"][bass.ds(2 * i + j, 1), :, :, :]
                                 .rearrange("a p h c -> p (a h) c")).then_inc((s.w0, s.w1)[j], 16)
            if n == 1:
                sp.wait_ge(s.f, 2 * PAIRS + 1)
                sp.wait_ge(s.m, 4 * PAIRS + 1)
                sp.dma_start(tables, d["rope1"]).then_inc(s.tab, 16)

        def pool_folded(n):
            pool, s = nc.gpsimd, att[n]
            x_ready(pool, 2 * n)
            prime(*((s.f, s.m, s.a) if n == 1 else (s.f, s.m)))
            pool.memset(kv_diag, 0.0).then_inc(s.zero, 1)
            if n == 1:
                for b in range(B):
                    pool.memset(fold_m[:, b, :, :, L:3 * L], 0.0).then_inc(s.zero, 1)
            pool_ln(2 * n)
            with pool.Fori(0, B) as b:
                for q in range(QT):
                    pool.wait_ge(soft.sums, NT * n + 2 * b + q + 1)
                    pool.tensor_tensor(heads_of(at_p[:, q, :]), heads_of(at_p[:, q, :]),
                                       over(small[:, q, 2, :], 2, L), ALU.mult).then_inc(norm.pn, 1)

        def pe_fold_values(n, j, q):
            pe, s = nc.tensor, att[n]
            for h in range(2):
                ins = pe.matmul(PS[L * h:L * (h + 1), 6, 0:D], head_w(j, h, W_KV, DC), head_w(j, h, W_O, D),
                                start=True, stop=True)
            ins.then_inc(s.e_ps, 1)

        def pe_values(n, q, first, second):
            pe, s = nc.tensor, att[n]
            pe.wait_ge(s.e, q + 1)
            for b in range(B):
                ins = pe.matmul(PS[:, (first, second)[b // 2], (b % 2) * D:(b % 2 + 1) * D], kv_diag[:, b, :], e_pair,
                                start=True, stop=True)
            ins.then_inc(s.f_ps, 1)

        def pe_fold1(i, j):
            pe, s = nc.tensor, att[1]
            q = 2 * i + j
            pe.wait_ge((s.w0, s.w1)[j], 16 * i + 16)
            pe.wait_ge(s.f, 2 * q + 1)
            pe.wait_ge(s.a, q + 1)
            for k in range(KT):
                for h in range(2):
                    ins = pe.matmul(PS[:, k, h * DCQ:(h + 1) * DCQ], head_w(j, h, W_Q + k * P, P),
                                    head_w(j, h, W_KCQ, DCQ), start=True, stop=True)
            ins.then_inc(s.a_ps, 1)
            for h in range(2):
                ins = pe.matmul(PS[0:DC, 2, h * DCQ:(h + 1) * DCQ], head_w(j, h, W_KR, DC, R),
                                head_w(j, h, W_QR, DCQ, R), start=True, stop=True)
            ins.then_inc(s.bt_ps, 1)
            pe_fold_values(1, j, q)
            pe.wait_ge(s.bt, 3 * q + 3)
            pe.wait_ge(s.m, 4 * q + 1)
            for c in range(2):
                for h, tile, rows, at, cols in ((0, 0, P, 0, P), (0, 1, DC, 0, DC), (1, 1, DC, DC, DC), (1, 2, P, 0, P)):
                    first = (0, P)[tile > 0] if h == 0 else (0, DC)[tile > 1]
                    ins = pe.matmul(PS[at:at + cols, 3 + tile, c * B * L:(c + 1) * B * L],
                                    bt[0:DC, c, h, first:first + cols], kvr[0:DC, :], start=True, stop=True)
            ins.then_inc(s.m_ps, 1)
            pe_values(1, q, 7, 2)

        def act_fold1(i, j):
            act, s = nc.scalar, att[1]
            q = 2 * i + j
            hold(act, s.a_ps, q + 1)
            act.activation(fold_a[:, :, bass.ds(q * 2 * DCQ, 2 * DCQ)], PS[:, 0:KT, 0:2 * DCQ], ACT.Copy).then_inc(s.a, 1)
            act.wait_ge(s.bt_ps, q + 1)
            act.activation(bt[0:DC, 0, :, :], PS[0:DC, 2, 0:2 * DCQ].rearrange("p (h c) -> p h c", h=2),
                           ACT.Copy).then_inc(s.bt, 1)
            for c in range(2):
                hold(act, s.f_ps, q + 1)
                act.activation(fold_f[:, 2 * c:2 * c + 2, bass.ds(q, 1), :],
                               PS[:, (7, 2)[c], :].rearrange("p (b a c) -> p b a c", b=2, a=1), ACT.Copy).then_inc(s.f, 1)

        def dve_fold1(i, j):
            dve, s = nc.vector, att[1]
            q = 2 * i + j
            half = DCQ // 2
            dve.wait_ge(s.bt, 3 * q + 1)
            for c in range(2):
                dve.tensor_copy(bt[0:DC, 1, :, (1 - c) * half:(2 - c) * half],
                                bt[0:DC, 0, :, c * half:(c + 1) * half]).then_inc(s.bt, 1)
            dve.wait_ge(s.e_ps, q + 1)
            dve.tensor_copy(e_pair, PS[:, 6, 0:D]).then_inc(s.e, 1)
            dve.wait_ge(s.m_ps, q + 1)
            for rows, tile, at in ((slice(0, P), 3, 0), (slice(0, DC), 4, L), (slice(DC, P), 4, 2 * L), (slice(0, P), 5, 3 * L)):
                for c in range(2):
                    ins = dve.tensor_scalar(fold_m[rows, :, bass.ds(q, 1), c, at:at + L],
                                            PS[rows, tile, c * B * L:(c + 1) * B * L].rearrange("p (b a l) -> p b a l", b=B, a=1),
                                            1.0, None, ALU.mult)
                ins.then_inc(s.m, 1)

        def pe_fold2(i, j):
            pe, s = nc.tensor, att[2]
            q = 2 * i + j
            half = DCQ // 2
            pe.wait_ge((s.w0, s.w1)[j], 16 * i + 16)
            pe.wait_ge(s.f, 2 * q + 1)
            for h in range(2):
                for k in range(2):
                    at = (h * 2 + k) * DC
                    ins = pe.matmul(PS[0:half, 2, at:at + DC], head_w(j, h, W_QR + k * half, half, R),
                                    head_w(j, h, W_KR, DC, R), start=True, stop=True)
            ins.then_inc(s.bt_ps, 1)
            pe_fold_values(2, j, q)
            pe.wait_ge(s.bt, q + 1)
            for h in range(2):
                for k in range(2):
                    ins = pe.matmul(PS[:, 3, h * DC:(h + 1) * DC], head_w(j, h, W_KCQ + k * P, P, half),
                                    bb[0:half, h, k, :], start=(k == 0), stop=(k == 1))
            ins.then_inc(s.c_ps, 1)
            pe_values(2, q, 7, 5)
            pe.wait_ge(s.c, q + 1)
            for h in range(2):
                ins = pe.matmul(PS[0:DC, 4, h * D:(h + 1) * D], cc[:, h, :], head_w(j, h, W_Q, D), start=True, stop=True)
            ins.then_inc(s.dt_ps, 1)
            pe.wait_ge(s.dt, q + 1)
            pe.wait_ge(s.m, 2 * q + 1)
            for k in range(KT):
                for h in range(2):
                    ins = pe.matmul(PS[:, k, h * B * L:(h + 1) * B * L], dt_[0:DC, h, k * P:(k + 1) * P], kvr[0:DC, :],
                                    start=True, stop=True)
            ins.then_inc(s.m_ps, 1)

        def act_fold2(i, j):
            act, s = nc.scalar, att[2]
            q = 2 * i + j
            act.wait_ge(s.bt_ps, q + 1)
            act.activation(bb[0:DCQ // 2, :, :, :], PS[0:DCQ // 2, 2, 0:4 * DC].rearrange("p (h k c) -> p h k c", h=2, k=2),
                           ACT.Copy).then_inc(s.bt, 1)
            for c in range(2):
                hold(act, s.f_ps, q + 1)
                act.activation(fold_f[:, 2 * c:2 * c + 2, bass.ds(q, 1), :],
                               PS[:, (7, 5)[c], :].rearrange("p (b a c) -> p b a c", b=2, a=1), ACT.Copy).then_inc(s.f, 1)
            act.wait_ge(s.dt_ps, q + 1)
            act.activation(dt_[0:DC, :, :], PS[0:DC, 4, :].rearrange("p (h c) -> p h c", h=2), ACT.Copy).then_inc(s.dt, 1)

        def dve_fold2(i, j):
            dve, s = nc.vector, att[2]
            q = 2 * i + j
            dve.wait_ge(s.e_ps, q + 1)
            dve.tensor_copy(e_pair, PS[:, 6, 0:D]).then_inc(s.e, 1)
            dve.wait_ge(s.c_ps, q + 1)
            dve.tensor_copy(cc, PS[:, 3, 0:2 * DC].rearrange("p (h c) -> p h c", h=2)).then_inc(s.c, 1)
            dve.wait_ge(s.m_ps, q + 1)
            for k in range(KT):
                for h in range(2):
                    ins = dve.tensor_scalar(fold_n[:, :, k, bass.ds((2 * q + h) * L, L)],
                                            PS[:, k, h * B * L:(h + 1) * B * L].rearrange("p (b l) -> p b l", b=B),
                                            1.0, None, ALU.mult)
                ins.then_inc(s.m, 1)

        def pe_folded(n):
            pe, s = nc.tensor, att[n]
            x_ready(pe, 2 * n)
            pe.wait_ge(s.zero, 5 if n == 1 else 1)
            pe.wait_ge(kvs.rot, 1)
            pe.wait_ge(kv_diag_done[n], 2)
            with pe.Fori(0, PAIRS // 2) as i:
                for j in range(2):
                    (pe_fold1 if n == 1 else pe_fold2)(i, j)
            if n == 2:
                pe.wait_ge(s.m, 2 * PAIRS + 1)
            else:
                pe.wait_ge(s.m, 4 * PAIRS + 1)
                pe.wait_ge(s.a, PAIRS + 1)
            pe.wait_ge(s.f, 2 * PAIRS + 1)
            pe_transpose_tiles(xn, ln.xn, 2 * n * NT, ln.xT_ps)
            pe.wait_ge(ln.xT, ln_xT_before[2 * n] + NT // 2)
            if n == 1:
                pe.wait_ge(s.tab, 16)
            with pe.Fori(0, B) as b:
                if n == 1:
                    pe.wait_ge(soft.x, NT * n + 2 * b)

                    def queries(j):
                        at = 4 + 2 * (j % 2)
                        for t in range(3):
                            for k in range(KT):
                                ins = pe.matmul(PS[:, at + t // 2, (t % 2) * S:(t % 2 + 1) * S],
                                                fold_a[:, k, (3 * j + t) * P:(3 * j + t + 1) * P],
                                                xT[:, k, bass.ds(QT * b, QT), :].rearrange("p t c -> p (t c)"),
                                                start=(k == 0), stop=(k == KT - 1))
                        ins.then_inc(s.q_ps, 1)

                    def scores(j):
                        pe.wait_ge(s.roped, 4 * PAIRS * b + 4 * (j + 1))
                        for q in range(QT):
                            for n_, (c, t, at, cols) in enumerate(((0, 1, 1, 2), (0, 0, 0, 1), (0, 2, 3, 1),
                                                                   (1, 0, 0, 1), (1, 2, 3, 1), (1, 1, 1, 2))):
                                to = (j % 4) * P + (L if t == 2 else 0)
                                ins = pe.matmul(PS[:, 2 * q + j // 4, to:to + cols * L],
                                                at_r[:, j % 2, c, t, q * P:(q + 1) * P],
                                                fold_m[:, bass.ds(b, 1), j, c, at * L:(at + cols) * L]
                                                .rearrange("p b c -> p (b c)"), start=(n_ == 0), stop=(n_ == 5))
                        return ins

                    queries(0)
                    for j in range(1, PAIRS):
                        queries(j)
                        scores(j - 1)
                    scores(PAIRS - 1).then_inc(s.s, 1)
                else:
                    pe.wait_ge(s.q, b + 1)
                    for q in range(QT):
                        for g in range(2):
                            for k in range(KT):
                                ins = pe.matmul(PS[:, 2 * q + g, :], fold_x[:, k, q, :],
                                                fold_n[:, bass.ds(b, 1), k, g * 512:(g + 1) * 512]
                                                .rearrange("p b c -> p (b c)"), start=(k == 0), stop=(k == KT - 1))
                        ins.then_inc(s.s, 1)
                    pe.wait_ge(soft.x, NT * n + 2 * b)

                def transposed(q):
                    pe.wait_ge(norm.pn, NT * (n - 1) + 2 * b + q + 1)
                    for j in range(PAIRS):
                        ins = pe.transpose(PS[:, 4 + j // 4, (j % 4) * P:(j % 4 + 1) * P],
                                           at_p[:, q, j * P:(j + 1) * P], ident[:])
                    ins.then_inc(soft.t_ps, 1)

                def output(q):
                    for j in range(PAIRS):
                        ins = pe.matmul(PS[:, 6 + q, 0:D], at_pt[:, q, j * P:(j + 1) * P],
                                        fold_f[:, bass.ds(b, 1), j, :].rearrange("p b c -> p (b c)"),
                                        start=(j == 0), stop=(j == PAIRS - 1))
                    ins.then_inc(soft.y_ps, 1)

                transposed(0)
                pe.wait_ge(soft.t, NT * n + 2 * b + 1)
                output(0)
                transposed(1)
                pe.wait_ge(soft.t, NT * n + 2 * b + 2)
                output(1)

        def act_folded(n):
            act, s = nc.scalar, att[n]
            x_ready(act, 2 * n)
            with act.Fori(0, PAIRS // 2) as i:
                for j in range(2):
                    (act_fold1 if n == 1 else act_fold2)(i, j)
            act_ln(2 * n)
            with act.Fori(0, B) as b:
                for q in range(QT):
                    act.wait_ge(soft.sub, NT * n + 2 * b + q + 1)
                    act.activation(at_p[:, q, :], at_p[:, q, :], ACT.Exp).then_inc(soft.p, 1)
                for q in range(QT):
                    act.wait_ge(soft.t_ps, NT * n + 2 * b + q + 1)
                    act.activation(at_pt[:, q, :], bank(4, 2), ACT.Copy).then_inc(soft.t, 1)

        def dve_folded(n):
            dve, s, me = nc.vector, att[n], own["dve"]
            x_ready(dve, 2 * n)
            dve.wait_ge(s.zero, 1 + (B if n == 1 else 0))
            for h in range(2):
                dve.tensor_copy(kv_diag[L * h:L * (h + 1), :, L * h:L * (h + 1)],
                                kvr[L * h:L * (h + 1), :].rearrange("p (b l) -> p b l", b=B)).then_inc(kv_diag_done[n], 1)
            with dve.Fori(0, PAIRS // 2) as i:
                for j in range(2):
                    (dve_fold1 if n == 1 else dve_fold2)(i, j)
            dve_ln(2 * n)
            steps = 4
            if n == 1:
                dve.wait_ge(s.tab, 16)
            else:
                dve.wait_ge(ln.xT, ln_xT_before[2 * n] + NT // 2)
            with dve.Fori(0, B) as b:
                me.open(b, steps)
                if n == 1:
                    for j in range(PAIRS):
                        at = 4 + 2 * (j % 2)
                        dve.wait_ge(s.q_ps, PAIRS * b + j + 1)
                        for c in range(2):
                            dve.tensor_tensor(at_r[:, j % 2, c, 0:2, :], PS[:, at, :].rearrange("p (t c) -> p t c", t=2),
                                              tables[:, c, 0:2, :], ALU.mult).then_inc(s.roped, 1)
                            dve.tensor_tensor(at_r[:, j % 2, c, 2, :], PS[:, at + 1, 0:S], tables[:, c, 2, :],
                                              ALU.mult).then_inc(s.roped, 1)
                else:
                    dve.tensor_scalar(fold_x.rearrange("p k q c -> p k (q c)"),
                                      xT[:, :, bass.ds(QT * b, QT), :].rearrange("p k q c -> p k (q c)"), 1.0, None,
                                      ALU.mult).then_inc(s.q, 1)
                for q in range(QT):
                    dve_scores(s.s, me, q, b + 1 if n == 1 else 2 * b + q + 1, 2 * q)
                for q in range(QT):
                    dve_sums(me, q, NT * n + 2 * b + q + 1)
                for q in range(QT):
                    dve.wait_ge(soft.y_ps, NT * n + 2 * b + q + 1)
                    tile = x[:, bass.ds(2 * b + q, 1), :]
                    dve.tensor_tensor(tile, tile, PS[:, 6 + q:7 + q, 0:D], ALU.add).then_inc(soft.x, 1)
            me.close(B)


        def chunk_cols(n, c):
            return FFNS[n].cols(c)

        def slot_of(c):
            return slice(c % 2, c % 2 + 1) if isinstance(c, int) else bass.ds(c % 2, 1)

        def step_of(n, c, i):
            return steps_before[n] + NT * c + i

        def chunk_of(n, c):
            return chunks_before[n] + c

        def part_experts(n, c):
            return chunk_cols(n, c) // FFNS[n].width

        def product_first(n, c):
            return FFNS[n].both and not (isinstance(c, int) and c == FFNS[n].chunks - 1)

        def over_chunks(engine, n, body):
            body(0)
            if FFNS[n].chunks > 2:
                with engine.Fori(1, FFNS[n].chunks - 1) as c:
                    body(c)
            body(FFNS[n].chunks - 1)

        def sp_ffn(n):
            sp, s, f = nc.sync, ffn, FFNS[n]
            up, dn = 4 * f.cols(0), len(k_tiles(f.cols(0))) * D
            for c in range(2):
                if c == 0:
                    sp.wait_ge(*((s.w_lo, chunks_before[n]) if n else (kvs.rot, 1)))
                elif c:
                    sp.wait_ge(s.w_lo, chunk_of(n, c))
                sp.dma_start(w_stage[:, 0:up], d[f"up{n}"][c]).then_inc(s.w_in, 16)
                if c == 0 and n:
                    sp.wait_ge(s.down, steps_before[n])
                elif c:
                    sp.wait_ge(s.down, steps_before[n] + 1)
                sp.dma_start(w_down[:, c, 0:dn], d[f"down{n}"][c]).then_inc(s.dn_in, 16)
            if f.chunks > 2:
                with sp.Fori(2, f.chunks) as c:
                    sp.wait_ge(s.w_lo, chunk_of(n, c))
                    sp.dma_start(w_stage[:, 0:up].rearrange("p (a c) -> p a c", a=1),
                                 d[f"up{n}"][bass.ds(c, 1), :, :].rearrange("a p c -> p a c")).then_inc(s.w_in, 16)
                    sp.wait_ge(s.down, step_of(n, c - 1, 0) + 1)
                    sp.dma_start(w_down[:, slot_of(c), 0:dn],
                                 d[f"down{n}"][bass.ds(c, 1), :, :].rearrange("a p c -> p a c")).then_inc(s.dn_in, 16)

        def pe_ffn(n):
            pe, s, f = nc.tensor, ffn, FFNS[n]

            def up(c, i):
                cols = chunk_cols(n, c)
                if i == 0:
                    pe.wait_ge(s.w_lo, chunk_of(n, c) + 1)
                if not (isinstance(c, int) and c == 0 and i < 2):
                    pe.wait_ge(s.prod, step_of(n, c, i) - 1)
                at = 2 * (i % 2)
                for k in range(KT):
                    for u in range(2):
                        w = [w_split[:, slot_of(c), hl, (2 * k + u) * cols:(2 * k + u + 1) * cols]
                             .rearrange("p a c -> p (a c)") for hl in range(2)]
                        g_ps = PS[:, at + u, 0:cols]
                        pe.matmul(g_ps, xh[:, k, i, :], w[0], start=(k == 0), stop=False)
                        pe.matmul(g_ps, xh[:, k, i, :], w[1], start=False, stop=False)
                        ins = pe.matmul(g_ps, xl[:, k, i, :], w[0], start=False, stop=(k == KT - 1))
                ins.then_inc(s.gu, 1)

            def transposes(c, i):
                pe.wait_ge(s.hid, step_of(n, c, i) + 1)
                for k, rows in k_tiles(chunk_cols(n, c)):
                    ins = pe.transpose(PS[0:rows, 4 + i % 2, k * P:(k + 1) * P], m_c[:, i % 2, k * P:k * P + rows], ident[:])
                ins.then_inc(s.hidT_ps, 1)

            def down(c, i):
                pe.wait_ge(s.hidT, step_of(n, c, i) + 1)
                if i == 0:
                    pe.wait_ge(s.dn_in, 16 * chunk_of(n, c) + 16)
                tiles = k_tiles(chunk_cols(n, c))
                for k, rows in tiles:
                    ins = pe.matmul(PS[:, 6 + i % 2, 0:D], hidT[0:rows, i % 2, k, :],
                                    w_down[0:rows, slot_of(c), k * D:(k + 1) * D].rearrange("p a c -> p (a c)"),
                                    start=(k == 0), stop=(k == len(tiles) - 1))
                ins.then_inc(s.down, 1)

            def chunk(c):
                for i in range(NT):
                    up(c, i)
                    before = (c, i - 2) if i >= 2 else (c - 1, i - 2 + NT)
                    if not (isinstance(c, int) and c == 0 and i < 2):
                        if not (isinstance(c, int) and c == 0 and i < 4):
                            pe.wait_ge(s.x, step_of(n, c, i) - 3)
                        down(*before)
                    before = (c, i - 1) if i >= 1 else (c - 1, NT - 1)
                    if not (isinstance(c, int) and c == 0 and i < 1):
                        transposes(*before)

            over_chunks(pe, n, chunk)
            last = f.chunks - 1
            pe.wait_ge(s.x, steps_before[n + 1] - 3)
            down(last, NT - 2)
            transposes(last, NT - 1)
            pe.wait_ge(s.x, steps_before[n + 1] - 2)
            down(last, NT - 1)

        def act_split(n, c):
            cols = 4 * FFNS[n].cols(0)
            hold(nc.scalar, ffn.w_in, 16 * chunk_of(n, c) + 16)
            nc.scalar.activation(w_split[:, slot_of(c), 0, 0:cols], w_stage[:, 0:cols].rearrange("p (a c) -> p a c", a=1),
                                 ACT.Copy, scale=SPLIT).then_inc(ffn.w_hi, 1)

        def dve_split(n, c):
            cols = 4 * FFNS[n].cols(0)
            nc.vector.wait_ge(ffn.w_hi, chunk_of(n, c) + 1)
            nc.vector.scalar_tensor_tensor(w_split[:, slot_of(c), 1, 0:cols],
                                           w_stage[:, 0:cols].rearrange("p (a c) -> p a c", a=1), SPLIT,
                                           w_split[:, slot_of(c), 0, 0:cols], ALU.mult, ALU.subtract).then_inc(ffn.w_lo, 1)

        def act_ffn(n):
            act, s, f = nc.scalar, ffn, FFNS[n]

            def evacuate(c, i):
                act.wait_ge(s.hidT_ps, step_of(n, c, i) + 1)
                tiles = k_tiles(chunk_cols(n, c))
                full = [k for k, rows in tiles if rows == P]
                if full:
                    ins = act.activation(hidT[:, i % 2, 0:len(full), :],
                                         PS[:, 4 + i % 2, 0:len(full) * P].rearrange("p (k c) -> p k c", k=len(full)), ACT.Copy)
                for k, rows in tiles[len(full):]:
                    ins = act.activation(hidT[0:rows, i % 2, k, :], PS[0:rows, 4 + i % 2, k * P:(k + 1) * P], ACT.Copy)
                ins.then_inc(s.hidT, 1)

            def chunk(c):
                cols = chunk_cols(n, c)
                for i in range(NT):
                    if i == 3 and not (isinstance(c, int) and c == f.chunks - 1):
                        act_split(n, c + 1)
                    act.wait_ge(s.gu, step_of(n, c, i) + 1)
                    t = m_t[:, i % 2, 0:cols]
                    if product_first(n, c):
                        act.activation(t, PS[:, 2 * (i % 2), 0:cols], ACT.Copy, scale=UNSPLIT).then_inc(s.g, 1)
                        act.wait_ge(s.act, NT * c + i + 1)
                        act.activation(t, m_a[:, i % 2, 0:cols], ACT.Tanh, scale=0.5 * UNSPLIT).then_inc(s.t, 1)
                    else:
                        act.activation(t, PS[:, 2 * (i % 2), 0:cols], ACT.Tanh, scale=0.5 * UNSPLIT).then_inc(s.t, 1)
                    if not (isinstance(c, int) and c == 0 and i == 0):
                        evacuate(*((c, i - 1) if i else (c - 1, NT - 1)))

            over_chunks(act, n, chunk)
            evacuate(f.chunks - 1, NT - 1)

        def dve_ffn(n):
            dve, s, f, me = nc.vector, ffn, FFNS[n], own["dve"]

            def add(c, i):
                dve.wait_ge(s.down, step_of(n, c, i) + 1)
                dve.tensor_tensor(x[:, i, :], x[:, i, :], PS[:, 6 + i % 2, 0:D], ALU.add).then_inc(s.x, 1)

            def chunk(c):
                cols = chunk_cols(n, c)
                loop = not isinstance(c, int)
                if loop:
                    me.open(c - 1, 0 if product_first(n, c) else NT)
                for i in range(NT):
                    if i == 3 and not (isinstance(c, int) and c == f.chunks - 1):
                        dve_split(n, c + 1)
                    t, a, b = (m[:, i % 2, 0:cols] for m in (m_t, m_a, m_b))
                    g_ps, u_ps = (PS[:, 2 * (i % 2) + u, 0:cols] for u in range(2))
                    if product_first(n, c):
                        dve.wait_ge(s.g, NT * c + i + 1)
                        dve.tensor_tensor(a, t, u_ps, ALU.mult).then_inc(s.act, 1)
                        if not (isinstance(c, int) and c == 0 and i < 2):
                            add(*((c, i - 2) if i >= 2 else (c - 1, i - 2 + NT)))
                        dve.wait_ge(s.t, step_of(n, c, i) + 1)
                        dve.scalar_tensor_tensor(b, t, 1.0, a, ALU.add, ALU.mult).then_inc(s.prod, 1)
                    else:
                        dve.wait_ge(s.t, step_of(n, c, i) + 1)
                        me.link(dve, dve.scalar_tensor_tensor(a, t, 1.0, g_ps, ALU.add, ALU.mult))
                        if not (isinstance(c, int) and c == 0 and i < 2):
                            dve.wait_ge(s.hid, step_of(n, c, i) - 1)
                        dve.tensor_tensor(b, a, u_ps, ALU.mult).then_inc(s.prod, 1)
                        if not (isinstance(c, int) and c == 0 and i < 2):
                            add(*((c, i - 2) if i >= 2 else (c - 1, i - 2 + NT)))
                if loop:
                    me.close(f.chunks - 2)

            over_chunks(dve, n, chunk)
            add(f.chunks - 1, NT - 2)
            add(f.chunks - 1, NT - 1)

        def pool_ffn(n):
            pool, s, f = nc.gpsimd, ffn, FFNS[n]

            def chunk(c):
                e = part_experts(n, c)
                at = slice(c, c + 1) if isinstance(c, int) else bass.ds(c, 1)
                for i in range(NT):
                    if not (isinstance(c, int) and c == 0 and i < 2):
                        pool.wait_ge(s.hidT_ps, step_of(n, c, i) - 1)
                    hold(pool, s.prod, step_of(n, c, i) + 1)
                    pool.tensor_tensor(m_c[:, i % 2, 0:e * f.width].rearrange("p (e w) -> p e w", e=e),
                                       m_b[:, i % 2, 0:e * f.width].rearrange("p (e w) -> p e w", e=e),
                                       over(gates[:, at, i, 0:e].rearrange("p a e -> p (a e)"), 2, f.width),
                                       ALU.mult).then_inc(s.hid, 1)

            over_chunks(pool, n, chunk)


        def act_parts(src_ready, before, done, scales, f32_scales=None, f32_done=None):
            for j in range(NT // 2):
                nc.scalar.wait_ge(src_ready, before + 2 * j + 2)
                for k in range(KT):
                    ps = pair_ps(j)[:, k, :, :]
                    if f32_scales is not None:
                        nc.scalar.activation(xT[:, k, 2 * j:2 * j + 2, :], ps, ACT.Copy,
                                             scale=f32_scales(k)).then_inc(f32_done, 1)
                    nc.scalar.activation(xh[:, k, 2 * j:2 * j + 2, :], ps, ACT.Copy, scale=scales(k)).then_inc(done, 1)

        def dve_parts(high_done, scales):
            for j in range(NT // 2):
                nc.vector.wait_ge(high_done, KT * (j + 1))
                for k in range(KT):
                    ins = nc.vector.scalar_tensor_tensor(xl[:, k, 2 * j:2 * j + 2, :], pair_ps(j)[:, k, :, :], scales(k),
                                                         xh[:, k, 2 * j:2 * j + 2, :], ALU.mult, ALU.subtract)
            return ins

        def plain_scale(k):
            return SPLIT

        def pe_logits(s, w, cols, ready, count):
            pe = nc.tensor
            pe.wait_ge(s.w, 16)
            pe.wait_ge(ready, count)
            for i in range(NT):
                for k in range(KT):
                    ins = pe.matmul(PS[:, 4 + i // 4, (i % 4) * cols:(i % 4 + 1) * cols], xT[:, k, i, :], w[:, k, :],
                                    start=(k == 0), stop=(k == KT - 1))
            ins.then_inc(s.logit, 1)

        def logits_ps(cols):
            return PS[:, 4:6, 0:4 * cols].rearrange("p b (t c) -> p b t c", t=4)

        def tiles_of(ap):
            return ap.rearrange("p (b t) c -> p b t c", b=2)

        def top_experts(me, values, k_top, width, ranked, rest):
            dve = nc.vector
            for i in range(NT):
                ins = dve.max(ranked[:, i, :], values[:, i, 0:width])
            me.link(dve, ins)
            if k_top < 8:
                me.link(dve, dve.tensor_copy(ranked[:, :, k_top:8], values[:, :, width:width + 8 - k_top]))
            for i in range(NT):
                ins = dve.match_replace(rest[:, i, :], ranked[:, i, :], values[:, i, :], 0.0)
            me.link(dve, ins)
            me.link(dve, dve.tensor_tensor(rest[:, :, 0:width], values[:, :, 0:width], rest[:, :, 0:width], ALU.subtract))

        def shape3(ap, n, c):
            return ap[:, 0:n * c].rearrange("p (n c) -> p n c", n=n)

        p0_wv, p0_wo = (ffn_w[:, a:a + 512].rearrange("p (k c) -> p k c", k=KT) for a in (0, 512))
        p0_fold = ffn_w[:, 1024:1536].rearrange("p (k c) -> p k c", k=KT)
        p0_bias = ffn_w[:, 1536:1792]
        p0_bv = ffn_v[:, 0:KT * P].rearrange("p (k c) -> p k c", k=KT)
        p0_router, p0_b, p0_n1, p0_n2 = ffn_v[:, 256:512], ffn_v[:, 512:513], ffn_v[:, 513:515], ffn_v[:, 515:517]
        p0_n2s = ffn_v[:, 520:522]
        p0_score, p0_route, p0_ssq = ffn_v[:, 528:536], ffn_v[:, 536:544], ffn_v[:, 544:552]
        p0_junk = ffn_v[:, 1024:1280]
        p0_att = ffn_v[:, 1280:1792].rearrange("p (a c) -> p a c", a=2)
        z = shape3(ffn_s, NT, D)
        zT = ffn_s[:, 2048:4096].rearrange("p (k t c) -> p k t c", k=KT, t=NT)

        def sp_pre0():
            x_ready(nc.sync, 1)
            nc.sync.dma_start(ffn_w[:, 0:1024], d["pre0"]).then_inc(pre[0].w, 16)
            nc.sync.dma_start(ffn_v[:, 0:517], d["vec0"]).then_inc(pre[0].w, 16)

        def pe_pre0():
            pe, s = nc.tensor, pre[0]
            x_ready(pe, 1)
            pe.wait_ge(s.w, 32)
            for m in range(KT):
                for k in range(KT):
                    pe.matmul(PS[:, 4, m * D:(m + 1) * D], p0_wv[:, k, m * P:(m + 1) * P], p0_wo[:, k, :],
                              start=(k == 0), stop=(k == KT - 1))
            for k in range(KT):
                ins = pe.matmul(PS[:, 5, 0:D], p0_bv[:, k, :], p0_wo[:, k, :], start=(k == 0), stop=(k == KT - 1))
            ins.then_inc(s.fold_ps, 1)
            pe_transpose_tiles(z, s.z, 0, s.zT_ps)
            pe.wait_ge(s.fold, 2)
            for i in range(NT):
                if i % 2 == 0:
                    pe.wait_ge(s.zT, i + 2)
                for k in range(KT):
                    ins = pe.matmul(PS[:, 4 + i // 2, (i % 2) * D:(i % 2 + 1) * D], zT[:, k, i, :], p0_fold[:, k, :],
                                    start=(k == 0), stop=(k == KT - 1))
                if i % 2:
                    ins.then_inc(s.y_ps, 1)
            pe_transpose_tiles(z, s.z2, 0, s.z2T_ps)
            pe.wait_ge(s.gates, 1)

        def act_pre0():
            act, s = nc.scalar, pre[0]
            x_ready(act, 1)
            act.wait_ge(s.fold_ps, 1)
            act.activation(p0_fold, PS[:, 4, :].rearrange("p (k c) -> p k c", k=KT), ACT.Copy).then_inc(s.fold, 1)
            act.activation(p0_bias, PS[:, 5, 0:D], ACT.Copy).then_inc(s.fold, 1)
            for j in range(NT // 2):
                act.wait_ge(s.zT_ps, 2 * j + 2)
                for k in range(KT):
                    act.activation(zT[:, k, 2 * j:2 * j + 2, :], pair_ps(j)[:, k, :, :], ACT.Copy,
                                   scale=p0_n1[:, k:k + 1]).then_inc(s.zT, 1)
            act_split(0, 0)
            act_parts(s.z2T_ps, 0, s.h, lambda k: p0_n2s[:, k:k + 1])

        def pool_pow(wait, count, out_, in_, done):
            nc.gpsimd.wait_ge(wait, count)
            nc.gpsimd.tensor_tensor(out_, in_, half_neg[:], ALU.pow).then_inc(done, 1)

        def pool_pre0():
            x_ready(nc.gpsimd, 1)
            pool_ln(1)
            pool_pow(pre[0].ms, 1, rms_r[:], rms_e[:], pre[0].r)
            pool_pow(pre[0].ssq, 1, rms_r[:], rms_e[:], pre[0].rr)
            nc.gpsimd.wait_ge(pre[0].gates, 1)

        def dve_norm_ms(me, ready, r_done):
            dve = nc.vector
            me.link(dve, dve.tensor_tensor(rms_e[:], rstd[:], rstd[:], ALU.mult))
            me.link(dve, dve.tensor_tensor(rms_e[:], rms_e[:], meanvar[:, :, 1], ALU.mult))
            dve.tensor_scalar(rms_e[:], rms_e[:], RMS_EPS, None, ALU.add).then_inc(ready, 1)
            dve.wait_ge(r_done, 1)

        def dve_pre0():
            dve, s, me = nc.vector, pre[0], own["dve"]
            dve_ln(1)
            dve_norm_ms(me, s.ms, s.r)
            for i in range(NT):
                dve.tensor_scalar(z[:, i, :], xn[:, i, :], rms_r[:, i:i + 1], None, ALU.mult).then_inc(s.z, 1)
            dve.wait_ge(s.w, 32)
            for i in range(NT):
                me.link(dve, dve.scalar_tensor_tensor(p0_junk, xn[:, i, :], 1.0, p0_router, ALU.mult, ALU.mult,
                                                      accum_out=p0_score[:, i:i + 1]))
            me.link(dve, dve.tensor_scalar(p0_route, p0_score, p0_b, 0.0, ALU.add, ALU.is_gt))
            me.link(dve, dve.tensor_scalar(p0_n2s, p0_n2, SPLIT, None, ALU.mult))
            me.link(dve, dve.tensor_scalar(gates[:, 0, :, 0], p0_route, 0.5 * UNSPLIT * UNSPLIT, None, ALU.mult))
            for c, e in ((0, 1), (1, 0), (1, 1)):
                ins = dve.tensor_copy(gates[:, c, :, e], gates[:, 0, :, 0])
            me.link(dve, ins)
            me.link(dve, dve.tensor_tensor(x[:], x[:], xn[:], ALU.add))
            dve_split(0, 0)
            dve.wait_ge(s.fold, 2)
            for i in range(NT):
                if i % 2 == 0:
                    dve.wait_ge(s.y_ps, i // 2 + 1)
                me.link(dve, dve.tensor_tensor(p0_att[:, i % 2, :], PS[:, 4 + i // 2, (i % 2) * D:(i % 2 + 1) * D], p0_bias,
                                               ALU.add))
                me.link(dve, dve.tensor_tensor(xn[:, i, :], xn[:, i, :], p0_att[:, i % 2, :], ALU.add))
                dve.scalar_tensor_tensor(x[:, i, :], p0_att[:, i % 2, :], p0_route[:, i:i + 1], x[:, i, :], ALU.mult, ALU.add)
                me.link(dve, dve.scalar_tensor_tensor(p0_junk, xn[:, i, :], 1.0, xn[:, i, :], ALU.mult, ALU.mult,
                                                      accum_out=p0_ssq[:, i:i + 1]))
            dve.tensor_scalar(rms_e[:], p0_ssq, 1.0 / D, RMS_EPS, ALU.mult, ALU.add).then_inc(s.ssq, 1)
            dve.wait_ge(s.rr, 1)
            for i in range(NT):
                dve.tensor_scalar(z[:, i, :], xn[:, i, :], rms_r[:, i:i + 1], None, ALU.mult).then_inc(s.z2, 1)
            dve_parts(s.h, lambda k: p0_n2s[:, k:k + 1]).then_inc(s.gates, 1)

        E1 = 64
        r1_w = ffn_w[:, 0:KT * (E1 + 1)].rearrange("p (k c) -> p k c", k=KT)
        lg1 = shape3(ffn_s, NT, E1 + 1)
        pr1 = shape3(ffn_s[:, 1024:], NT, E1)
        rest1 = shape3(ffn_s[:, 2048:], NT, E1)
        ranked = shape3(ffn_s[:, 3072:], NT, 8)
        row1, row2, row3 = (ffn_s[:, 3200 + 8 * a:3208 + 8 * a] for a in range(3))
        sig = ffn_s[:, 3232:3240]

        def sp_router(n, cols):
            x_ready(nc.sync, 2 * n + 1)
            nc.sync.dma_start(ffn_w[:, 0:cols], d[f"router{n}"]).then_inc(pre[n].w, 16)

        def pe_pre1(n, w, cols):
            x_ready(nc.tensor, 2 * n + 1)
            pe_transpose_tiles(xn, ln.xn, (2 * n + 1) * NT, ln.xT_ps)
            pe_logits(pre[n], w, cols, ln.xT, ln_xT_before[2 * n + 1] + NT)
            nc.tensor.wait_ge(pre[n].gates, 1)
            nc.tensor.wait_ge(pre[n].lg, 1)

        def act_pre1(n):
            act, s = nc.scalar, pre[n]
            x_ready(act, 2 * n + 1)
            act_split(n, 0)
            act_parts(ln.xT_ps, ln_T_before[2 * n + 1], s.h, plain_scale, lambda k: 1.0, ln.xT)
            if n == 1:
                act.wait_ge(s.e, 1)
                act.activation(pr1, pr1, ACT.Exp).then_inc(s.t, 1)
                act.activation(sig, lg1[:, :, E1], ACT.Tanh, scale=0.5).then_inc(s.t, 1)

        def pool_pre1(n):
            x_ready(nc.gpsimd, 2 * n + 1)
            pool_ln(2 * n + 1)
            nc.gpsimd.wait_ge(pre[n].lg, 2)

        def dve_softmax_over(me, logits, probs, e, s, width):
            dve = nc.vector
            me.link(dve, dve.tensor_reduce(row1, logits, AX.X, ALU.max))
            dve.tensor_tensor(probs, logits, over(row1, 2, width), ALU.subtract).then_inc(s.e, 1)
            dve.wait_ge(s.t, 2)
            me.link(dve, dve.tensor_reduce(row2, probs, AX.X, ALU.add))
            me.link(dve, dve.reciprocal(row3, row2))
            me.link(dve, dve.tensor_tensor(probs, probs, over(row3, 2, width), ALU.mult))

        def dve_pre1():
            dve, s, me = nc.vector, pre[1], own["dve"]
            dve_ln(3)
            dve_split(1, 0)
            dve_parts(s.h, plain_scale).then_inc(s.gates, 1)
            dve.wait_ge(s.logit, 1)
            me.link(dve, dve.tensor_copy(tiles_of(lg1), logits_ps(E1 + 1)))
            dve_softmax_over(me, lg1[:, :, 0:E1], pr1, E1, s, E1)
            top_experts(me, pr1, 8, E1, ranked, rest1)
            me.link(dve, dve.tensor_reduce(row1, rest1, AX.X, ALU.add))
            me.link(dve, dve.reciprocal(row2, row1))
            me.link(dve, dve.tensor_scalar(row3, row2, 0.5 * UNSPLIT * UNSPLIT, None, ALU.mult))
            me.link(dve, dve.tensor_tensor(rest1, rest1, over(row3, 2, E1), ALU.mult))
            dve.tensor_copy(gates[:, 0:8, :, :].rearrange("p c t e -> p t c e"),
                            rest1.rearrange("p t (c e) -> p t c e", c=8)).then_inc(s.lg, 1)
            dve.tensor_scalar(gates[:, 8, :, 0], sig, 1.0, 0.25 * UNSPLIT * UNSPLIT, ALU.add, ALU.mult).then_inc(s.lg, 1)

        E3 = 16
        r3_w = ffn_w[:, 0:KT * E3].rearrange("p (k c) -> p k c", k=KT)
        r3_b = ffn_w[:, KT * E3:KT * E3 + E3]
        sc3 = shape3(ffn_s, NT, E3 + 4)
        rest3 = shape3(ffn_s[:, 2048:], NT, E3 + 4)
        lg3 = shape3(ffn_s[:, 1024:], NT, E3)

        def dve_pre3():
            dve, s, me = nc.vector, pre[3], own["dve"]
            dve_ln(7)
            dve_split(3, 0)
            dve_parts(s.h, plain_scale).then_inc(s.gates, 1)
            dve.wait_ge(s.logit, 1)
            me.link(dve, dve.memset(sc3[:, :, E3:E3 + 4], -1e30))
            dve.tensor_copy(tiles_of(lg3), logits_ps(E3)).then_inc(s.lg, 1)
            dve.wait_ge(s.t, 1)
            me.link(dve, dve.tensor_scalar(lg3, lg3, 0.5, 0.5, ALU.mult, ALU.add))
            me.link(dve, dve.tensor_tensor(sc3[:, :, 0:E3], lg3, over(r3_b, 1, NT), ALU.add))
            top_experts(me, sc3, 4, E3, ranked, rest3)
            me.link(dve, dve.tensor_reduce(row1, rest3[:, :, 0:E3], AX.X, ALU.add))
            me.link(dve, dve.reciprocal(row2, row1))
            me.link(dve, dve.tensor_scalar(row3, row2, 0.5 * UNSPLIT, None, ALU.mult))
            me.link(dve, dve.tensor_tensor(rest3[:, :, 0:E3], rest3[:, :, 0:E3], over(row3, 2, E3), ALU.mult))
            me.link(dve, dve.tensor_copy(gates[:, 0:8, :, 0:2].rearrange("p c t e -> p t c e"),
                                         rest3[:, :, 0:E3].rearrange("p t (c e) -> p t c e", c=8)))
            dve.memset(gates[:, 8, :, 0], 0.5 * UNSPLIT * UNSPLIT).then_inc(s.lg, 1)

        def act_pre3():
            act, s = nc.scalar, pre[3]
            act_pre1(3)
            act.wait_ge(s.lg, 1)
            act.activation(lg3, lg3, ACT.Tanh, scale=0.5).then_inc(s.t, 1)

        E2 = 8
        p2_wo = ffn_w[:, 0:512].rearrange("p (k c) -> p k c", k=G)
        r2_w = ffn_w[:, 512:512 + KT * (E2 + 1)].rearrange("p (k c) -> p k c", k=KT)
        p2_bias = ffn_v[:, 0:3 * D]
        p2_cos, p2_sin = (ffn_v[:, a:a + 64].rearrange("p (q a c) -> p q a c", q=QT, a=2) for a in (768, 832))
        p2_n1, p2_n2, p2_n2s = ffn_v[:, 896:898], ffn_v[:, 898:900], ffn_v[:, 904:906]
        p2_ssq, p2_negmax = ffn_v[:, 912:920], ffn_v[:, 920:924].rearrange("p (r c) -> p r c", r=2)
        p2_junk = ffn_v[:, 1024:1280]
        sa_x = ffn_s[:, 2048:2560].rearrange("p (k q c) -> p k q c", k=KT, q=QT)
        sa_b = ffn_s[:, 2560:3072]
        sa_v = ffn_s[:, 3072:3584].rearrange("p (q c) -> p q c", q=QT)
        sa_r = ffn_s[:, 3584:4608].rearrange("p (q c) -> p q c", q=QT)
        sa_q = ffn_s[:, 4608:5120].rearrange("p (q g c) -> p q g c", q=QT, g=G)
        sa_k = ffn_s[:, 5120:6144].rearrange("p (g a c) -> p g a c", g=G, a=2)
        sa_p, sa_pt, sa_t = m_a, m_b, m_c
        sa_o = m_t[:, 0, :].rearrange("p (q c) -> p q c", q=QT)
        sa_oT = m_t[:, 1, :].rearrange("p (q g c) -> p q g c", q=QT, g=G)
        SA_STEPS = QT * PAIRS
        lg2 = shape3(ffn_s[:, 2048:], NT, E2 + 1)
        pr2 = shape3(ffn_s[:, 2560:], NT, E2 + 6)
        rest2 = shape3(ffn_s[:, 4096:], NT, E2 + 6)

        def sp_pre2():
            sp = nc.sync
            x_ready(sp, 5)
            sp.dma_start(qkv_w.rearrange("p k c -> p (k c)"), d["qkv2"]).then_inc(pre[2].w, 16)
            sp.dma_start(ffn_w[:, 0:512 + KT * (E2 + 1)], d["router2"]).then_inc(pre[2].w, 16)
            sp.dma_start(ffn_v[:, 0:900], d["vec2"]).then_inc(pre[2].w, 16)

        def sa_keys(t):
            return (t // PAIRS + 1) * P

        def pe_self(b):
            pe, s = nc.tensor, pre[2]
            pe.wait_ge(s.stage, b + 1)
            for q in range(QT):
                for k in range(KT):
                    pe.matmul(PS[:, q, :], sa_x[:, k, q, :], qkv_w[:, k, 0:512], start=(k == 0), stop=(k == KT - 1))
                for k in range(KT):
                    ins = pe.matmul(PS[:, 2 + q, 0:D], sa_x[:, k, q, :], qkv_w[:, k, 512:768], start=(k == 0),
                                    stop=(k == KT - 1))
                ins.then_inc(s.qkv, 1)
            for q in range(QT):
                pe.wait_ge(s.qr, 2 * b + q + 1)
                for k in range(4):
                    ins = pe.transpose(PS[:, 4 + q, k * P:(k + 1) * P], sa_r[:, q, k * P:(k + 1) * P], ident[:])
                ins.then_inc(s.qrT_ps, 1)
            pe.wait_ge(s.kT, 2 * b + 2)

            def scores(t):
                q, j, keys = t // PAIRS, t % PAIRS, sa_keys(t)
                rows = slice(32 * (j % 4), 32 * (j % 4) + 32)
                both = PS[:, t % 2, 0:2 * keys].rearrange("p (a c) -> p a c", a=2)
                pe.matmul(both, sa_q[rows, q, j // 4, :], sa_k[rows, j // 4, :, 0:keys], start=True, stop=False)
                pe.matmul(both[:, :, keys - P:keys], ident_b[:], mask_self.rearrange("p (a c) -> p a c", a=2),
                          start=False, stop=True).then_inc(s.s, 1)

            def project(q):
                pe.wait_ge(s.o, 2 * b + q + 1)
                pe.wait_ge(s.x2, 2 * b + q + 1)
                for g in range(G):
                    ins = pe.transpose(PS[:, 7, g * P:(g + 1) * P], sa_o[:, q, g * P:(g + 1) * P], ident[:])
                ins.then_inc(s.ot_ps, 1)
                pe.wait_ge(s.ot, 2 * b + q + 1)
                for g in range(G):
                    ins = pe.matmul(PS[:, 7, D:2 * D], sa_oT[:, q, g, :], p2_wo[:, g, :], start=(g == 0), stop=(g == G - 1))
                ins.then_inc(s.y_ps, 1)

            scores(0)
            scores(1)
            for t in range(SA_STEPS):
                q, j, keys = t // PAIRS, t % PAIRS, sa_keys(t)
                pe.wait_ge(s.p, SA_STEPS * b + t + 1)
                for a in range(2):
                    for k in range(q + 1):
                        ins = pe.transpose(PS[:, 2 + t % 2, (a * (q + 1) + k) * P:(a * (q + 1) + k + 1) * P],
                                           sa_p[:, t % 2, a * keys + k * P:a * keys + (k + 1) * P], ident[:])
                ins.then_inc(s.pt_ps, 1)
                if t + 2 < SA_STEPS:
                    scores(t + 2)
                pe.wait_ge(s.pt, SA_STEPS * b + t + 1)
                if t == PAIRS:
                    pe.wait_ge(s.o, 2 * b + 1)
                for a in range(2):
                    at = (2 * j + a) * HD
                    for k in range(q + 1):
                        ins = pe.matmul(PS[:, 6, at:at + HD],
                                        sa_pt[:, t % 2, (a * (q + 1) + k) * P:(a * (q + 1) + k + 1) * P],
                                        sa_v[:, k, at:at + HD], start=(k == 0), stop=(k == q))
                if j == PAIRS - 1:
                    ins.then_inc(s.o_ps, 1)
                if t == PAIRS + 1:
                    project(0)
            project(1)

        def act_self(b):
            act, s = nc.scalar, pre[2]
            act.activation(sa_x.rearrange("p k q c -> p k (q c)"),
                           xT[:, :, bass.ds(QT * b, QT), :].rearrange("p k q c -> p k (q c)"), ACT.Copy).then_inc(s.stage, 1)
            for q in range(QT):
                act.wait_ge(s.qrT_ps, 2 * b + q + 1)
                act.activation(sa_q[:, q, :, :], PS[:, 4 + q, 0:D].rearrange("p (g c) -> p g c", g=G), ACT.Copy).then_inc(s.qT, 1)

            def projected(q):
                act.wait_ge(s.ot_ps, 2 * b + q + 1)
                act.activation(sa_oT[:, q, :, :], PS[:, 7, 0:D].rearrange("p (g c) -> p g c", g=G), ACT.Copy).then_inc(s.ot, 1)

            for t in range(SA_STEPS):
                q, j, keys = t // PAIRS, t % PAIRS, sa_keys(t)
                act.wait_ge(s.mx, SA_STEPS * b + t + 1)
                for a in range(2):
                    ins = act.activation(sa_p[:, t % 2, a * keys:(a + 1) * keys], PS[:, t % 2, a * keys:(a + 1) * keys], ACT.Exp,
                                         bias=p2_negmax[:, t % 2, a:a + 1],
                                         accum_out=small[:, q, 1, 2 * j + a:2 * j + a + 1])
                ins.then_inc(s.p, 1)
                if t == PAIRS + 3:
                    projected(0)
            projected(1)

        def dve_self(b, me):
            dve, s = nc.vector, pre[2]
            for q in range(QT):
                dve.wait_ge(s.qkv, 2 * b + q + 1)
                dve.tensor_tensor(sa_v[:, q, :], PS[:, 2 + q, 0:D], p2_bias[:, 2 * D:3 * D], ALU.add)
                me.link(dve, dve.tensor_tensor(sa_b, PS[:, q, :], p2_bias[:, 0:2 * D], ALU.add))
                by_head = sa_b.rearrange("p (a h c) -> p a h c", a=2, h=H)
                cos_t = sa_t[:, 0, :].rearrange("p (a h c) -> p a h c", a=2, h=H)
                sin_t = sa_t[:, 1, :].rearrange("p (a h c) -> p a h c", a=2, h=H)
                half = HD // 2
                dve.tensor_tensor(cos_t, by_head, over(p2_cos[:, q, :, :], 2, H), ALU.mult)
                for lo, hi in ((0, half), (half, 0)):
                    ins = dve.tensor_tensor(sin_t[:, :, :, lo:lo + half], by_head[:, :, :, hi:hi + half],
                                            over(p2_sin[:, q, :, lo:lo + half], 2, H), ALU.mult)
                me.link(dve, ins)
                dve.tensor_tensor(sa_r[:, q, :], sa_t[:, 0, :], sa_t[:, 1, :], ALU.add).then_inc(s.qr, 1)
            for q in range(QT):
                dve.wait_ge(s.qT, 2 * b + q + 1)
                for a in range(2):
                    ins = dve.tensor_scalar(sa_k[:, :, a, q * P:(q + 1) * P],
                                            PS[:, 4 + q, D:2 * D].rearrange("p (g c) -> p g c", g=G), parity[:, a:a + 1], None,
                                            ALU.mult)
                ins.then_inc(s.kT, 1)

            def maxima(t):
                keys = sa_keys(t)
                dve.wait_ge(s.s, SA_STEPS * b + t + 1)
                dve.tensor_reduce(p2_negmax[:, t % 2, :], PS[:, t % 2, 0:2 * keys].rearrange("p (a c) -> p a c", a=2), AX.X,
                                  ALU.max, negate=True).then_inc(s.mx, 1)

            def normalised(q):
                dve.wait_ge(s.o_ps, 2 * b + q + 1)
                me.link(dve, dve.reciprocal(small[:, q, 2, :], small[:, q, 1, :]))
                dve.tensor_tensor(sa_o[:, q, :].rearrange("p (h c) -> p h c", h=H),
                                  PS[:, 6, 0:D].rearrange("p (h c) -> p h c", h=H), over(small[:, q, 2, :], 2, HD),
                                  ALU.mult).then_inc(s.o, 1)

            def added(q):
                dve.wait_ge(s.y_ps, 2 * b + q + 1)
                xn_t, x_t = (a[:, bass.ds(2 * b + q, 1), :] for a in (xn, x))
                me.link(dve, dve.tensor_tensor(xn_t, xn_t, PS[:, 7:8, D:2 * D], ALU.add))
                dve.tensor_tensor(x_t, x_t, xn_t, ALU.add).then_inc(s.x2, 1)

            maxima(0)
            maxima(1)
            for t in range(SA_STEPS):
                cols = 2 * sa_keys(t)
                dve.wait_ge(s.pt_ps, SA_STEPS * b + t + 1)
                dve.tensor_copy(sa_pt[:, t % 2, 0:cols], PS[:, 2 + t % 2, 0:cols]).then_inc(s.pt, 1)
                if t == PAIRS:
                    normalised(0)
                if t + 2 < SA_STEPS:
                    maxima(t + 2)
                if t == PAIRS + 4:
                    added(0)
            normalised(1)
            added(1)

        def pe_pre2():
            pe, s = nc.tensor, pre[2]
            x_ready(pe, 5)
            pe_transpose_tiles(z, s.z, 0, s.zT_ps)
            pe.wait_ge(s.w, 48)
            pe.wait_ge(s.hT, NT)
            with pe.Fori(0, B) as b:
                pe_self(b)
            pe_transpose_tiles(z, s.z2, 0, s.z2T_ps)
            pe_logits(s, r2_w, E2 + 1, s.f, NT)
            pe.wait_ge(s.gates, 1)
            pe.wait_ge(s.lg, 1)

        def act_pre2():
            act, s = nc.scalar, pre[2]
            x_ready(act, 5)
            act.wait_ge(s.w, 48)
            for j in range(NT // 2):
                act.wait_ge(s.zT_ps, 2 * j + 2)
                for k in range(KT):
                    act.activation(xT[:, k, 2 * j:2 * j + 2, :], pair_ps(j)[:, k, :, :], ACT.Copy,
                                   scale=p2_n1[:, k:k + 1]).then_inc(s.hT, 1)
            act_split(2, 0)
            act.wait_ge(s.hT, NT)
            with act.Fori(0, B) as b:
                act_self(b)
            act_parts(s.z2T_ps, 0, s.h, lambda k: p2_n2s[:, k:k + 1], lambda k: p2_n2[:, k:k + 1], s.f)
            act.wait_ge(s.e, 1)
            act.activation(pr2[:, :, 0:E2], pr2[:, :, 0:E2], ACT.Exp).then_inc(s.t, 1)
            act.activation(sig, lg2[:, :, E2], ACT.Tanh, scale=0.5).then_inc(s.t, 1)

        def pool_pre2():
            x_ready(nc.gpsimd, 5)
            prime(pre[2].x2)
            pool_ln(5)
            pool_pow(pre[2].ms, 1, rms_r[:], rms_e[:], pre[2].r)
            pool_pow(pre[2].ssq, 1, rms_r[:], rms_e[:], pre[2].rr)
            nc.gpsimd.wait_ge(pre[2].lg, 2)

        def dve_pre2():
            dve, s, me = nc.vector, pre[2], own["dve"]
            dve_ln(5)
            dve_norm_ms(me, s.ms, s.r)
            for i in range(NT):
                dve.tensor_scalar(z[:, i, :], xn[:, i, :], rms_r[:, i:i + 1], None, ALU.mult).then_inc(s.z, 1)
            dve.wait_ge(s.w, 48)
            me.link(dve, dve.tensor_scalar(p2_n2s, p2_n2, SPLIT, None, ALU.mult))
            dve_split(2, 0)
            with dve.Fori(0, B) as b:
                me.open(b, 8)
                dve_self(b, me)
            me.close(B)
            for i in range(NT):
                ins = dve.scalar_tensor_tensor(p2_junk, xn[:, i, :], 1.0, xn[:, i, :], ALU.mult, ALU.mult,
                                               accum_out=p2_ssq[:, i:i + 1])
                me.link(dve, ins)
            dve.tensor_scalar(rms_e[:], p2_ssq, 1.0 / D, RMS_EPS, ALU.mult, ALU.add).then_inc(s.ssq, 1)
            dve.wait_ge(s.rr, 1)
            for i in range(NT):
                dve.tensor_scalar(z[:, i, :], xn[:, i, :], rms_r[:, i:i + 1], None, ALU.mult).then_inc(s.z2, 1)
            dve_parts(s.h, lambda k: p2_n2s[:, k:k + 1]).then_inc(s.gates, 1)
            dve.wait_ge(s.logit, 1)
            me.link(dve, dve.tensor_copy(tiles_of(lg2), logits_ps(E2 + 1)))
            me.link(dve, dve.memset(pr2[:, :, E2:E2 + 6], -1.0))
            dve_softmax_over(me, lg2[:, :, 0:E2], pr2[:, :, 0:E2], E2, s, E2)
            top_experts(me, pr2, 2, E2, ranked, rest2)
            me.link(dve, dve.tensor_scalar(gates[:, 0:4, :, 0:2].rearrange("p c t e -> p t c e"),
                                           rest2[:, :, 0:E2].rearrange("p t (c e) -> p t c e", c=4),
                                           0.5 * UNSPLIT * UNSPLIT, None, ALU.mult))
            dve.tensor_scalar(gates[:, 4, :, 0], sig, 1.0, 0.25 * UNSPLIT * UNSPLIT, ALU.add, ALU.mult).then_inc(s.lg, 1)
            dve.wait_ge(s.lg, 1)
            for c, e in ((4, 1), (5, 0), (5, 1)):
                ins = dve.tensor_copy(gates[:, c, :, e], gates[:, 4, :, 0])
            ins.then_inc(s.lg, 1)


        @block.sync
        def _(sp):
            sp.dma_start(x[:], d["x"].rearrange("t p c -> p t c")).then_inc(load.x, 16)
            sp.dma_start(ctx_t[:], d["ctx_t"]).then_inc(load.ctx, 16)
            sp.dma_start(ctx_d[:], d["ctx_d"]).then_inc(load.ctx, 16)
            for to, name in ((ident[:], "ident"), (causal_f, "causal"), (heads_c[:], "heads_c")):
                sp.dma_start(to, d[name]).then_inc(load.const, 16)
            sp.dma_start(rot_in[:, 0:3 * B * L], d["rotk"]).then_inc(load.rot, 16)
            sp_latent(0)
            sp_pre0()
            sp_ffn(0)
            sp_folded(1)
            sp_router(1, KT * (E1 + 1))
            sp_ffn(1)
            sp_folded(2)
            sp_pre2()
            sp_ffn(2)
            sp_latent(3)
            sp_router(3, KT * E3 + E3)
            sp_ffn(3)
            for i in range(NT):
                x_ready(sp, 8, i)
                sp.dma_start(out[i], x[:, i, :]).then_inc(load.out, 16)
            sp.wait_ge(load.out, 16 * NT)

        @block.tensor
        def _(pe):
            pe.wait_ge(load.const, 48)
            pe.wait_ge(kvs.rot, 1)
            pe_latent(0)
            pe_pre0()
            pe_ffn(0)
            pe_folded(1)
            pe_pre1(1, r1_w, E1 + 1)
            pe_ffn(1)
            pe_folded(2)
            pe_pre2()
            pe_ffn(2)
            pe_latent(3)
            pe_pre1(3, r3_w, E3)
            pe_ffn(3)

        @block.scalar
        def _(act):
            act_latent(0)
            act_pre0()
            act_ffn(0)
            act_folded(1)
            act_pre1(1)
            act_ffn(1)
            act_folded(2)
            act_pre2()
            act_ffn(2)
            act_latent(3)
            act_pre3()
            act_ffn(3)

        @block.vector
        def _(dve):
            me = own["dve"]
            dve.wait_ge(load.ctx, 32)
            dve.wait_ge(load.rot, 16)
            cos_k, sin_k, swapped = (rot_in[:, a * B * L:(a + 1) * B * L] for a in range(3))
            me.link(dve, dve.tensor_tensor(sin_k, sin_k, swapped, ALU.mult))
            me.link(dve, dve.tensor_tensor(kvr[:], ctx_t[:], cos_k, ALU.mult))
            dve.wait_ge(load.const, 48)
            dve.tensor_copy(ident_b[:], ident[:])
            dve.tensor_copy(causal_b[:], causal_f)
            dve.tensor_tensor(kvr[:], kvr[:], sin_k, ALU.add).then_inc(kvs.rot, 1)
            dve.wait_ge(kvs.rot, 1)
            dve_latent(0)
            dve_pre0()
            dve_ffn(0)
            dve_folded(1)
            dve_pre1()
            dve_ffn(1)
            dve_folded(2)
            dve_pre2()
            dve_ffn(2)
            dve_latent(3)
            dve_pre3()
            dve_ffn(3)

        @block.gpsimd
        def _(pool):
            me = own["pool"]
            me.link(pool, pool.memset(half_neg[:], -0.5))
            pool_ln(0)
            pool_pre0()
            pool_ffn(0)
            pool_folded(1)
            pool_pre1(1)
            pool_ffn(1)
            pool_folded(2)
            pool_pre2()
            pool_ffn(2)
            pool_ln(6)
            pool_pre1(3)
            pool_ffn(3)



def rope_table(length, dim, base):
    inv = (np.float32(1.0) / np.float32(base) ** (np.arange(0, dim, 2, dtype=np.float32) / np.float32(dim))).astype(np.float32)
    return (np.arange(length, dtype=np.float32)[:, None] * inv[None, :]).astype(np.float32)


def constants():
    f = np.float32
    p = np.arange(P)
    out = {"ident": np.eye(P, dtype=f)}
    lat = np.where(np.arange(L)[None, :] > p[:, None], f(-1e30), f(0))
    own = np.where(np.arange(P)[None, :] > p[:, None], f(-1e30), f(0))
    causal = np.concatenate([np.tile(lat, (1, 8)), np.tile(own, (1, 2))], 1)
    out["causal"] = causal.astype(f)
    own_head = np.where(p[:, None] // HD == np.arange(HG)[None, :], f(HD ** -0.5), f(0))
    own_half = np.where(np.arange(D)[None, :] // HD % 2 == p[:, None] // L, f(1), f(0))
    parity = np.where(p[:, None] // HD % 2 == np.arange(2)[None, :], f(1), f(0))
    out["heads_c"] = np.concatenate([own_head, own_half, parity], 1).astype(f)
    a = rope_table(L, DC, 10000.0)
    cos, sin = (np.repeat(t(a), 2, axis=-1).T.astype(f) for t in (np.cos, np.sin))
    sin = np.concatenate([-sin[:DC // 2], sin[DC // 2:]])
    out["rot_k"] = np.concatenate([np.tile(cos, (2, B)), np.tile(sin, (2, B))], 1)
    a = rope_table(S, DCQ, 10000.0)
    cos, sin = (np.repeat(t(a), 2, axis=-1).T.astype(f) for t in (np.cos, np.sin))
    sin = np.concatenate([sin[DCQ // 2:], -sin[:DCQ // 2]])
    out["rope1"] = np.stack([np.tile(t, (2, 1)).reshape(3, P, S) for t in (cos, sin)]).transpose(2, 0, 1, 3).copy()
    a = rope_table(S, HD, 1000000.0)
    a = np.concatenate([a, a], -1)
    cos, sin = np.cos(a).astype(f), np.sin(a).astype(f)
    sin = np.concatenate([-sin[:, :HD // 2], sin[:, HD // 2:]], 1)
    scale = np.array([HD ** -0.5, 1.0], f)
    cs = [(t[:, None, :] * scale[None, :, None]).reshape(QT, P, 2 * HD).transpose(1, 0, 2).reshape(P, -1) for t in (cos, sin)]
    out["self_rope"] = np.concatenate(cs, 1)
    return out


def rows_on_partitions(w):
    k, n = w.shape
    return w.reshape(k // P, P, n).transpose(1, 0, 2).reshape(P, -1)


def wide(a, rows, cols):
    out = np.zeros((rows, cols), a.dtype)
    out[:a.shape[0], :a.shape[1]] = a
    return out


def chunk_layout(gate, up, down, cols, full):
    ups, downs = [], []
    for c in range(gate.shape[1] // cols):
        at = slice(c * cols, (c + 1) * cols)
        gu = np.stack([gate[:, at], up[:, at]], 1).reshape(KT, P, 2 * cols).transpose(1, 0, 2).reshape(P, -1)
        ups.append(wide(gu, P, 4 * full))
        tiles = [wide(down[at][k * P:k * P + rows], P, D) for k, rows in k_tiles(cols)]
        downs.append(wide(np.concatenate(tiles, 1), P, len(k_tiles(full)) * D))
    return ups, downs


def layouts(a):
    d, con = {}, constants()
    f = np.float32
    d["x"] = a["x"].reshape(NT, P, D)
    cx = a["ctx_512"].transpose(2, 0, 1)
    flat = cx.reshape(DC, B * L)
    d["ctx_t"] = np.concatenate([flat, flat], 0)
    d["ctx_d"] = np.stack([cx, cx], 2)
    swapped = np.concatenate([flat[DC // 2:], flat[:DC // 2]], 0)
    d["rotk"] = np.concatenate([con.pop("rot_k"), np.concatenate([swapped, swapped], 0)], 1)
    self_rope = con.pop("self_rope")
    d.update(con)
    for n in (0, 3):
        kv = wide(a[f"L{n}_xattn_Wkv_expand"].T, P, 2 * D)
        d[f"lat{n}"] = np.concatenate([rows_on_partitions(a[f"L{n}_xattn_Wq"].T), rows_on_partitions(a[f"L{n}_xattn_Wout"].T), kv], 1)
    for n in (1, 2):
        wq = a[f"L{n}_xattn_Wq"].reshape(H, P, D)
        wo = a[f"L{n}_xattn_Wo"].T.reshape(H, P, D)
        kcq, kv = a[f"L{n}_xattn_w_kc_q"], a[f"L{n}_xattn_w_kc_kv"]
        kr, qr = a[f"L{n}_xattn_W_kr"].transpose(0, 2, 1), a[f"L{n}_xattn_W_qr"].transpose(0, 2, 1)
        heads = np.zeros((H, P, HEAD_W), f)
        if n == 1:
            heads[:, :, 0:DCQ] = kcq
        else:
            t = kcq.transpose(0, 2, 1).reshape(H, 2, DCQ // 2, P).transpose(0, 2, 1, 3)
            heads[:, :DCQ // 2, 0:2 * P] = t.reshape(H, DCQ // 2, 2 * P)
        heads[:, :, 256:512] = wq
        heads[:, :, 512:576] = kv
        heads[:, :, 576:832] = wo
        heads[:, :R, 832:896] = kr
        heads[:, :R, 896:1088] = qr
        d[f"heads{n}"] = heads.reshape(PAIRS, 2, P, HEAD_W).transpose(0, 2, 1, 3)
    g = lambda name: a[f"L0_ffn_{name}"]
    d["pre0"] = np.concatenate([rows_on_partitions(g("wv").T), rows_on_partitions(g("wo"))], 1)
    cols = lambda v: v.reshape(KT, P).T
    d["vec0"] = np.concatenate([np.repeat(cols(g("bv"))[:, :, None], P, 2).reshape(P, -1), np.tile(g("w_router"), (P, 1)),
                                np.tile(g("b_router").reshape(1, 1), (P, 1)), cols(g("norm1_w")), cols(g("norm2_w"))], 1)
    up, down = chunk_layout(g("w_gate"), g("w_up"), g("w_down"), 352, 352)
    d["up0"], d["down0"] = np.stack(up), np.stack(down)
    g = lambda name: a[f"L1_ffn_{name}"]
    gu = g("gate_up_proj")
    flat = lambda w: w.transpose(2, 0, 1).reshape(D, -1)
    up, down = chunk_layout(flat(gu[:, :64]), flat(gu[:, 64:]), g("down_proj").transpose(0, 2, 1).reshape(-1, D), 512, 512)
    su, sd = chunk_layout(g("shared_gate_w").T, g("shared_up_w").T, g("shared_down_w").T, 64, 512)
    d["up1"], d["down1"] = np.stack(up + su), np.stack(down + sd)
    d["router1"] = rows_on_partitions(np.concatenate([g("router_w").T, g("shared_expert_gate_w").T], 1))
    g = lambda name: a[f"L2_ffn_{name}"]
    d["qkv2"] = rows_on_partitions(np.concatenate([g("wq"), g("wk"), g("wv")], 1))
    d["router2"] = np.concatenate([rows_on_partitions(g("wo")), rows_on_partitions(np.concatenate([g("w_router"), g("w_sh_eg")], 1))], 1)
    d["vec2"] = np.concatenate([np.tile(np.concatenate([g("bq"), g("bk"), g("bv")]), (P, 1)), self_rope,
                                cols(g("w_ln1")), cols(g("w_ln2"))], 1)
    wide_e = lambda w: w.transpose(1, 0, 2).reshape(D, -1)
    up, down = chunk_layout(wide_e(g("w_gate_e")), wide_e(g("w_up_e")), g("w_down_e").reshape(-1, D), 352, 352)
    su, sd = chunk_layout(g("w_sh_gate"), g("w_sh_up"), g("w_sh_down"), 352, 352)
    d["up2"], d["down2"] = np.stack(up + su), np.stack(down + sd)
    g = lambda name: a[f"L3_ffn_{name}"]
    up, down = chunk_layout(wide_e(g("w1_routed")), wide_e(g("w3_routed")), g("w2_routed").reshape(-1, D), 352, 352)
    su, sd = chunk_layout(g("w1_shared"), g("w3_shared"), g("w2_shared"), 176, 352)
    d["up3"], d["down3"] = np.stack(up + su), np.stack(down + sd)
    d["router3"] = np.concatenate([rows_on_partitions(g("gate_w").T), np.tile(g("gate_b"), (P, 1))], 1)
    return {k: np.ascontiguousarray(v) for k, v in d.items()}


def kernel(**inputs):
    import concourse.bacc as bacc
    from concourse.bass_utils import run_bass_kernel_spmd

    arrays = layouts({k: np.asarray(v) for k, v in inputs.items()})
    nc = bacc.Bacc("TRN2", target_bir_lowering=False, num_devices=1)
    d = {k: nc.dram_tensor(f"in_{k}", v.shape, mybir.dt.from_np(v.dtype), kind="ExternalInput").ap() for k, v in arrays.items()}
    out = nc.dram_tensor("out", (NT, P, D), F32, kind="ExternalOutput").ap()
    build(nc, d, out)
    r = run_bass_kernel_spmd(nc, [{f"in_{k}": v for k, v in arrays.items()}], core_ids=[0])
    return r.results[0]["out"].reshape(B, S, D)
```

```python
import concourse.bass as bass
from concourse import mybir
from collections import namedtuple
from contextlib import ExitStack
import numpy as np

F32, F16, BF16 = mybir.dt.float32, mybir.dt.float16, mybir.dt.bfloat16
ALU, ACT, AX = mybir.AluOpType, mybir.ActivationFunctionType, mybir.AxisListType

P = 128
D = 256
KT = D // P
B, S, L = 4, 256, 64
NT = B * S // P
QT = S // P
H = 16
HD = 16
PAIRS = H // 2
G = H * HD // P
HG = H // G
DC, DCQ, R = 64, 192, 64
HEAD_W = 1088
SPLIT = 64.0
UNSPLIT = 1.0 / (SPLIT * SPLIT)
LN_EPS, RMS_EPS = 1e-5, 1e-6


class Count:

    def __init__(self, sem):
        self.sem, self.done, self.turn, self.steps = sem, 0, 0, 0

    def open(self, turn, steps):
        self.turn, self.steps, self.begun = turn, steps, self.done

    def close(self, turns):
        assert self.done - self.begun == self.steps, (self.sem, self.done - self.begun)
        self.done, self.turn, self.steps = self.begun + turns * self.steps, 0, 0

    def link(self, engine, instruction):
        instruction.then_inc(self.sem, 1)
        self.done += 1
        engine.wait_ge(self.sem, self.done + (self.turn * self.steps if self.steps else 0))


class Ffn:

    def __init__(self, name, chunks, experts, width, last=None, both=False):
        self.name, self.chunks, self.experts, self.width = name, chunks, experts, width
        self.last_experts = last or experts
        self.both = both
        self.steps = chunks * NT

    def cols(self, c):
        last = isinstance(c, int) and c == self.chunks - 1
        return (self.last_experts if last else self.experts) * self.width


FFNS = [Ffn("ffn0", 2, 2, 352 // 2), Ffn("ffn1", 9, 8, 64, last=1),
        Ffn("ffn2", 6, 2, 352 // 2), Ffn("ffn3", 9, 2, 352 // 2, last=1, both=True)]


def k_tiles(cols):
    return [(k, min(P, cols - k * P)) for k in range((cols + P - 1) // P)]


def build(nc, d, out):
    ctx = ExitStack()
    with ctx:
        def sb(name, shape, dt=F32):
            return ctx.enter_context(nc.sbuf_tensor(name, shape, dt))

        def Sems(part, names):
            return namedtuple(part, names)(*(ctx.enter_context(nc.semaphore(f"{part}_{n}")) for n in names.split()))

        x = sb("x", [P, NT, D])
        xn = sb("xn", [P, NT, D])
        xT = sb("xT", [P, KT, NT, P])
        ident = sb("ident", [P, P])
        ident_b = sb("ident_b", [P, P], BF16)
        causal_b = sb("causal_b", [P, 8 * L + 2 * P], BF16)
        mask_lat = causal_b[:, 0:8 * L]
        mask_self = causal_b[:, 8 * L:]
        heads_c = sb("heads_c", [P, HG + D + 2])
        own_head = heads_c[:, 0:HG]
        own_half = heads_c[:, HG:HG + D]
        parity = heads_c[:, HG + D:HG + D + 2]
        primer = sb("primer", [P, 8])
        half_neg = sb("half_neg", [P, NT])
        ctx_t = sb("ctx_t", [P, B * L])
        ctx_d = sb("ctx_d", [L, B, 2, L])
        kvr = sb("kvr", [P, B * L])
        stats = sb("stats", [P, NT, 6])
        meanvar = sb("meanvar", [P, NT, 2])
        var_e = sb("var_e", [P, NT])
        rstd = sb("rstd", [P, NT])
        rms_e = sb("rms_e", [P, NT])
        rms_r = sb("rms_r", [P, NT])
        gates = sb("gates", [P, 9, NT, 8])
        w_stage = sb("w_stage", [P, 2048])
        w_down = sb("w_down", [P, 2, 1024])
        arena = sb("arena", [P, 39424])

        def take(at, shape, dt=F32):
            n = int(np.prod(shape)) // (1 if dt == F32 else 2)
            a = arena[:, at:at + n]
            if dt != F32:
                a = a.bitcast(dt)
            if len(shape) > 1:
                names = " ".join("abcdefg"[:len(shape)])
                kw = {"abcdefg"[i]: shape[i] for i in range(1, len(shape))}
                a = a.rearrange(f"p ({names}) -> p {names}", **kw)
            return a, at + n

        at = 0
        w_split, at = take(at, [2, 2, 2048], F16)
        xh, at = take(at, [KT, NT, P], F16)
        xl, at = take(at, [KT, NT, P], F16)
        m_t, at = take(at, [2, 512])
        m_a, at = take(at, [2, 512])
        m_b, at = take(at, [2, 512])
        m_c, at = take(at, [2, 512])
        hidT, at = take(at, [2, 4, P])
        ffn_w, at = take(at, [4096])
        ffn_v, at = take(at, [2048])
        ffn_s, at = take(at, [6144])

        at = 0
        at_w, at = take(at, [6144])
        at_m, at = take(at, [16384])
        at_f, at = take(at, [8192])
        at_p, at = take(at, [2, 1024])
        at_pt, at = take(at, [2, 1024])
        tables = xn.rearrange("p t c -> p (t c)")[:, 0:2 * 3 * S].rearrange("p (a t c) -> p a t c", a=2, t=3)
        at_o, _ = take(at, [2, 512])
        at_r, at = take(at + 1536, [2, 2, 3, 256])
        heads = arena[:, 30720:30720 + 4 * HEAD_W].rearrange("p (s h c) -> p s h c", s=2, h=2)
        at = 30720 + 4 * HEAD_W
        kv_diag, at = take(at, [B, P])
        bt, at = take(at, [2, 2, DCQ])
        e_pair, at = take(at, [D])
        bb, at = take(at, [2, 2, DC])
        cc, at = take(at, [2, DC])
        dt_, at = take(at, [2, D])
        small = sb("small", [P, 2, 4, H])
        causal_f = w_stage[:, 1024:1024 + 8 * L + 2 * P]
        rot_in = w_stage

        PS = ctx.enter_context(nc.psum_tensor("PS", [P, 8, 512], F32))

        def bank(n, k=1):
            return PS[:, n:n + k, :].rearrange("p b c -> p (b c)")

        load = Sems("load", "x const ctx rot out")
        kvs = Sems("kv", "rot")
        kv_diag_done = {n: ctx.enter_context(nc.semaphore(f"kv_diag{n}")) for n in (1, 2)}
        own = {n: Count(ctx.enter_context(nc.semaphore(f"own_{n}"))) for n in ("dve", "pool")}
        ln = Sems("ln", "var rstd xn xT_ps xT")
        ln_T_before = {0: 0, 2: 8, 3: 16, 4: 24, 6: 32, 7: 40}
        ln_xT_before = {0: 0, 2: 4, 3: 8, 4: 16, 6: 20, 7: 24}
        soft = Sems("soft", "sub p sums t_ps t y_ps x")
        turns_before = {0: 0, 2: NT, 3: 2 * NT}
        norm = Sems("norm", "pn")
        lat = Sems("lat", "w kv_ps kv q_ps q_sb q v s o_ps ot")
        att = {1: Sems("att1", "w0 w1 zero a_ps a bt_ps bt e_ps e m_ps m f_ps f tab q_ps roped s t_ps t"),
               2: Sems("att2", "w0 w1 zero bt_ps bt e_ps e m_ps m f_ps f c_ps c dt_ps dt q s")}
        pre = [Sems("pre0", "w fold_ps fold ms r z zT_ps zT y_ps ssq rr z2 z2T_ps h gates"),
               Sems("pre1", "w h logit lg e t gates"),
               Sems("pre2", "w hT z zT_ps ms r stage qkv biased qr qrT_ps qT s mx p pt_ps pt one oneT_ps oneT v o_ps o y_ps x2 "
                    "ssq rr z2 z2T_ps h f logit lg e t gates"),
               Sems("pre3", "w h logit lg t gates")]
        ffn = Sems("ffn", "w_in w_hi w_lo dn_in gu g act t prod hid hidT_ps hidT down x")
        chunks_before = [sum(f.chunks for f in FFNS[:n]) for n in range(5)]
        steps_before = [sum(f.steps for f in FFNS[:n]) for n in range(5)]

        def x_ready(engine, m, i=NT - 1):
            n = (m - 1) // 2
            if m == 0:
                engine.wait_ge(load.x, 16)
            elif m % 2:
                engine.wait_ge(soft.x, NT * n + i + 1)
            else:
                engine.wait_ge(ffn.x, steps_before[n + 1] - NT + i + 1)

        def hold(engine, sem, value):
            engine.wait_ge(load.const, 48)
            engine.wait_ge(sem, value)

        primed = [0]

        def prime(*sems):
            for sem in sems:
                nc.gpsimd.memset(primer[:, primed[0]:primed[0] + 1], 0.0).then_inc(sem, 1)
                primed[0] += 1

        def span(at, n):
            return slice(at, at + n) if isinstance(at, int) else bass.ds(at, n)

        def at_batch(b):
            return span(b, 1)

        def tile_of(b, q):
            return span(QT * b + q, 1)

        def over(ap, axis, n):
            a = ap.unsqueeze(axis)
            shape = list(a.shape)
            shape[axis] = n
            return a.broadcast_to(shape)

        block = ctx.enter_context(nc.Block())


        def dve_stats(m, i):
            x_ready(nc.vector, m, i)
            at = slice(i, i + 1) if isinstance(i, int) else bass.ds(i, 1)
            ins = nc.vector.bn_stats(stats[:, at, :].rearrange("p t c -> p (t c)"), x[:, at, :].rearrange("p t c -> p (t c)"))
            if isinstance(i, int) and i == NT - 1:
                own["dve"].link(nc.vector, ins)

        def dve_ln(m):
            s, me = ln, own["dve"]
            if m == 0:
                x_ready(nc.vector, 0)
                for i in range(NT):
                    ins = nc.vector.bn_stats(stats[:, i, :], x[:, i, :])
                me.link(nc.vector, ins)
            for i in range(NT):
                ins = nc.vector.bn_aggr(meanvar[:, i, :], stats[:, i, :])
            me.link(nc.vector, ins)
            nc.vector.tensor_scalar(var_e[:], meanvar[:, :, 1], LN_EPS, None, ALU.add).then_inc(s.var, 1)
            nc.vector.wait_ge(s.rstd, m + 1)
            for i in range(NT):
                nc.vector.tensor_scalar(xn[:, i, :], x[:, i, :], meanvar[:, i, 0:1], rstd[:, i:i + 1],
                                        ALU.subtract, ALU.mult).then_inc(s.xn, 1)

        def pool_ln(m):
            nc.gpsimd.wait_ge(ln.var, m + 1)
            nc.gpsimd.tensor_tensor(rstd[:], var_e[:], half_neg[:], ALU.pow).then_inc(ln.rstd, 1)

        def pe_transpose_tiles(src, ready, before, done):
            for i in range(NT):
                nc.tensor.wait_ge(ready, before + i + 1)
                for k in range(KT):
                    ins = nc.tensor.transpose(PS[:, i // 2, (i % 2) * D + k * P:(i % 2) * D + (k + 1) * P],
                                              src[:, i, k * P:(k + 1) * P], ident[:])
                ins.then_inc(done, 1)

        def pair_ps(j):
            return PS[:, j, :].rearrange("p (t k c) -> p k t c", t=2, k=KT)

        def act_ln(m):
            for j in range(NT // 2):
                nc.scalar.wait_ge(ln.xT_ps, ln_T_before[m] + 2 * j + 2)
                nc.scalar.activation(xT[:, :, 2 * j:2 * j + 2, :], pair_ps(j), ACT.Copy).then_inc(ln.xT, 1)

        lat_w = at_w[:, 4096:5632]
        lat_wq = lat_w[:, 0:KT * D].rearrange("p (k c) -> p k c", k=KT)
        lat_wo = lat_w[:, 512:512 + G * D].rearrange("p (k c) -> p k c", k=G)
        lat_wkv = lat_w[0:L, 1024:1536]
        lat_k = at_m[:, 0:B * G * HG * L].rearrange("p (b g h l) -> p b g h l", b=B, g=G, h=HG)
        lat_v = at_f[:, 0:B * D].rearrange("p (b c) -> p b c", b=B)
        lat_qs = at_f[:, B * D:B * D + B * QT * G * P].rearrange("p (b q g c) -> p b q g c", b=B, q=QT, g=G)
        lat_q = at_o[:, 0, :].rearrange("p (q g c) -> p q g c", q=QT, g=G)
        lat_vb = at_o[:, 1, 0:D]
        lat_oT = at_r[:, 0, 0, 0:2, :].rearrange("p q (g c) -> p q g c", g=G)

        def heads_of(ap):
            return ap.rearrange("p (h l) -> p h l", h=H)

        def pool_normalise(n):
            pool = nc.gpsimd
            with pool.Fori(0, B) as b:
                for q in range(QT):
                    pool.wait_ge(soft.sums, NT * n + 2 * b + q + 1)
                    pool.tensor_tensor(heads_of(at_p[:, q, :]), heads_of(at_p[:, q, :]),
                                       over(small[:, q, 2, :], 2, L), ALU.mult).then_inc(norm.pn, 1)

        def sp_latent(n):
            if n:
                x_ready(nc.sync, 2 * n)
            nc.sync.dma_start(lat_w, d[f"lat{n}"]).then_inc(lat.w, 16)

        def pe_latent(n):
            pe, s, again = nc.tensor, lat, n // 3
            x_ready(pe, 2 * n)
            pe.wait_ge(load.ctx, 32)
            pe.wait_ge(s.w, 16 * again + 16)
            for g in range(G):
                ins = pe.matmul(PS[:, 4, g * B * L:(g + 1) * B * L], lat_wkv[:, g * P:(g + 1) * P], ctx_t[0:L, :],
                                start=True, stop=True)
            ins.then_inc(s.kv_ps, 1)
            for b in range(B):
                ins = pe.matmul(PS[:, 5 + b // 2, (b % 2) * D:(b % 2 + 1) * D],
                                ctx_d[:, b, :, :].rearrange("p a l -> p (a l)"), lat_wkv[:, D:2 * D],
                                start=True, stop=True)
            ins.then_inc(s.kv_ps, 1)
            pe.wait_ge(load.const, 48)
            pe_transpose_tiles(xn, ln.xn, 2 * n * NT, ln.xT_ps)
            pe.wait_ge(ln.xT, ln_xT_before[2 * n] + NT // 2)
            pe.wait_ge(kvs.rot, 1)
            pe.wait_ge(s.kv, 4 * again + 4)
            for t in range(2):
                for g in range(G):
                    for k in range(KT):
                        ins = pe.matmul(PS[:, 1 + 2 * t + g, :], lat_wq[:, k, g * P:(g + 1) * P],
                                        xT[:, k, t * NT // 2:(t + 1) * NT // 2, :].rearrange("p t c -> p (t c)"),
                                        start=(k == 0), stop=(k == KT - 1))
                    ins.then_inc(s.q_ps, 1)

            def scores(b, q):
                pe.wait_ge(s.q, (B + 1) * again + b + 1)
                for g in range(G):
                    ins = pe.matmul(PS[:, 1 + 2 * q + g, :], lat_q[:, q, g, :],
                                    lat_k[:, at_batch(b), g, :, :].rearrange("p b h l -> p (b h l)"),
                                    start=True, stop=(q > 0))
                    if q == 0:
                        ins = pe.matmul(PS[:, 1 + g, :], ident_b[:], mask_lat, start=False, stop=True)
                ins.then_inc(s.s, 1)

            def transposed(b, q):
                pe.wait_ge(norm.pn, NT * n + 2 * b + q + 1)
                for j in range(PAIRS):
                    ins = pe.transpose(PS[:, 5 + j // 4, (j % 4) * P:(j % 4 + 1) * P],
                                       at_p[:, q, j * P:(j + 1) * P], ident[:])
                ins.then_inc(soft.t_ps, 1)

            def times_values(b, q):
                pe.wait_ge(soft.t, turns_before[n] + 2 * b + q + 1)
                if q == 0:
                    pe.wait_ge(s.v, B * again + b + 1)
                for j in range(PAIRS):
                    ins = pe.matmul(PS[32 * (j % 4):32 * (j % 4) + 32, 7, (j // 4) * P:(j // 4 + 1) * P],
                                    lat_vb[:, j * 2 * HD:(j + 1) * 2 * HD], at_pt[:, q, j * P:(j + 1) * P],
                                    start=True, stop=True)
                ins.then_inc(s.o_ps, 1)

            def output(b, q):
                pe.wait_ge(s.ot, NT * again + 2 * b + q + 1)
                if q:
                    pe.wait_ge(soft.x, NT * n + 2 * b + 1)
                for g in range(G):
                    ins = pe.matmul(PS[:, 0, D:2 * D], lat_oT[:, q, g, :], lat_wo[:, g, :],
                                    start=(g == 0), stop=(g == G - 1))
                ins.then_inc(soft.y_ps, 1)

            def batch(b, last=False):
                if not last:
                    scores(b + 1, 0)
                times_values(b, 0)
                transposed(b, 1)
                if not last:
                    scores(b + 1, 1)
                output(b, 0)
                times_values(b, 1)
                output(b, 1)
                if not last:
                    transposed(b + 1, 0)
                pe.wait_ge(soft.x, NT * n + 2 * b + 2)

            pe.wait_ge(s.q_sb, 4 * again + 4)
            scores(0, 0)
            scores(0, 1)
            transposed(0, 0)
            with pe.Fori(0, B - 1) as b:
                batch(b)
            batch(B - 1, last=True)

        def act_latent(n):
            act, s, again = nc.scalar, lat, n // 3
            act_ln(2 * n)
            for t in range(2):
                for g in range(G):
                    act.wait_ge(s.q_ps, 4 * again + 2 * t + g + 1)
                    act.activation(lat_qs[:, t * B // 2:(t + 1) * B // 2, :, g, :],
                                   PS[:, 1 + 2 * t + g, :].rearrange("p (b q c) -> p b q c", b=B // 2, q=QT),
                                   ACT.Copy).then_inc(s.q_sb, 1)

            def stage(b):
                if not isinstance(b, int) or b:
                    hold(act, s.s, NT * again + 2 * b)
                act.activation(lat_q.rearrange("p q g c -> p (q g c)"),
                               lat_qs[:, at_batch(b % B)].rearrange("p b q g c -> p (b q g c)"), ACT.Copy).then_inc(s.q, 1)

            def exponential(b, q):
                act.wait_ge(soft.sub, NT * n + 2 * b + q + 1)
                act.activation(at_p[:, q, :], at_p[:, q, :], ACT.Exp).then_inc(soft.p, 1)

            def stage_values(b):
                act.activation(lat_vb, lat_v[:, at_batch(b % B), :].rearrange("p b c -> p (b c)"), ACT.Copy).then_inc(s.v, 1)

            def batch(b, last=False):
                for q in range(QT):
                    act.wait_ge(soft.t_ps, turns_before[n] + 2 * b + q + 1)
                    act.activation(at_pt[:, q, :], bank(5, 2), ACT.Copy).then_inc(soft.t, 1)
                    act.wait_ge(s.o_ps, NT * again + 2 * b + q + 1)
                    act.activation(lat_oT[:, q, :, :], PS[:, 7, 0:D].rearrange("p (g c) -> p g c", g=G),
                                   ACT.Copy).then_inc(s.ot, 1)
                    if not last:
                        if q:
                            stage_values(b + 1)
                        exponential(b + 1, q)
                if not last:
                    stage(b + 2)

            act.wait_ge(s.q_sb, 4 * again + 4)
            stage(0)
            act.wait_ge(s.kv, 4 * again + 4)
            stage_values(0)
            act_split(n, 0)
            exponential(0, 0)
            exponential(0, 1)
            stage(1)
            with act.Fori(0, B - 1) as b:
                batch(b)
            batch(B - 1, last=True)

        def dve_scores(ready, me, q, count, first_bank):
            scores = heads_of(bank(first_bank, 2))
            nc.vector.wait_ge(ready, count)
            me.link(nc.vector, nc.vector.tensor_reduce(small[:, q, 0, :], scores, AX.X, ALU.max))
            nc.vector.tensor_tensor(heads_of(at_p[:, q, :]), scores, over(small[:, q, 0, :], 2, L),
                                    ALU.subtract).then_inc(soft.sub, 1)

        def dve_sums(me, q, count):
            nc.vector.wait_ge(soft.p, count)
            me.link(nc.vector, nc.vector.tensor_reduce(small[:, q, 1, :], heads_of(at_p[:, q, :]), AX.X, ALU.add))
            nc.vector.reciprocal(small[:, q, 2, :], small[:, q, 1, :]).then_inc(soft.sums, 1)

        def dve_masks():
            dve, me = nc.vector, own["dve"]
            dve.wait_ge(load.ctx, 32)
            dve.wait_ge(load.rot, 16)
            cos_k, sin_k, swapped = (rot_in[:, a * B * L:(a + 1) * B * L] for a in range(3))
            me.link(dve, dve.tensor_tensor(sin_k, sin_k, swapped, ALU.mult))
            me.link(dve, dve.tensor_tensor(kvr[:], ctx_t[:], cos_k, ALU.mult))
            dve.wait_ge(load.const, 48)
            dve.tensor_copy(ident_b[:], ident[:])
            dve.tensor_copy(causal_b[:], causal_f)
            dve.tensor_tensor(kvr[:], kvr[:], sin_k, ALU.add).then_inc(kvs.rot, 1)
            dve.wait_ge(kvs.rot, 1)

        def dve_latent(n):
            dve, s, again, me = nc.vector, lat, n // 3, own["dve"]
            x_ready(dve, 2 * n)
            dve.wait_ge(load.const, 48)
            dve.wait_ge(s.kv_ps, 2 * again + 1)
            for g in range(G):
                dve.tensor_tensor(lat_k[:, :, g, :, :],
                                  over(PS[:, 4, g * B * L:(g + 1) * B * L].rearrange("p (b l) -> p b l", b=B), 2, HG),
                                  over(over(own_head, 1, B), 3, L), ALU.mult).then_inc(s.kv, 1)
            dve.wait_ge(s.kv_ps, 2 * again + 2)
            for j in range(2):
                dve.tensor_tensor(lat_v[:, 2 * j:2 * j + 2, :], PS[:, 5 + j, :].rearrange("p (b c) -> p b c", b=2),
                                  over(own_half, 1, 2), ALU.mult).then_inc(s.kv, 1)
            dve_ln(2 * n)

            if n == 0:
                dve_masks()

            def scores(b, q):
                if not (isinstance(b, int) and b == 0):
                    dve.wait_ge(soft.t_ps, turns_before[n] + 2 * b + q - 1)
                dve_scores(s.s, me, q, NT * again + 2 * b + q + 1, 1 + 2 * q)

            def added(b, q):
                dve.wait_ge(soft.y_ps, NT * n + 2 * b + q + 1)
                tile = x[:, tile_of(b, q), :]
                dve.tensor_tensor(tile, tile, PS[:, 0:1, D:2 * D], ALU.add).then_inc(soft.x, 1)
                dve_stats(2 * n + 1, QT * b + q)

            def batch(b, last=False):
                if last:
                    added(b, 0)
                else:
                    scores(b + 1, 0)
                    added(b, 0)
                    dve_sums(me, 0, NT * n + 2 * b + 3)
                    scores(b + 1, 1)
                    dve_sums(me, 1, NT * n + 2 * b + 4)
                added(b, 1)

            scores(0, 0)
            scores(0, 1)
            dve_sums(me, 0, NT * n + 1)
            dve_sums(me, 1, NT * n + 2)
            dve_split(n, 0)
            with dve.Fori(0, B - 1) as b:
                me.open(b, 4)
                batch(b)
            me.close(B - 1)
            batch(B - 1, last=True)

        fold_a = at_w.rearrange("p (k c) -> p k c", k=KT)
        fold_m = at_m.rearrange("p (b j s c) -> p b j s c", b=B, j=PAIRS, s=2)
        fold_n = arena[:, 0:B * KT * H * L].rearrange("p (b k c) -> p b k c", b=B, k=KT)
        fold_f = at_f.rearrange("p (b j c) -> p b j c", b=B, j=PAIRS)
        fold_x = at_o[:, 0, :].rearrange("p (k q c) -> p k q c", k=KT, q=QT)
        W_KCQ, W_Q, W_KV, W_O, W_KR, W_QR = 0, 256, 512, 576, 832, 896

        def head_w(slot, h, at, cols, rows=P):
            return heads[0:rows, slot, h, at:at + cols]

        def over_pairs(engine, body):
            for j in range(2):
                body(0, j)
            with engine.Fori(1, PAIRS // 2) as i:
                for j in range(2):
                    body(i, j)

        def sp_heads(n):
            sp, s = nc.sync, att[n]
            x_ready(sp, 2 * n - 1)
            for j in range(2):
                sp.dma_start(heads[:, j, :, :], d[f"heads{n}"][j]).then_inc((s.w0, s.w1)[j], 16)

        def sp_folded(n):
            sp, s = nc.sync, att[n]
            if n == 1:
                sp.wait_ge(ln.xT, ln_xT_before[2] + NT // 2)
                sp.dma_start(tables, d["rope1"]).then_inc(s.tab, 16)
            with sp.Fori(1, PAIRS // 2) as i:
                for j in range(2):
                    sp.wait_ge(s.a_ps if n == 1 else s.dt_ps, 2 * i + j - 1)
                    sp.dma_start(heads[:, j, :, :], d[f"heads{n}"][bass.ds(2 * i + j, 1), :, :, :]
                                 .rearrange("a p h c -> p (a h) c")).then_inc((s.w0, s.w1)[j], 16)

        def pool_folded(n):
            pool, s = nc.gpsimd, att[n]
            x_ready(pool, 2 * n)
            pool_ln(2 * n)
            prime(*((s.f, s.m, s.a) if n == 1 else (s.f, s.m)))
            pool.memset(kv_diag, 0.0).then_inc(s.zero, 1)
            if n == 1:
                for b in range(B):
                    pool.memset(fold_m[:, b, :, :, L:3 * L], 0.0).then_inc(s.zero, 1)
            pool_normalise(n)

        def pe_fold_values(n, j, q):
            pe, s = nc.tensor, att[n]
            for h in range(2):
                if h and n == 1:
                    pe.wait_ge(s.f, 2 * q + 1)
                ins = pe.matmul(PS[L * h:L * (h + 1), 6, 0:D], head_w(j, h, W_KV, DC), head_w(j, h, W_O, D),
                                start=True, stop=True)
            ins.then_inc(s.e_ps, 1)

        def pe_values(n, q, first, second):
            pe, s = nc.tensor, att[n]
            pe.wait_ge(s.e, q + 1)
            for b in range(B):
                ins = pe.matmul(PS[:, (first, second)[b // 2], (b % 2) * D:(b % 2 + 1) * D], kv_diag[:, b, :], e_pair,
                                start=True, stop=True)
            ins.then_inc(s.f_ps, 1)

        def pe_fold1(i, j):
            pe, s = nc.tensor, att[1]
            q = 2 * i + j
            pe.wait_ge((s.w0, s.w1)[j], 16 * i + 16)
            pe.wait_ge(s.a, q + 1)

            def folded(k):
                for h in range(2):
                    ins = pe.matmul(PS[:, k, h * DCQ:(h + 1) * DCQ], head_w(j, h, W_Q + k * P, P),
                                    head_w(j, h, W_KCQ, DCQ), start=True, stop=True)
                return ins

            folded(0)
            pe_fold_values(1, j, q)
            for h in range(2):
                ins = pe.matmul(PS[0:DC, 2, h * DCQ:(h + 1) * DCQ], head_w(j, h, W_KR, DC, R),
                                head_w(j, h, W_QR, DCQ, R), start=True, stop=True)
            ins.then_inc(s.bt_ps, 1)
            folded(1).then_inc(s.a_ps, 1)
            pe.wait_ge(s.bt, 3 * q + 3)
            pe.wait_ge(s.m, 4 * q + 1)
            for c in range(2):
                for h, tile, rows, at, cols in ((0, 0, P, 0, P), (0, 1, DC, 0, DC), (1, 1, DC, DC, DC), (1, 2, P, 0, P)):
                    first = (0, P)[tile > 0] if h == 0 else (0, DC)[tile > 1]
                    ins = pe.matmul(PS[at:at + cols, 3 + tile, c * B * L:(c + 1) * B * L],
                                    bt[0:DC, c, h, first:first + cols], kvr[0:DC, :], start=True, stop=True)
            ins.then_inc(s.m_ps, 1)
            pe_values(1, q, 7, 2)

        def act_fold1(i, j):
            act, s = nc.scalar, att[1]
            q = 2 * i + j
            act.wait_ge(s.bt_ps, q + 1)
            act.activation(bt[0:DC, 0, :, :], PS[0:DC, 2, 0:2 * DCQ].rearrange("p (h c) -> p h c", h=2),
                           ACT.Copy).then_inc(s.bt, 1)
            hold(act, s.a_ps, q + 1)
            act.activation(fold_a[:, :, span(q * 2 * DCQ, 2 * DCQ)], PS[:, 0:KT, 0:2 * DCQ], ACT.Copy).then_inc(s.a, 1)
            for c in range(2):
                hold(act, s.f_ps, q + 1)
                act.activation(fold_f[:, 2 * c:2 * c + 2, span(q, 1), :],
                               PS[:, (7, 2)[c], :].rearrange("p (b a c) -> p b a c", b=2, a=1), ACT.Copy).then_inc(s.f, 1)

        def dve_fold1(i, j):
            dve, s = nc.vector, att[1]
            q = 2 * i + j
            half = DCQ // 2
            dve.wait_ge(s.e_ps, q + 1)
            dve.tensor_copy(e_pair, PS[:, 6, 0:D]).then_inc(s.e, 1)
            dve.wait_ge(s.bt, 3 * q + 1)
            for c in range(2):
                dve.tensor_copy(bt[0:DC, 1, :, (1 - c) * half:(2 - c) * half],
                                bt[0:DC, 0, :, c * half:(c + 1) * half]).then_inc(s.bt, 1)
            dve.wait_ge(s.m_ps, q + 1)
            for rows, tile, at in ((slice(0, P), 3, 0), (slice(0, DC), 4, L), (slice(DC, P), 4, 2 * L), (slice(0, P), 5, 3 * L)):
                for c in range(2):
                    ins = dve.tensor_scalar(fold_m[rows, :, span(q, 1), c, at:at + L],
                                            PS[rows, tile, c * B * L:(c + 1) * B * L].rearrange("p (b a l) -> p b a l", b=B, a=1),
                                            1.0, None, ALU.mult)
                ins.then_inc(s.m, 1)

        def pe_fold2(i, j):
            pe, s = nc.tensor, att[2]
            q = 2 * i + j
            half = DCQ // 2
            pe.wait_ge((s.w0, s.w1)[j], 16 * i + 16)
            pe.wait_ge(s.f, 2 * q + 1)
            for h in range(2):
                for k in range(2):
                    at = (h * 2 + k) * DC
                    ins = pe.matmul(PS[0:half, 2, at:at + DC], head_w(j, h, W_QR + k * half, half, R),
                                    head_w(j, h, W_KR, DC, R), start=True, stop=True)
            ins.then_inc(s.bt_ps, 1)
            pe_fold_values(2, j, q)
            if not (isinstance(q, int) and q == 0):
                pe_keys2(q - 1)
            pe.wait_ge(s.bt, q + 1)
            for h in range(2):
                for k in range(2):
                    ins = pe.matmul(PS[:, 3, h * DC:(h + 1) * DC], head_w(j, h, W_KCQ + k * P, P, half),
                                    bb[0:half, h, k, :], start=(k == 0), stop=(k == 1))
            ins.then_inc(s.c_ps, 1)
            pe_values(2, q, 7, 5)
            pe.wait_ge(s.c, q + 1)
            for h in range(2):
                ins = pe.matmul(PS[0:DC, 4, h * D:(h + 1) * D], cc[:, h, :], head_w(j, h, W_Q, D), start=True, stop=True)
            ins.then_inc(s.dt_ps, 1)

        def pe_keys2(q):
            pe, s = nc.tensor, att[2]
            pe.wait_ge(s.dt, q + 1)
            pe.wait_ge(s.m, 2 * q + 1)
            for k in range(KT):
                for h in range(2):
                    ins = pe.matmul(PS[:, k, h * B * L:(h + 1) * B * L], dt_[0:DC, h, k * P:(k + 1) * P], kvr[0:DC, :],
                                    start=True, stop=True)
            ins.then_inc(s.m_ps, 1)

        def act_fold2(i, j):
            act, s = nc.scalar, att[2]
            q = 2 * i + j
            act.wait_ge(s.bt_ps, q + 1)
            act.activation(bb[0:DCQ // 2, :, :, :], PS[0:DCQ // 2, 2, 0:4 * DC].rearrange("p (h k c) -> p h k c", h=2, k=2),
                           ACT.Copy).then_inc(s.bt, 1)
            for c in range(2):
                hold(act, s.f_ps, q + 1)
                act.activation(fold_f[:, 2 * c:2 * c + 2, span(q, 1), :],
                               PS[:, (7, 5)[c], :].rearrange("p (b a c) -> p b a c", b=2, a=1), ACT.Copy).then_inc(s.f, 1)
            act.wait_ge(s.dt_ps, q + 1)
            act.activation(dt_[0:DC, :, :], PS[0:DC, 4, :].rearrange("p (h c) -> p h c", h=2), ACT.Copy).then_inc(s.dt, 1)

        def dve_fold2(i, j):
            dve, s = nc.vector, att[2]
            q = 2 * i + j
            dve.wait_ge(s.e_ps, q + 1)
            dve.tensor_copy(e_pair, PS[:, 6, 0:D]).then_inc(s.e, 1)
            if not (isinstance(q, int) and q == 0):
                dve_keys2(q - 1)
            dve.wait_ge(s.c_ps, q + 1)
            dve.tensor_copy(cc, PS[:, 3, 0:2 * DC].rearrange("p (h c) -> p h c", h=2)).then_inc(s.c, 1)

        def dve_keys2(q):
            dve, s = nc.vector, att[2]
            dve.wait_ge(s.m_ps, q + 1)
            for k in range(KT):
                for h in range(2):
                    ins = dve.tensor_scalar(fold_n[:, :, k, span((2 * q + h) * L, L)],
                                            PS[:, k, h * B * L:(h + 1) * B * L].rearrange("p (b l) -> p b l", b=B),
                                            1.0, None, ALU.mult)
                ins.then_inc(s.m, 1)

        def pe_folded(n):
            pe, s = nc.tensor, att[n]
            x_ready(pe, 2 * n)
            pe_transpose_tiles(xn, ln.xn, 2 * n * NT, ln.xT_ps)
            pe.wait_ge(ln.xT, ln_xT_before[2 * n] + NT // 2)
            pe.wait_ge(s.zero, 5 if n == 1 else 1)
            pe.wait_ge(kvs.rot, 1)
            pe.wait_ge(kv_diag_done[n], 2)
            over_pairs(pe, pe_fold1 if n == 1 else pe_fold2)
            if n == 2:
                pe_keys2(PAIRS - 1)
                pe.wait_ge(s.m, 2 * PAIRS + 1)
            else:
                pe.wait_ge(s.m, 4 * PAIRS + 1)
                pe.wait_ge(s.a, PAIRS + 1)
            pe.wait_ge(s.f, 2 * PAIRS + 1)
            if n == 1:
                pe.wait_ge(s.tab, 16)
            (pe_rotated if n == 1 else pe_plain)()


        LAST_T, LAST_Y = ((6, 4), (5, 0)), (7, 1)

        def pe_rotated():
            pe, s = nc.tensor, att[1]

            def queries(b, j):
                for q in range(QT):
                    if j:
                        pe.wait_ge(s.roped, 4 * PAIRS * b + 4 * (j - 1) + 2 * (q + 1))
                    for t in range(3):
                        for k in range(KT):
                            ins = pe.matmul(PS[:, 4 + q, t * P:(t + 1) * P],
                                            fold_a[:, k, (3 * j + t) * P:(3 * j + t + 1) * P],
                                            xT[:, k, tile_of(b, q), :].rearrange("p t c -> p (t c)"),
                                            start=(k == 0), stop=(k == KT - 1))
                    ins.then_inc(s.q_ps, 1)

            def scores(b, j):
                pe.wait_ge(s.roped, 4 * PAIRS * b + 4 * (j + 1))
                for q in range(QT):
                    if j == 0 and not isinstance(b, int):
                        pe.wait_ge(soft.sub, NT + 2 * b - QT + q + 1)
                    for n_, (c, t, at, cols) in enumerate(((0, 1, 1, 2), (0, 0, 0, 1), (0, 2, 3, 1),
                                                           (1, 0, 0, 1), (1, 2, 3, 1), (1, 1, 1, 2))):
                        to = (j % 4) * P + (L if t == 2 else 0)
                        ins = pe.matmul(PS[:, 2 * q + j // 4, to:to + cols * L],
                                        at_r[:, j % 2, c, t, q * P:(q + 1) * P],
                                        fold_m[:, at_batch(b), j, c, at * L:(at + cols) * L]
                                        .rearrange("p b c -> p (b c)"), start=(n_ == 0), stop=(n_ == 5))
                if j == PAIRS - 1:
                    ins.then_inc(s.s, 1)

            def transposed(b, q, half, bank_=6):
                pe.wait_ge(norm.pn, NT + 2 * b + q + 1)
                for j in range(4 * half, 4 * half + 4):
                    ins = pe.transpose(PS[:, bank_, (j % 4) * P:(j % 4 + 1) * P], at_p[:, q, j * P:(j + 1) * P], ident[:])
                ins.then_inc(s.t_ps, 1)

            def output(b, q, half, bank_=7):
                pe.wait_ge(s.t, 4 * b + 2 * q + half + 1)
                if half == 0 and bank_ == 7:
                    pe.wait_ge(soft.x, NT + 2 * b + q)
                for j in range(4 * half, 4 * half + 4):
                    ins = pe.matmul(PS[:, bank_, 0:D], at_pt[:, q, j * P:(j + 1) * P],
                                    fold_f[:, at_batch(b), j, :].rearrange("p b c -> p (b c)"),
                                    start=(j == 0), stop=(j == PAIRS - 1))
                if half:
                    ins.then_inc(soft.y_ps, 1)

            def batch(b, tail):
                for j in range(PAIRS):
                    queries(b, j)
                    if j:
                        scores(b, j - 1)
                    if tail and j in (3, 4, 6, 7):
                        output(b - 1, *divmod((3, 4, 6, 7).index(j), 2))
                    if tail and j in (2, 3, 5, 6):
                        transposed(b - 1, *divmod((2, 3, 5, 6).index(j), 2))
                scores(b, PAIRS - 1)

            batch(0, tail=False)
            with pe.Fori(1, B) as b:
                batch(b, tail=True)
            for q in range(QT):
                for half in range(2):
                    transposed(B - 1, q, half, LAST_T[q][half])
                for half in range(2):
                    output(B - 1, q, half, LAST_Y[q])

        def act_rotated():
            act, s = nc.scalar, att[1]

            def exponentials(b):
                for q in range(QT):
                    act.wait_ge(soft.sub, NT + 2 * b + q + 1)
                    act.activation(at_p[:, q, :], at_p[:, q, :], ACT.Exp).then_inc(soft.p, 1)

            def evacuations(b, banks=((6, 6), (6, 6))):
                for q in range(QT):
                    for half in range(2):
                        act.wait_ge(s.t_ps, 4 * b + 2 * q + half + 1)
                        act.activation(at_pt[:, q, half * 512:(half + 1) * 512], PS[:, banks[q][half], :], ACT.Copy).then_inc(s.t, 1)

            with act.Fori(0, B - 1) as b:
                exponentials(b)
                evacuations(b)
            exponentials(B - 1)
            evacuations(B - 1, LAST_T)

        def dve_rotated(me):
            dve, s = nc.vector, att[1]

            def rotated(b, j):
                for q in range(QT):
                    dve.wait_ge(s.q_ps, 2 * PAIRS * b + 2 * j + q + 1)
                    for c in range(2):
                        dve.tensor_tensor(at_r[:, j % 2, c, :, q * P:(q + 1) * P],
                                          PS[:, 4 + q, 0:3 * P].rearrange("p (t c) -> p t c", t=3),
                                          tables[:, c, :, q * P:(q + 1) * P], ALU.mult).then_inc(s.roped, 1)

            def added(b, q, bank_=7):
                dve.wait_ge(soft.y_ps, NT + 2 * b + q + 1)
                tile = x[:, tile_of(b, q), :]
                dve.tensor_tensor(tile, tile, PS[:, bank_:bank_ + 1, 0:D], ALU.add).then_inc(soft.x, 1)
                dve_stats(3, QT * b + q)

            def scores(b, q):
                dve_scores(s.s, me, q, b + 1, 2 * q)

            def sums(b, q):
                dve_sums(me, q, NT + 2 * b + q + 1)

            for j in range(PAIRS):
                rotated(0, j)
            with dve.Fori(1, B) as b:
                me.open(b - 1, 4)
                scores(b - 1, 0)
                rotated(b, 0)
                scores(b - 1, 1)
                rotated(b, 1)
                sums(b - 1, 0)
                rotated(b, 2)
                sums(b - 1, 1)
                for j in range(3, PAIRS):
                    rotated(b, j)
                    if j == 5:
                        added(b - 1, 0)
                added(b - 1, 1)
            me.close(B - 1)
            scores(B - 1, 0)
            scores(B - 1, 1)
            sums(B - 1, 0)
            sums(B - 1, 1)
            added(B - 1, 0, LAST_Y[0])
            added(B - 1, 1, LAST_Y[1])


        def pe_plain():
            pe, s = nc.tensor, att[2]

            def scores(b, q):
                pe.wait_ge(s.q, b + 1)
                for g in range(2):
                    for k in range(KT):
                        ins = pe.matmul(PS[:, 2 * q + g, :], fold_x[:, k, q, :],
                                        fold_n[:, at_batch(b), k, g * 512:(g + 1) * 512]
                                        .rearrange("p b c -> p (b c)"), start=(k == 0), stop=(k == KT - 1))
                ins.then_inc(s.s, 1)

            def transposed(b, q):
                pe.wait_ge(norm.pn, 2 * NT + 2 * b + q + 1)
                for j in range(PAIRS):
                    ins = pe.transpose(PS[:, 4 + j // 4, (j % 4) * P:(j % 4 + 1) * P],
                                       at_p[:, q, j * P:(j + 1) * P], ident[:])
                ins.then_inc(soft.t_ps, 1)

            def output(b, q):
                pe.wait_ge(soft.t, turns_before[2] + 2 * b + q + 1)
                pe.wait_ge(soft.x, 2 * NT + 2 * b - 1 + q)
                for j in range(PAIRS):
                    ins = pe.matmul(PS[:, 6 + q, 0:D], at_pt[:, q, j * P:(j + 1) * P],
                                    fold_f[:, at_batch(b), j, :].rearrange("p b c -> p (b c)"),
                                    start=(j == 0), stop=(j == PAIRS - 1))
                ins.then_inc(soft.y_ps, 1)

            def batch(b, last=False):
                for q in range(QT):
                    transposed(b, q)
                    if not last:
                        scores(b + 1, q)
                    output(b, q)

            for q in range(QT):
                scores(0, q)
            with pe.Fori(0, B - 1) as b:
                batch(b)
            batch(B - 1, last=True)

        def act_plain():
            act = nc.scalar

            def exponential(b, q):
                act.wait_ge(soft.sub, 2 * NT + 2 * b + q + 1)
                act.activation(at_p[:, q, :], at_p[:, q, :], ACT.Exp).then_inc(soft.p, 1)

            def batch(b, last=False):
                for q in range(QT):
                    act.wait_ge(soft.t_ps, turns_before[2] + 2 * b + q + 1)
                    act.activation(at_pt[:, q, :], bank(4, 2), ACT.Copy).then_inc(soft.t, 1)
                    if not last:
                        exponential(b + 1, q)

            for q in range(QT):
                exponential(0, q)
            with act.Fori(0, B - 1) as b:
                batch(b)
            batch(B - 1, last=True)

        def dve_plain(me):
            dve, s = nc.vector, att[2]

            def stage(b):
                dve.tensor_scalar(fold_x.rearrange("p k q c -> p k (q c)"),
                                  xT[:, :, bass.ds(QT * (b % B), QT) if not isinstance(b, int) else slice(QT * b, QT * b + QT), :]
                                  .rearrange("p k q c -> p k (q c)"), 1.0, None, ALU.mult).then_inc(s.q, 1)

            def scores(b, q):
                if not (isinstance(b, int) and b == 0):
                    dve.wait_ge(soft.t_ps, turns_before[2] + 2 * b + q - 1)
                dve_scores(s.s, me, q, 2 * b + q + 1, 2 * q)

            def added(b, q):
                dve.wait_ge(soft.y_ps, 2 * NT + 2 * b + q + 1)
                tile = x[:, tile_of(b, q), :]
                dve.tensor_tensor(tile, tile, PS[:, 6 + q:7 + q, 0:D], ALU.add).then_inc(soft.x, 1)
                dve_stats(5, QT * b + q)

            def batch(b, last=False):
                for q in range(QT):
                    dve_sums(me, q, 2 * NT + 2 * b + q + 1)
                for q in range(QT):
                    if not last:
                        scores(b + 1, q)
                        if q:
                            stage(b + 2)
                    added(b, q)

            stage(0)
            for q in range(QT):
                scores(0, q)
            stage(1)
            with dve.Fori(0, B - 1) as b:
                me.open(b, 4)
                batch(b)
            me.close(B - 1)
            batch(B - 1, last=True)

        def act_folded(n):
            act, s = nc.scalar, att[n]
            act_ln(2 * n)
            over_pairs(act, act_fold1 if n == 1 else act_fold2)
            (act_rotated if n == 1 else act_plain)()

        def dve_folded(n):
            dve, s, me = nc.vector, att[n], own["dve"]
            dve_ln(2 * n)
            dve.wait_ge(s.zero, 1 + (B if n == 1 else 0))
            for h in range(2):
                dve.tensor_copy(kv_diag[L * h:L * (h + 1), :, L * h:L * (h + 1)],
                                kvr[L * h:L * (h + 1), :].rearrange("p (b l) -> p b l", b=B)).then_inc(kv_diag_done[n], 1)
            over_pairs(dve, dve_fold1 if n == 1 else dve_fold2)
            if n == 2:
                dve_keys2(PAIRS - 1)
            if n == 1:
                dve.wait_ge(s.tab, 16)
            else:
                dve.wait_ge(ln.xT, ln_xT_before[2 * n] + NT // 2)
            (dve_rotated if n == 1 else dve_plain)(me)


        def chunk_cols(n, c):
            return FFNS[n].cols(c)

        def slot_of(c):
            return slice(c % 2, c % 2 + 1) if isinstance(c, int) else bass.ds(c % 2, 1)

        def step_of(n, c, i):
            return steps_before[n] + NT * c + i

        def chunk_of(n, c):
            return chunks_before[n] + c

        def part_experts(n, c):
            return chunk_cols(n, c) // FFNS[n].width

        def product_first(n, c):
            return FFNS[n].both and not (isinstance(c, int) and c == FFNS[n].chunks - 1)

        def over_chunks(engine, n, body):
            body(0)
            if FFNS[n].chunks > 2:
                with engine.Fori(1, FFNS[n].chunks - 1) as c:
                    body(c)
            body(FFNS[n].chunks - 1)

        def sp_first_chunk(n):
            sp, s, f = nc.sync, ffn, FFNS[n]
            up, dn = 4 * f.cols(0), len(k_tiles(f.cols(0))) * D
            sp.wait_ge(*((s.w_lo, chunks_before[n]) if n else (kvs.rot, 1)))
            sp.dma_start(w_stage[:, 0:up], d[f"up{n}"][0]).then_inc(s.w_in, 16)
            if n:
                sp.wait_ge(s.down, steps_before[n])
            sp.dma_start(w_down[:, 0, 0:dn], d[f"down{n}"][0]).then_inc(s.dn_in, 16)

        def sp_ffn(n):
            sp, s, f = nc.sync, ffn, FFNS[n]
            up, dn = 4 * f.cols(0), len(k_tiles(f.cols(0))) * D
            sp.wait_ge(s.w_lo, chunk_of(n, 1))
            sp.dma_start(w_stage[:, 0:up], d[f"up{n}"][1]).then_inc(s.w_in, 16)
            sp.wait_ge(s.down, steps_before[n] + 1)
            sp.dma_start(w_down[:, 1, 0:dn], d[f"down{n}"][1]).then_inc(s.dn_in, 16)
            if f.chunks > 2:
                with sp.Fori(2, f.chunks) as c:
                    sp.wait_ge(s.w_lo, chunk_of(n, c))
                    sp.dma_start(w_stage[:, 0:up].rearrange("p (a c) -> p a c", a=1),
                                 d[f"up{n}"][bass.ds(c, 1), :, :].rearrange("a p c -> p a c")).then_inc(s.w_in, 16)
                    sp.wait_ge(s.down, step_of(n, c - 1, 0) + 1)
                    sp.dma_start(w_down[:, slot_of(c), 0:dn],
                                 d[f"down{n}"][bass.ds(c, 1), :, :].rearrange("a p c -> p a c")).then_inc(s.dn_in, 16)

        def pe_ffn(n):
            pe, s, f = nc.tensor, ffn, FFNS[n]

            def up(c, i):
                cols = chunk_cols(n, c)
                if i == 0:
                    pe.wait_ge(s.w_lo, chunk_of(n, c) + 1)
                if not (isinstance(c, int) and c == 0 and i < 2):
                    pe.wait_ge(s.prod, step_of(n, c, i) - 1)
                at = 2 * (i % 2)
                for k in range(KT):
                    for u in range(2):
                        w = [w_split[:, slot_of(c), hl, (2 * k + u) * cols:(2 * k + u + 1) * cols]
                             .rearrange("p a c -> p (a c)") for hl in range(2)]
                        g_ps = PS[:, at + u, 0:cols]
                        pe.matmul(g_ps, xh[:, k, i, :], w[0], start=(k == 0), stop=False)
                        pe.matmul(g_ps, xh[:, k, i, :], w[1], start=False, stop=False)
                        ins = pe.matmul(g_ps, xl[:, k, i, :], w[0], start=False, stop=(k == KT - 1))
                ins.then_inc(s.gu, 1)

            def transposes(c, i):
                pe.wait_ge(s.hid, step_of(n, c, i) + 1)
                for k, rows in k_tiles(chunk_cols(n, c)):
                    ins = pe.transpose(PS[0:rows, 4 + i % 2, k * P:(k + 1) * P], m_c[:, i % 2, k * P:k * P + rows], ident[:])
                ins.then_inc(s.hidT_ps, 1)

            def down(c, i):
                pe.wait_ge(s.hidT, step_of(n, c, i) + 1)
                if i == 0:
                    pe.wait_ge(s.dn_in, 16 * chunk_of(n, c) + 16)
                tiles = k_tiles(chunk_cols(n, c))
                for k, rows in tiles:
                    ins = pe.matmul(PS[:, 6 + i % 2, 0:D], hidT[0:rows, i % 2, k, :],
                                    w_down[0:rows, slot_of(c), k * D:(k + 1) * D].rearrange("p a c -> p (a c)"),
                                    start=(k == 0), stop=(k == len(tiles) - 1))
                ins.then_inc(s.down, 1)

            def chunk(c):
                for i in range(NT):
                    up(c, i)
                    before = (c, i - 2) if i >= 2 else (c - 1, i - 2 + NT)
                    if not (isinstance(c, int) and c == 0 and i < 2):
                        if not (isinstance(c, int) and c == 0 and i < 4):
                            pe.wait_ge(s.x, step_of(n, c, i) - 3)
                        down(*before)
                    before = (c, i - 1) if i >= 1 else (c - 1, NT - 1)
                    if not (isinstance(c, int) and c == 0 and i < 1):
                        transposes(*before)

            over_chunks(pe, n, chunk)
            last = f.chunks - 1
            pe.wait_ge(s.x, steps_before[n + 1] - 3)
            down(last, NT - 2)
            transposes(last, NT - 1)
            pe.wait_ge(s.x, steps_before[n + 1] - 2)
            down(last, NT - 1)

        def act_split(n, c):
            cols = 4 * FFNS[n].cols(0)
            hold(nc.scalar, ffn.w_in, 16 * chunk_of(n, c) + 16)
            nc.scalar.activation(w_split[:, slot_of(c), 0, 0:cols], w_stage[:, 0:cols].rearrange("p (a c) -> p a c", a=1),
                                 ACT.Copy, scale=SPLIT).then_inc(ffn.w_hi, 1)

        def dve_split(n, c):
            cols = 4 * FFNS[n].cols(0)
            nc.vector.wait_ge(ffn.w_hi, chunk_of(n, c) + 1)
            nc.vector.scalar_tensor_tensor(w_split[:, slot_of(c), 1, 0:cols],
                                           w_stage[:, 0:cols].rearrange("p (a c) -> p a c", a=1), SPLIT,
                                           w_split[:, slot_of(c), 0, 0:cols], ALU.mult, ALU.subtract).then_inc(ffn.w_lo, 1)

        def act_ffn(n):
            act, s, f = nc.scalar, ffn, FFNS[n]

            def evacuate(c, i):
                act.wait_ge(s.hidT_ps, step_of(n, c, i) + 1)
                tiles = k_tiles(chunk_cols(n, c))
                full = [k for k, rows in tiles if rows == P]
                if full:
                    ins = act.activation(hidT[:, i % 2, 0:len(full), :],
                                         PS[:, 4 + i % 2, 0:len(full) * P].rearrange("p (k c) -> p k c", k=len(full)), ACT.Copy)
                for k, rows in tiles[len(full):]:
                    ins = act.activation(hidT[0:rows, i % 2, k, :], PS[0:rows, 4 + i % 2, k * P:(k + 1) * P], ACT.Copy)
                ins.then_inc(s.hidT, 1)

            def chunk(c):
                cols = chunk_cols(n, c)
                for i in range(NT):
                    if i == 3 and not (isinstance(c, int) and c == f.chunks - 1):
                        act_split(n, c + 1)
                    act.wait_ge(s.gu, step_of(n, c, i) + 1)
                    t = m_t[:, i % 2, 0:cols]
                    if product_first(n, c):
                        act.activation(t, PS[:, 2 * (i % 2), 0:cols], ACT.Copy, scale=UNSPLIT).then_inc(s.g, 1)
                        act.wait_ge(s.act, NT * c + i + 1)
                        act.activation(t, m_a[:, i % 2, 0:cols], ACT.Tanh, scale=0.5 * UNSPLIT).then_inc(s.t, 1)
                    else:
                        act.activation(t, PS[:, 2 * (i % 2), 0:cols], ACT.Tanh, scale=0.5 * UNSPLIT).then_inc(s.t, 1)
                    if not (isinstance(c, int) and c == 0 and i == 0):
                        evacuate(*((c, i - 1) if i else (c - 1, NT - 1)))

            over_chunks(act, n, chunk)
            evacuate(f.chunks - 1, NT - 1)

        def dve_ffn(n):
            dve, s, f, me = nc.vector, ffn, FFNS[n], own["dve"]

            def add(c, i):
                dve.wait_ge(s.down, step_of(n, c, i) + 1)
                dve.tensor_tensor(x[:, i, :], x[:, i, :], PS[:, 6 + i % 2, 0:D], ALU.add).then_inc(s.x, 1)
                if isinstance(c, int) and c == f.chunks - 1 and n < 3:
                    dve_stats(2 * n + 2, i)

            def chunk(c):
                cols = chunk_cols(n, c)
                loop = not isinstance(c, int)
                if loop:
                    me.open(c - 1, 0 if product_first(n, c) else NT)
                for i in range(NT):
                    if i == 3 and not (isinstance(c, int) and c == f.chunks - 1):
                        dve_split(n, c + 1)
                    t, a, b = (m[:, i % 2, 0:cols] for m in (m_t, m_a, m_b))
                    g_ps, u_ps = (PS[:, 2 * (i % 2) + u, 0:cols] for u in range(2))
                    if product_first(n, c):
                        dve.wait_ge(s.g, NT * c + i + 1)
                        dve.tensor_tensor(a, t, u_ps, ALU.mult).then_inc(s.act, 1)
                        if not (isinstance(c, int) and c == 0 and i < 2):
                            add(*((c, i - 2) if i >= 2 else (c - 1, i - 2 + NT)))
                        dve.wait_ge(s.t, step_of(n, c, i) + 1)
                        dve.scalar_tensor_tensor(b, t, 1.0, a, ALU.add, ALU.mult).then_inc(s.prod, 1)
                    else:
                        dve.wait_ge(s.t, step_of(n, c, i) + 1)
                        me.link(dve, dve.scalar_tensor_tensor(a, t, 1.0, g_ps, ALU.add, ALU.mult))
                        if not (isinstance(c, int) and c == 0 and i < 2):
                            dve.wait_ge(s.hid, step_of(n, c, i) - 1)
                        dve.tensor_tensor(b, a, u_ps, ALU.mult).then_inc(s.prod, 1)
                        if not (isinstance(c, int) and c == 0 and i < 2):
                            add(*((c, i - 2) if i >= 2 else (c - 1, i - 2 + NT)))
                if loop:
                    me.close(f.chunks - 2)

            over_chunks(dve, n, chunk)
            add(f.chunks - 1, NT - 2)
            add(f.chunks - 1, NT - 1)

        def pool_ffn(n):
            pool, s, f = nc.gpsimd, ffn, FFNS[n]

            def chunk(c):
                e = part_experts(n, c)
                at = slice(c, c + 1) if isinstance(c, int) else bass.ds(c, 1)
                for i in range(NT):
                    if not (isinstance(c, int) and c == 0 and i < 2):
                        pool.wait_ge(s.hidT_ps, step_of(n, c, i) - 1)
                    hold(pool, s.prod, step_of(n, c, i) + 1)
                    pool.tensor_tensor(m_c[:, i % 2, 0:e * f.width].rearrange("p (e w) -> p e w", e=e),
                                       m_b[:, i % 2, 0:e * f.width].rearrange("p (e w) -> p e w", e=e),
                                       over(gates[:, at, i, 0:e].rearrange("p a e -> p (a e)"), 2, f.width),
                                       ALU.mult).then_inc(s.hid, 1)

            over_chunks(pool, n, chunk)


        def act_parts(src_ready, before, done, scales, f32_scales=None, f32_done=None):
            for j in range(NT // 2):
                nc.scalar.wait_ge(src_ready, before + 2 * j + 2)
                for k in range(KT):
                    ps = pair_ps(j)[:, k, :, :]
                    if f32_scales is not None:
                        nc.scalar.activation(xT[:, k, 2 * j:2 * j + 2, :], ps, ACT.Copy,
                                             scale=f32_scales(k)).then_inc(f32_done, 1)
                    nc.scalar.activation(xh[:, k, 2 * j:2 * j + 2, :], ps, ACT.Copy, scale=scales(k)).then_inc(done, 1)

        def dve_parts(high_done, scales):
            for j in range(NT // 2):
                nc.vector.wait_ge(high_done, KT * (j + 1))
                for k in range(KT):
                    ins = nc.vector.scalar_tensor_tensor(xl[:, k, 2 * j:2 * j + 2, :], pair_ps(j)[:, k, :, :], scales(k),
                                                         xh[:, k, 2 * j:2 * j + 2, :], ALU.mult, ALU.subtract)
            return ins

        def plain_scale(k):
            return SPLIT

        def pe_logits(s, w, cols, ready, count):
            pe = nc.tensor
            pe.wait_ge(s.w, 16)
            pe.wait_ge(ready, count)
            for i in range(NT):
                for k in range(KT):
                    ins = pe.matmul(PS[:, 4 + i // 4, (i % 4) * cols:(i % 4 + 1) * cols], xT[:, k, i, :], w[:, k, :],
                                    start=(k == 0), stop=(k == KT - 1))
            ins.then_inc(s.logit, 1)

        def logits_ps(cols):
            return PS[:, 4:6, 0:4 * cols].rearrange("p b (t c) -> p b t c", t=4)

        def tiles_of(ap):
            return ap.rearrange("p (b t) c -> p b t c", b=2)

        def top_experts(me, values, k_top, width, ranked, rest):
            dve = nc.vector
            for i in range(NT):
                ins = dve.max(ranked[:, i, :], values[:, i, 0:width])
            me.link(dve, ins)
            if k_top < 8:
                me.link(dve, dve.tensor_copy(ranked[:, :, k_top:8], values[:, :, width:width + 8 - k_top]))
            for i in range(NT):
                ins = dve.match_replace(rest[:, i, :], ranked[:, i, :], values[:, i, :], 0.0)
            me.link(dve, ins)
            me.link(dve, dve.tensor_tensor(rest[:, :, 0:width], values[:, :, 0:width], rest[:, :, 0:width], ALU.subtract))

        def shape3(ap, n, c):
            return ap[:, 0:n * c].rearrange("p (n c) -> p n c", n=n)

        p0_wv, p0_wo = (ffn_w[:, a:a + 512].rearrange("p (k c) -> p k c", k=KT) for a in (0, 512))
        p0_fold = ffn_w[:, 1024:1536].rearrange("p (k c) -> p k c", k=KT)
        p0_bias = ffn_w[:, 1536:1792]
        p0_bv = ffn_v[:, 0:KT * P].rearrange("p (k c) -> p k c", k=KT)
        p0_router, p0_b, p0_n1, p0_n2 = ffn_v[:, 256:512], ffn_v[:, 512:513], ffn_v[:, 513:515], ffn_v[:, 515:517]
        p0_n2s = ffn_v[:, 520:522]
        p0_score, p0_route, p0_ssq = ffn_v[:, 528:536], ffn_v[:, 536:544], ffn_v[:, 544:552]
        p0_junk = ffn_v[:, 1024:1280]
        z = shape3(ffn_s, NT, D)
        zT = ffn_s[:, 2048:4096].rearrange("p (k t c) -> p k t c", k=KT, t=NT)

        def sp_pre0():
            nc.sync.dma_start(ffn_w[:, 0:1024], d["pre0"]).then_inc(pre[0].w, 16)
            nc.sync.dma_start(ffn_v[:, 0:517], d["vec0"]).then_inc(pre[0].w, 16)

        def pe_pre0():
            pe, s = nc.tensor, pre[0]
            x_ready(pe, 1)
            pe.wait_ge(s.w, 32)
            for m in range(KT):
                for k in range(KT):
                    pe.matmul(PS[:, 4, m * D:(m + 1) * D], p0_wv[:, k, m * P:(m + 1) * P], p0_wo[:, k, :],
                              start=(k == 0), stop=(k == KT - 1))
            for k in range(KT):
                ins = pe.matmul(PS[:, 5, 0:D], p0_bv[:, k, :], p0_wo[:, k, :], start=(k == 0), stop=(k == KT - 1))
            ins.then_inc(s.fold_ps, 1)
            pe_transpose_tiles(z, s.z, 0, s.zT_ps)
            pe.wait_ge(s.fold, 2)
            for i in range(NT):
                if i % 2 == 0:
                    pe.wait_ge(s.zT, i + 2)
                for k in range(KT):
                    pe.matmul(PS[:, 4 + i // 2, (i % 2) * D:(i % 2 + 1) * D], zT[:, k, i, :], p0_fold[:, k, :],
                              start=(k == 0), stop=False)
                ins = pe.matmul(PS[:, 4 + i // 2, (i % 2) * D:(i % 2 + 1) * D], ident[:], p0_bias, start=False, stop=True)
                if i % 2:
                    ins.then_inc(s.y_ps, 1)
            pe_transpose_tiles(z, s.z2, 0, s.z2T_ps)
            pe.wait_ge(s.gates, 1)

        def act_pre0():
            act, s = nc.scalar, pre[0]
            x_ready(act, 1)
            act.wait_ge(s.fold_ps, 1)
            act.activation(p0_fold, PS[:, 4, :].rearrange("p (k c) -> p k c", k=KT), ACT.Copy).then_inc(s.fold, 1)
            act.activation(p0_bias, PS[:, 5, 0:D], ACT.Copy).then_inc(s.fold, 1)
            for j in range(NT // 2):
                act.wait_ge(s.zT_ps, 2 * j + 2)
                for k in range(KT):
                    act.activation(zT[:, k, 2 * j:2 * j + 2, :], pair_ps(j)[:, k, :, :], ACT.Copy,
                                   scale=p0_n1[:, k:k + 1]).then_inc(s.zT, 1)
            act_parts(s.z2T_ps, 0, s.h, lambda k: p0_n2s[:, k:k + 1])

        def pool_pow(wait, count, out_, in_, done):
            nc.gpsimd.wait_ge(wait, count)
            nc.gpsimd.tensor_tensor(out_, in_, half_neg[:], ALU.pow).then_inc(done, 1)

        def pool_pre0():
            x_ready(nc.gpsimd, 1)
            pool_ln(1)
            pool_pow(pre[0].ms, 1, rms_r[:], rms_e[:], pre[0].r)
            pool_pow(pre[0].ssq, 1, rms_r[:], rms_e[:], pre[0].rr)
            nc.gpsimd.wait_ge(pre[0].gates, 1)

        def dve_norm_ms(me, ready, r_done):
            dve = nc.vector
            me.link(dve, dve.tensor_tensor(rms_e[:], rstd[:], rstd[:], ALU.mult))
            me.link(dve, dve.tensor_tensor(rms_e[:], rms_e[:], meanvar[:, :, 1], ALU.mult))
            dve.tensor_scalar(rms_e[:], rms_e[:], RMS_EPS, None, ALU.add).then_inc(ready, 1)
            dve.wait_ge(r_done, 1)

        def dve_pre0():
            dve, s, me = nc.vector, pre[0], own["dve"]
            dve_ln(1)
            dve_norm_ms(me, s.ms, s.r)
            for i in range(NT):
                dve.tensor_scalar(z[:, i, :], xn[:, i, :], rms_r[:, i:i + 1], None, ALU.mult).then_inc(s.z, 1)
            dve.wait_ge(s.w, 32)
            for i in range(NT):
                me.link(dve, dve.scalar_tensor_tensor(p0_junk, xn[:, i, :], 1.0, p0_router, ALU.mult, ALU.mult,
                                                      accum_out=p0_score[:, i:i + 1]))
            me.link(dve, dve.tensor_scalar(p0_route, p0_score, p0_b, 0.0, ALU.add, ALU.is_gt))
            me.link(dve, dve.tensor_scalar(p0_n2s, p0_n2, SPLIT, None, ALU.mult))
            me.link(dve, dve.tensor_scalar(gates[:, 0, :, 0], p0_route, 0.5 * UNSPLIT * UNSPLIT, None, ALU.mult))
            for c, e in ((0, 1), (1, 0), (1, 1)):
                ins = dve.tensor_copy(gates[:, c, :, e], gates[:, 0, :, 0])
            me.link(dve, ins)
            me.link(dve, dve.tensor_tensor(x[:], x[:], xn[:], ALU.add))
            dve.wait_ge(s.fold, 2)
            for i in range(NT):
                if i % 2 == 0:
                    dve.wait_ge(s.y_ps, i // 2 + 1)
                a_ps = PS[:, 4 + i // 2, (i % 2) * D:(i % 2 + 1) * D]
                ins = dve.tensor_tensor(xn[:, i, :], xn[:, i, :], a_ps, ALU.add)
                ins.then_inc(me.sem, 1)
                me.done += 1
                dve.scalar_tensor_tensor(x[:, i, :], a_ps, p0_route[:, i:i + 1], x[:, i, :], ALU.mult, ALU.add)
                dve.wait_ge(me.sem, me.done)
                me.link(dve, dve.scalar_tensor_tensor(p0_junk, xn[:, i, :], 1.0, xn[:, i, :], ALU.mult, ALU.mult,
                                                      accum_out=p0_ssq[:, i:i + 1]))
            dve.tensor_scalar(rms_e[:], p0_ssq, 1.0 / D, RMS_EPS, ALU.mult, ALU.add).then_inc(s.ssq, 1)
            dve.wait_ge(s.rr, 1)
            for i in range(NT):
                dve.tensor_scalar(z[:, i, :], xn[:, i, :], rms_r[:, i:i + 1], None, ALU.mult).then_inc(s.z2, 1)
            dve_parts(s.h, lambda k: p0_n2s[:, k:k + 1]).then_inc(s.gates, 1)

        E1 = 64
        r1_w = ffn_w[:, 0:KT * (E1 + 1)].rearrange("p (k c) -> p k c", k=KT)
        lg1 = shape3(ffn_s, NT, E1 + 1)
        pr1 = shape3(ffn_s[:, 1024:], NT, E1)
        rest1 = shape3(ffn_s[:, 2048:], NT, E1)
        ranked = shape3(ffn_s[:, 3072:], NT, 8)
        row1, row2, row3 = (ffn_s[:, 3200 + 8 * a:3208 + 8 * a] for a in range(3))
        sig = ffn_s[:, 3232:3240]

        def sp_router(n, cols):
            x_ready(nc.sync, 2 * n + (1 if n == 1 else 0))
            nc.sync.dma_start(ffn_w[:, 0:cols], d[f"router{n}"]).then_inc(pre[n].w, 16)

        def pe_pre1(n, w, cols):
            x_ready(nc.tensor, 2 * n + 1)
            pe_transpose_tiles(xn, ln.xn, (2 * n + 1) * NT, ln.xT_ps)
            pe_logits(pre[n], w, cols, ln.xT, ln_xT_before[2 * n + 1] + NT)
            nc.tensor.wait_ge(pre[n].gates, 1)

        def act_pre1(n):
            act, s = nc.scalar, pre[n]
            x_ready(act, 2 * n + 1)
            if n == 1:
                act_split(n, 0)
            act_parts(ln.xT_ps, ln_T_before[2 * n + 1], s.h, plain_scale, lambda k: 1.0, ln.xT)
            if n == 1:
                act.wait_ge(s.e, 1)
                act.activation(pr1, pr1, ACT.Exp).then_inc(s.t, 1)
                act.activation(sig, lg1[:, :, E1], ACT.Tanh, scale=0.5).then_inc(s.t, 1)

        def pool_pre1(n):
            x_ready(nc.gpsimd, 2 * n + 1)
            pool_ln(2 * n + 1)
            nc.gpsimd.wait_ge(pre[n].lg, 2)

        def dve_softmax_over(me, logits, probs, e, s, width):
            dve = nc.vector
            me.link(dve, dve.tensor_reduce(row1, logits, AX.X, ALU.max))
            dve.tensor_tensor(probs, logits, over(row1, 2, width), ALU.subtract).then_inc(s.e, 1)
            dve.wait_ge(s.t, 2)
            me.link(dve, dve.tensor_reduce(row2, probs, AX.X, ALU.add))
            me.link(dve, dve.reciprocal(row3, row2))
            me.link(dve, dve.tensor_tensor(probs, probs, over(row3, 2, width), ALU.mult))

        def dve_pre1():
            dve, s, me = nc.vector, pre[1], own["dve"]
            dve_ln(3)
            dve_split(1, 0)
            dve_parts(s.h, plain_scale).then_inc(s.gates, 1)
            dve.wait_ge(s.logit, 1)
            me.link(dve, dve.tensor_copy(tiles_of(lg1), logits_ps(E1 + 1)))
            dve_softmax_over(me, lg1[:, :, 0:E1], pr1, E1, s, E1)
            top_experts(me, pr1, 8, E1, ranked, rest1)
            me.link(dve, dve.tensor_reduce(row1, rest1, AX.X, ALU.add))
            me.link(dve, dve.reciprocal(row2, row1))
            me.link(dve, dve.tensor_scalar(row3, row2, 0.5 * UNSPLIT * UNSPLIT, None, ALU.mult))
            me.link(dve, dve.tensor_tensor(rest1, rest1, over(row3, 2, E1), ALU.mult))
            dve.tensor_copy(gates[:, 0:8, :, :].rearrange("p c t e -> p t c e"),
                            rest1.rearrange("p t (c e) -> p t c e", c=8)).then_inc(s.lg, 1)
            dve.tensor_scalar(gates[:, 8, :, 0], sig, 1.0, 0.25 * UNSPLIT * UNSPLIT, ALU.add, ALU.mult).then_inc(s.lg, 1)

        E3 = 16
        r3_w = ffn_w[:, 0:KT * E3].rearrange("p (k c) -> p k c", k=KT)
        r3_b = ffn_w[:, KT * E3:KT * E3 + E3]
        sc3 = shape3(ffn_s, NT, E3 + 4)
        rest3 = shape3(ffn_s[:, 2048:], NT, E3 + 4)
        lg3 = shape3(ffn_s[:, 1024:], NT, E3)

        def dve_pre3():
            dve, s, me = nc.vector, pre[3], own["dve"]
            dve_ln(7)
            dve_parts(s.h, plain_scale).then_inc(s.gates, 1)
            dve.wait_ge(s.logit, 1)
            me.link(dve, dve.memset(sc3[:, :, E3:E3 + 4], -1e30))
            dve.tensor_copy(tiles_of(lg3), logits_ps(E3)).then_inc(s.lg, 1)
            dve.wait_ge(s.t, 1)
            me.link(dve, dve.tensor_scalar(lg3, lg3, 0.5, 0.5, ALU.mult, ALU.add))
            me.link(dve, dve.tensor_tensor(sc3[:, :, 0:E3], lg3, over(r3_b, 1, NT), ALU.add))
            top_experts(me, sc3, 4, E3, ranked, rest3)
            me.link(dve, dve.tensor_reduce(row1, rest3[:, :, 0:E3], AX.X, ALU.add))
            me.link(dve, dve.reciprocal(row2, row1))
            me.link(dve, dve.tensor_scalar(row3, row2, 0.5 * UNSPLIT, None, ALU.mult))
            me.link(dve, dve.tensor_tensor(rest3[:, :, 0:E3], rest3[:, :, 0:E3], over(row3, 2, E3), ALU.mult))
            me.link(dve, dve.tensor_copy(gates[:, 0:8, :, 0:2].rearrange("p c t e -> p t c e"),
                                         rest3[:, :, 0:E3].rearrange("p t (c e) -> p t c e", c=8)))
            dve.memset(gates[:, 8, :, 0], 0.5 * UNSPLIT * UNSPLIT).then_inc(s.lg, 1)

        def act_pre3():
            act, s = nc.scalar, pre[3]
            act_pre1(3)
            act.wait_ge(s.lg, 1)
            act.activation(lg3, lg3, ACT.Tanh, scale=0.5).then_inc(s.t, 1)

        E2 = 8
        qkv_w = ffn_s[:, 2048:3584].rearrange("p (k c) -> p k c", k=KT)
        p2_wo = ffn_w[:, 0:512].rearrange("p (k c) -> p k c", k=G)
        r2_w = ffn_w[:, 512:512 + KT * (E2 + 1)].rearrange("p (k c) -> p k c", k=KT)
        p2_bias = ffn_v[:, 0:3 * D]
        p2_cos, p2_sin = (ffn_v[:, a:a + 64].rearrange("p (q a c) -> p q a c", q=QT, a=2) for a in (768, 832))
        p2_n1, p2_n2, p2_n2s = ffn_v[:, 896:898], ffn_v[:, 898:900], ffn_v[:, 904:906]
        p2_ssq, p2_negmax = ffn_v[:, 912:920], ffn_v[:, 920:928].rearrange("p (r c) -> p r c", r=4)
        p2_junk = ffn_v[:, 1024:1280]
        at = 25088
        sa_v, at = take(at, [NT, D])
        sa_kT, at = take(at, [B, G, 2, S])
        sa_qT, at = take(at, [B, QT, G, P])
        sa_r, at = take(at, [2, 512])
        sa_b, at = take(at, [2, 512])
        sa_t, _ = take(at, [2, 2, 512])
        sa_k = ffn_s[:, 5120:6144].rearrange("p (g a c) -> p g a c", g=G, a=2)
        sa_q = ffn_s[:, 4608:5120].rearrange("p (q g c) -> p q g c", q=QT, g=G)
        sa_p, at = take(at, [4, 512])
        sa_pt = m_b
        sa_vm = m_c.rearrange("p k (j a e c) -> p k j a e c", j=PAIRS, a=2, e=2)
        sa_one = m_t[:, 0, 0:D]
        sa_oneT = m_t[:, 0, D:2 * D]
        sa_oT = m_t[:, 1, :].rearrange("p (q g c) -> p q g c", q=QT, g=G)
        SA_AHEAD = 4
        SA_STEPS = QT * PAIRS
        lg2 = shape3(ffn_s[:, 2048:], NT, E2 + 1)
        pr2 = shape3(ffn_s[:, 2560:], NT, E2 + 6)
        rest2 = shape3(ffn_s[:, 4096:], NT, E2 + 6)

        def sp_pre2():
            sp = nc.sync
            sp.dma_start(qkv_w.rearrange("p k c -> p (k c)"), d["qkv2"]).then_inc(pre[2].w, 16)
            sp.dma_start(ffn_w[:, 0:512 + KT * (E2 + 1)], d["router2"]).then_inc(pre[2].w, 16)
            sp.dma_start(ffn_v[:, 0:900], d["vec2"]).then_inc(pre[2].w, 16)

        def sa_keys(t):
            return (t // PAIRS + 1) * P

        def score_bank(t):
            return (0, 1, 4, 5)[t % SA_AHEAD]

        def pe_qkv():
            pe, s = nc.tensor, pre[2]

            def turned(i):
                pe.wait_ge(s.qr, i + 1)
                if i >= 2:
                    pe.wait_ge(s.qT, i - 1)
                for k in range(4):
                    ins = pe.transpose(PS[:, 4 + i % 2, k * P:(k + 1) * P], sa_r[:, i % 2, k * P:(k + 1) * P], ident[:])
                ins.then_inc(s.qrT_ps, 1)

            for i in range(NT):
                if i >= 2:
                    pe.wait_ge(s.biased, i - 1)
                for k in range(KT):
                    pe.matmul(PS[:, i % 2, :], xT[:, k, i, :], qkv_w[:, k, 0:512], start=(k == 0), stop=(k == KT - 1))
                for k in range(KT):
                    ins = pe.matmul(PS[:, 2 + i % 2, 0:D], xT[:, k, i, :], qkv_w[:, k, 512:768], start=(k == 0),
                                    stop=(k == KT - 1))
                ins.then_inc(s.qkv, 1)
                if i:
                    turned(i - 1)
            turned(NT - 1)
            pe.wait_ge(s.biased, NT)
            pe.wait_ge(s.qT, NT)

        def act_qkv():
            act, s = nc.scalar, pre[2]
            for i in range(NT):
                b, q = divmod(i, QT)
                act.wait_ge(s.qrT_ps, i + 1)
                act.activation(sa_qT[:, b, q, :, :], PS[:, 4 + i % 2, 0:D].rearrange("p (g c) -> p g c", g=G), ACT.Copy)
                for a in range(2):
                    ins = act.activation(sa_kT[:, b, :, a, q * P:(q + 1) * P],
                                         PS[:, 4 + i % 2, D:2 * D].rearrange("p (g c) -> p g c", g=G), ACT.Copy,
                                         scale=parity[:, a:a + 1])
                ins.then_inc(s.qT, 1)

        def dve_qkv(me):
            dve, s = nc.vector, pre[2]
            half = HD // 2

            def biased(i):
                dve.wait_ge(s.qkv, i + 1)
                dve.tensor_tensor(sa_v[:, i, :], PS[:, 2 + i % 2, 0:D], p2_bias[:, 2 * D:3 * D], ALU.add)
                dve.tensor_tensor(sa_b[:, i % 2, :], PS[:, i % 2, :], p2_bias[:, 0:2 * D], ALU.add).then_inc(s.biased, 1)

            for i in range(NT):
                biased(i)
                dve.wait_ge(s.biased, i + 1)
                by_head = sa_b[:, i % 2, :].rearrange("p (a h c) -> p a h c", a=2, h=H)
                cos_t, sin_t = (sa_t[:, i % 2, c, :].rearrange("p (a h c) -> p a h c", a=2, h=H) for c in range(2))
                dve.tensor_tensor(cos_t, by_head, over(p2_cos[:, i % QT, :, :], 2, H), ALU.mult)
                for lo, hi in ((0, half), (half, 0)):
                    ins = dve.tensor_tensor(sin_t[:, :, :, lo:lo + half], by_head[:, :, :, hi:hi + half],
                                            over(p2_sin[:, i % QT, :, lo:lo + half], 2, H), ALU.mult)
                me.link(dve, ins)
                if i >= 2:
                    dve.wait_ge(s.qrT_ps, i - 1)
                dve.tensor_tensor(sa_r[:, i % 2, :], sa_t[:, i % 2, 0, :], sa_t[:, i % 2, 1, :], ALU.add).then_inc(s.qr, 1)

        def pe_scores(b, t):
            pe, s = nc.tensor, pre[2]
            q, j, keys = t // PAIRS, t % PAIRS, sa_keys(t)
            if j == 0 or t == 4:
                pe.wait_ge(s.stage, 4 * b + {0: 2, 4: 3, 8: 4}[t])
            rows = slice(32 * (j % 4), 32 * (j % 4) + 32)
            both = PS[:, score_bank(t), 0:2 * keys].rearrange("p (a c) -> p a c", a=2)
            pe.matmul(both, sa_q[rows, q, j // 4, :], sa_k[rows, j // 4, :, 0:keys], start=True, stop=False)
            pe.matmul(both[:, :, keys - P:keys], ident_b[:], mask_self.rearrange("p (a c) -> p a c", a=2),
                      start=False, stop=True).then_inc(s.s, 1)

        def pe_self(b):
            pe, s = nc.tensor, pre[2]

            def sums_transposed(q):
                pe.wait_ge(s.one, 2 * b + q + 1)
                pe.wait_ge(s.x2, 2 * b + q + 1)
                for g in range(G):
                    ins = pe.transpose(PS[:, 7, g * P:(g + 1) * P], sa_one[:, g * P:(g + 1) * P], ident[:])
                ins.then_inc(s.oneT_ps, 1)

            def project(q):
                pe.wait_ge(s.oneT, 2 * b + q + 1)
                pe.wait_ge(s.o, 2 * b + q + 1)
                for g in range(G):
                    ins = pe.matmul(PS[:, 7, D:2 * D], sa_oT[:, q, g, :], p2_wo[:, g, :], start=(g == 0), stop=(g == G - 1))
                ins.then_inc(s.y_ps, 1)

            for t in range(SA_STEPS):
                q, j, keys = t // PAIRS, t % PAIRS, sa_keys(t)
                pe.wait_ge(s.p, SA_STEPS * b + t + 1)
                for a in range(2):
                    for k in range(q + 1):
                        ins = pe.transpose(PS[:, 2 + t % 2, (a * (q + 1) + k) * P:(a * (q + 1) + k + 1) * P],
                                           sa_p[:, t % SA_AHEAD, a * keys + k * P:a * keys + (k + 1) * P], ident[:])
                ins.then_inc(s.pt_ps, 1)
                turn, ahead = divmod(t + SA_AHEAD, SA_STEPS)
                pe_scores(b + turn, ahead)
                if j == PAIRS - 1:
                    sums_transposed(q)
                pe.wait_ge(s.pt, SA_STEPS * b + t + 1)
                if t in (0, 4, 8):
                    pe.wait_ge(s.v, 3 * b + t // 4 + 1)
                if t == PAIRS:
                    pe.wait_ge(s.o, 2 * b + 1)
                out_ps = PS[32 * (j % 4):32 * (j % 4) + 32, 6, (j // 4) * P:(j // 4 + 1) * P]
                for a in range(2):
                    for k in range(q + 1):
                        ins = pe.matmul(out_ps, sa_vm[:, k, j, a, :, :].rearrange("p e c -> p (e c)"),
                                        sa_pt[:, t % 2, (a * (q + 1) + k) * P:(a * (q + 1) + k + 1) * P],
                                        start=(a == 0 and k == 0), stop=(a == 1 and k == q))
                if j == PAIRS - 1:
                    ins.then_inc(s.o_ps, 1)
                if t == PAIRS + 1:
                    project(0)
            project(1)

        def pool_stage(b):
            pool, s = nc.gpsimd, pre[2]
            first = isinstance(b, int)
            at = slice(0, 1) if first else bass.ds(b % B, 1)

            def operand(scores_made, to, source):
                if not first:
                    hold(pool, s.s, SA_STEPS * (b - 1) + scores_made)
                pool.tensor_copy(to.rearrange("p g c -> p (g c)"),
                                 source.rearrange("p b g c -> p (b g c)")).then_inc(s.stage, 1)

            def values(k, pairs):
                tile = slice(k, k + 1) if first else bass.ds(QT * (b % B) + k, 1)
                for a in range(2):
                    source = sa_v[:, tile, :].rearrange("p b (j a c) -> p (b j) a c", a=2, c=HD)[:, pairs, a, :]
                    ins = pool.tensor_copy(sa_vm[:, k, pairs, a, a, :], source)
                return ins

            operand(8, sa_q[:, 0, :, :], sa_qT[:, at, 0, :, :])
            operand(12, sa_k[:, 0, :, :], sa_kT[:, at, 0, :, :])
            operand(16, sa_k[:, 1, :, :], sa_kT[:, at, 1, :, :])
            operand(16, sa_q[:, 1, :, :], sa_qT[:, at, 1, :, :])
            if not first:
                hold(pool, s.pt_ps, SA_STEPS * (b - 1) + PAIRS + PAIRS // 2 + 1)
            values(0, slice(0, PAIRS // 2)).then_inc(s.v, 1)
            if not first:
                hold(pool, s.o_ps, QT * b)
            values(0, slice(PAIRS // 2, PAIRS)).then_inc(s.v, 1)
            values(1, slice(0, PAIRS)).then_inc(s.v, 1)

        def act_self(b):
            act, s = nc.scalar, pre[2]
            def sums_evacuated(q):
                act.wait_ge(s.oneT_ps, 2 * b + q + 1)
                act.activation(sa_oneT, PS[:, 7, 0:D], ACT.Copy).then_inc(s.oneT, 1)

            for t in range(SA_STEPS):
                q, j, keys = t // PAIRS, t % PAIRS, sa_keys(t)
                act.wait_ge(s.mx, SA_STEPS * b + t + 1)
                for a in range(2):
                    ins = act.activation(sa_p[:, t % SA_AHEAD, a * keys:(a + 1) * keys],
                                         PS[:, score_bank(t), a * keys:(a + 1) * keys], ACT.Exp,
                                         bias=p2_negmax[:, t % SA_AHEAD, a:a + 1],
                                         accum_out=small[:, q, 1, 2 * j + a:2 * j + a + 1])
                ins.then_inc(s.p, 1)
                if t == PAIRS - 1:
                    sums_evacuated(0)
            sums_evacuated(1)

        def dve_maxima(b, t):
            dve, s = nc.vector, pre[2]
            keys = sa_keys(t)
            dve.wait_ge(s.s, SA_STEPS * b + t + 1)
            dve.tensor_reduce(p2_negmax[:, t % SA_AHEAD, :],
                              PS[:, score_bank(t), 0:2 * keys].rearrange("p (a c) -> p a c", a=2), AX.X,
                              ALU.max, negate=True).then_inc(s.mx, 1)

        def dve_self(b, me):
            dve, s = nc.vector, pre[2]

            def reciprocals(q):
                dve.wait_ge(s.p, SA_STEPS * b + PAIRS * (q + 1))
                me.link(dve, dve.reciprocal(small[:, q, 2, :], small[:, q, 1, :]))
                dve.tensor_copy(sa_one.rearrange("p (h c) -> p h c", h=H), over(small[:, q, 2, :], 2, HD)).then_inc(s.one, 1)

            def normalised(q):
                dve.wait_ge(s.o_ps, 2 * b + q + 1)
                dve.wait_ge(s.oneT, 2 * b + q + 1)
                dve.tensor_tensor(sa_oT[:, q, :, :].rearrange("p g c -> p (g c)"), PS[:, 6, 0:D], sa_oneT,
                                  ALU.mult).then_inc(s.o, 1)

            def added(q):
                dve.wait_ge(s.y_ps, 2 * b + q + 1)
                xn_t, x_t = (a[:, bass.ds(2 * b + q, 1), :] for a in (xn, x))
                me.link(dve, dve.tensor_tensor(xn_t, xn_t, PS[:, 7:8, D:2 * D], ALU.add))
                dve.tensor_tensor(x_t, x_t, xn_t, ALU.add).then_inc(s.x2, 1)

            for t in range(SA_STEPS):
                cols = 2 * sa_keys(t)
                if t % PAIRS == PAIRS - 1:
                    reciprocals(t // PAIRS)
                dve.wait_ge(s.pt_ps, SA_STEPS * b + t + 1)
                dve.tensor_copy(sa_pt[:, t % 2, 0:cols], PS[:, 2 + t % 2, 0:cols]).then_inc(s.pt, 1)
                if t == PAIRS:
                    normalised(0)
                turn, ahead = divmod(t + SA_AHEAD, SA_STEPS)
                dve_maxima(b + turn, ahead)
                if t == PAIRS + 4:
                    added(0)
            normalised(1)
            added(1)

        def pe_pre2():
            pe, s = nc.tensor, pre[2]
            x_ready(pe, 5)
            pe_transpose_tiles(z, s.z, 0, s.zT_ps)
            pe.wait_ge(s.w, 48)
            pe.wait_ge(s.hT, NT)
            pe_qkv()
            for t in range(SA_AHEAD):
                pe_scores(0, t)
            with pe.Fori(0, B) as b:
                pe_self(b)
            pe_transpose_tiles(z, s.z2, 0, s.z2T_ps)
            pe_logits(s, r2_w, E2 + 1, s.f, NT)
            pe.wait_ge(s.gates, 1)

        def act_pre2():
            act, s = nc.scalar, pre[2]
            x_ready(act, 5)
            act.wait_ge(s.w, 48)
            for j in range(NT // 2):
                act.wait_ge(s.zT_ps, 2 * j + 2)
                for k in range(KT):
                    act.activation(xT[:, k, 2 * j:2 * j + 2, :], pair_ps(j)[:, k, :, :], ACT.Copy,
                                   scale=p2_n1[:, k:k + 1]).then_inc(s.hT, 1)
            act_split(2, 0)
            act_qkv()
            with act.Fori(0, B) as b:
                act_self(b)
            act_parts(s.z2T_ps, 0, s.h, lambda k: p2_n2s[:, k:k + 1], lambda k: p2_n2[:, k:k + 1], s.f)
            act.wait_ge(s.e, 1)
            act.activation(pr2[:, :, 0:E2], pr2[:, :, 0:E2], ACT.Exp).then_inc(s.t, 1)
            act.activation(sig, lg2[:, :, E2], ACT.Tanh, scale=0.5).then_inc(s.t, 1)

        def pool_pre2():
            x_ready(nc.gpsimd, 5)
            prime(pre[2].x2)
            pool_ln(5)
            pool_pow(pre[2].ms, 1, rms_r[:], rms_e[:], pre[2].r)
            me = own["pool"]
            me.link(nc.gpsimd, nc.gpsimd.memset(m_c, 0.0))
            nc.gpsimd.wait_ge(pre[2].qT, 2)
            pool_stage(0)
            with nc.gpsimd.Fori(1, B + 1) as b:
                pool_stage(b)
            pool_pow(pre[2].ssq, 1, rms_r[:], rms_e[:], pre[2].rr)
            nc.gpsimd.wait_ge(pre[2].lg, 2)

        def dve_pre2():
            dve, s, me = nc.vector, pre[2], own["dve"]
            dve_ln(5)
            dve_norm_ms(me, s.ms, s.r)
            for i in range(NT):
                dve.tensor_scalar(z[:, i, :], xn[:, i, :], rms_r[:, i:i + 1], None, ALU.mult).then_inc(s.z, 1)
            dve.wait_ge(s.w, 48)
            me.link(dve, dve.tensor_scalar(p2_n2s, p2_n2, SPLIT, None, ALU.mult))
            dve_split(2, 0)
            dve_qkv(me)
            for t in range(SA_AHEAD):
                dve_maxima(0, t)
            with dve.Fori(0, B) as b:
                me.open(b, 4)
                dve_self(b, me)
            me.close(B)
            for i in range(NT):
                ins = dve.scalar_tensor_tensor(p2_junk, xn[:, i, :], 1.0, xn[:, i, :], ALU.mult, ALU.mult,
                                               accum_out=p2_ssq[:, i:i + 1])
                me.link(dve, ins)
            dve.tensor_scalar(rms_e[:], p2_ssq, 1.0 / D, RMS_EPS, ALU.mult, ALU.add).then_inc(s.ssq, 1)
            dve.wait_ge(s.rr, 1)
            for i in range(NT):
                dve.tensor_scalar(z[:, i, :], xn[:, i, :], rms_r[:, i:i + 1], None, ALU.mult).then_inc(s.z2, 1)
            dve_parts(s.h, lambda k: p2_n2s[:, k:k + 1]).then_inc(s.gates, 1)
            dve.wait_ge(s.logit, 1)
            me.link(dve, dve.tensor_copy(tiles_of(lg2), logits_ps(E2 + 1)))
            me.link(dve, dve.memset(pr2[:, :, E2:E2 + 6], -1.0))
            dve_softmax_over(me, lg2[:, :, 0:E2], pr2[:, :, 0:E2], E2, s, E2)
            top_experts(me, pr2, 2, E2, ranked, rest2)
            me.link(dve, dve.tensor_scalar(gates[:, 0:4, :, 0:2].rearrange("p c t e -> p t c e"),
                                           rest2[:, :, 0:E2].rearrange("p t (c e) -> p t c e", c=4),
                                           0.5 * UNSPLIT * UNSPLIT, None, ALU.mult))
            dve.tensor_scalar(gates[:, 4, :, 0], sig, 1.0, 0.25 * UNSPLIT * UNSPLIT, ALU.add, ALU.mult).then_inc(s.lg, 1)
            dve.wait_ge(s.lg, 1)
            for c, e in ((4, 1), (5, 0), (5, 1)):
                ins = dve.tensor_copy(gates[:, c, :, e], gates[:, 4, :, 0])
            ins.then_inc(s.lg, 1)


        @block.sync
        def _(sp):
            sp.dma_start(ctx_t[:], d["ctx_t"]).then_inc(load.ctx, 16)
            sp.dma_start(x[:], d["x"].rearrange("t p c -> p t c")).then_inc(load.x, 16)
            sp.dma_start(ctx_d[:], d["ctx_d"]).then_inc(load.ctx, 16)
            sp_latent(0)
            for to, name in ((ident[:], "ident"), (causal_f, "causal"), (heads_c[:], "heads_c")):
                sp.dma_start(to, d[name]).then_inc(load.const, 16)
            sp.dma_start(rot_in[:, 0:3 * B * L], d["rotk"]).then_inc(load.rot, 16)
            sp_pre0()
            sp_first_chunk(0)
            sp_heads(1)
            sp_ffn(0)
            sp_folded(1)
            sp_first_chunk(1)
            sp_router(1, KT * (E1 + 1))
            sp_heads(2)
            sp_ffn(1)
            sp_folded(2)
            sp_pre2()
            sp_first_chunk(2)
            sp_ffn(2)
            sp_latent(3)
            sp_first_chunk(3)
            sp_router(3, KT * E3 + E3)
            sp_ffn(3)
            for i in range(NT):
                x_ready(sp, 8, i)
                sp.dma_start(out[i], x[:, i, :]).then_inc(load.out, 16)
            sp.wait_ge(load.out, 16 * NT)

        @block.tensor
        def _(pe):
            pe_latent(0)
            pe_pre0()
            pe_ffn(0)
            pe_folded(1)
            pe_pre1(1, r1_w, E1 + 1)
            pe_ffn(1)
            pe_folded(2)
            pe_pre2()
            pe_ffn(2)
            pe_latent(3)
            pe_pre1(3, r3_w, E3)
            pe_ffn(3)

        @block.scalar
        def _(act):
            act_latent(0)
            act_pre0()
            act_ffn(0)
            act_folded(1)
            act_pre1(1)
            act_ffn(1)
            act_folded(2)
            act_pre2()
            act_ffn(2)
            act_latent(3)
            act_pre3()
            act_ffn(3)

        @block.vector
        def _(dve):
            me = own["dve"]
            dve_latent(0)
            dve_pre0()
            dve_ffn(0)
            dve_folded(1)
            dve_pre1()
            dve_ffn(1)
            dve_folded(2)
            dve_pre2()
            dve_ffn(2)
            dve_latent(3)
            dve_pre3()
            dve_ffn(3)

        @block.gpsimd
        def _(pool):
            me = own["pool"]
            me.link(pool, pool.memset(half_neg[:], -0.5))
            pool_ln(0)
            pool_normalise(0)
            pool_pre0()
            pool_ffn(0)
            pool_folded(1)
            pool_pre1(1)
            pool_ffn(1)
            pool_folded(2)
            pool_pre2()
            pool_ffn(2)
            pool_ln(6)
            pool_normalise(3)
            pool_pre1(3)
            pool_ffn(3)



def rope_table(length, dim, base):
    inv = (np.float32(1.0) / np.float32(base) ** (np.arange(0, dim, 2, dtype=np.float32) / np.float32(dim))).astype(np.float32)
    return (np.arange(length, dtype=np.float32)[:, None] * inv[None, :]).astype(np.float32)


def constants():
    f = np.float32
    p = np.arange(P)
    out = {"ident": np.eye(P, dtype=f)}
    lat = np.where(np.arange(L)[None, :] > p[:, None], f(-1e30), f(0))
    own = np.where(np.arange(P)[None, :] > p[:, None], f(-1e30), f(0))
    causal = np.concatenate([np.tile(lat, (1, 8)), np.tile(own, (1, 2))], 1)
    out["causal"] = causal.astype(f)
    own_head = np.where(p[:, None] // HD == np.arange(HG)[None, :], f(HD ** -0.5), f(0))
    own_half = np.where(np.arange(D)[None, :] // HD % 2 == p[:, None] // L, f(1), f(0))
    parity = np.where(p[:, None] // HD % 2 == np.arange(2)[None, :], f(1), f(0))
    out["heads_c"] = np.concatenate([own_head, own_half, parity], 1).astype(f)
    a = rope_table(L, DC, 10000.0)
    cos, sin = (np.repeat(t(a), 2, axis=-1).T.astype(f) for t in (np.cos, np.sin))
    sin = np.concatenate([-sin[:DC // 2], sin[DC // 2:]])
    out["rot_k"] = np.concatenate([np.tile(cos, (2, B)), np.tile(sin, (2, B))], 1)
    a = rope_table(S, DCQ, 10000.0)
    cos, sin = (np.repeat(t(a), 2, axis=-1).T.astype(f) for t in (np.cos, np.sin))
    sin = np.concatenate([sin[DCQ // 2:], -sin[:DCQ // 2]])
    out["rope1"] = np.stack([np.tile(t, (2, 1)).reshape(3, P, S) for t in (cos, sin)]).transpose(2, 0, 1, 3).copy()
    a = rope_table(S, HD, 1000000.0)
    a = np.concatenate([a, a], -1)
    cos, sin = np.cos(a).astype(f), np.sin(a).astype(f)
    sin = np.concatenate([-sin[:, :HD // 2], sin[:, HD // 2:]], 1)
    scale = np.array([HD ** -0.5, 1.0], f)
    cs = [(t[:, None, :] * scale[None, :, None]).reshape(QT, P, 2 * HD).transpose(1, 0, 2).reshape(P, -1) for t in (cos, sin)]
    out["self_rope"] = np.concatenate(cs, 1)
    return out


def rows_on_partitions(w):
    k, n = w.shape
    return w.reshape(k // P, P, n).transpose(1, 0, 2).reshape(P, -1)


def wide(a, rows, cols):
    out = np.zeros((rows, cols), a.dtype)
    out[:a.shape[0], :a.shape[1]] = a
    return out


def chunk_layout(gate, up, down, cols, full):
    ups, downs = [], []
    for c in range(gate.shape[1] // cols):
        at = slice(c * cols, (c + 1) * cols)
        gu = np.stack([gate[:, at], up[:, at]], 1).reshape(KT, P, 2 * cols).transpose(1, 0, 2).reshape(P, -1)
        ups.append(wide(gu, P, 4 * full))
        tiles = [wide(down[at][k * P:k * P + rows], P, D) for k, rows in k_tiles(cols)]
        downs.append(wide(np.concatenate(tiles, 1), P, len(k_tiles(full)) * D))
    return ups, downs


def layouts(a):
    d, con = {}, constants()
    f = np.float32
    d["x"] = a["x"].reshape(NT, P, D)
    cx = a["ctx_512"].transpose(2, 0, 1)
    flat = cx.reshape(DC, B * L)
    d["ctx_t"] = np.concatenate([flat, flat], 0)
    d["ctx_d"] = np.stack([cx, cx], 2)
    swapped = np.concatenate([flat[DC // 2:], flat[:DC // 2]], 0)
    d["rotk"] = np.concatenate([con.pop("rot_k"), np.concatenate([swapped, swapped], 0)], 1)
    self_rope = con.pop("self_rope")
    d.update(con)
    for n in (0, 3):
        kv = wide(a[f"L{n}_xattn_Wkv_expand"].T, P, 2 * D)
        d[f"lat{n}"] = np.concatenate([rows_on_partitions(a[f"L{n}_xattn_Wq"].T), rows_on_partitions(a[f"L{n}_xattn_Wout"].T), kv], 1)
    for n in (1, 2):
        wq = a[f"L{n}_xattn_Wq"].reshape(H, P, D)
        wo = a[f"L{n}_xattn_Wo"].T.reshape(H, P, D)
        kcq, kv = a[f"L{n}_xattn_w_kc_q"], a[f"L{n}_xattn_w_kc_kv"]
        kr, qr = a[f"L{n}_xattn_W_kr"].transpose(0, 2, 1), a[f"L{n}_xattn_W_qr"].transpose(0, 2, 1)
        heads = np.zeros((H, P, HEAD_W), f)
        if n == 1:
            heads[:, :, 0:DCQ] = kcq
        else:
            t = kcq.transpose(0, 2, 1).reshape(H, 2, DCQ // 2, P).transpose(0, 2, 1, 3)
            heads[:, :DCQ // 2, 0:2 * P] = t.reshape(H, DCQ // 2, 2 * P)
        heads[:, :, 256:512] = wq
        heads[:, :, 512:576] = kv
        heads[:, :, 576:832] = wo
        heads[:, :R, 832:896] = kr
        heads[:, :R, 896:1088] = qr
        d[f"heads{n}"] = heads.reshape(PAIRS, 2, P, HEAD_W).transpose(0, 2, 1, 3)
    g = lambda name: a[f"L0_ffn_{name}"]
    d["pre0"] = np.concatenate([rows_on_partitions(g("wv").T), rows_on_partitions(g("wo"))], 1)
    cols = lambda v: v.reshape(KT, P).T
    d["vec0"] = np.concatenate([np.repeat(cols(g("bv"))[:, :, None], P, 2).reshape(P, -1), np.tile(g("w_router"), (P, 1)),
                                np.tile(g("b_router").reshape(1, 1), (P, 1)), cols(g("norm1_w")), cols(g("norm2_w"))], 1)
    up, down = chunk_layout(g("w_gate"), g("w_up"), g("w_down"), 352, 352)
    d["up0"], d["down0"] = np.stack(up), np.stack(down)
    g = lambda name: a[f"L1_ffn_{name}"]
    gu = g("gate_up_proj")
    flat = lambda w: w.transpose(2, 0, 1).reshape(D, -1)
    up, down = chunk_layout(flat(gu[:, :64]), flat(gu[:, 64:]), g("down_proj").transpose(0, 2, 1).reshape(-1, D), 512, 512)
    su, sd = chunk_layout(g("shared_gate_w").T, g("shared_up_w").T, g("shared_down_w").T, 64, 512)
    d["up1"], d["down1"] = np.stack(up + su), np.stack(down + sd)
    d["router1"] = rows_on_partitions(np.concatenate([g("router_w").T, g("shared_expert_gate_w").T], 1))
    g = lambda name: a[f"L2_ffn_{name}"]
    d["qkv2"] = rows_on_partitions(np.concatenate([g("wq"), g("wk"), g("wv")], 1))
    d["router2"] = np.concatenate([rows_on_partitions(g("wo")), rows_on_partitions(np.concatenate([g("w_router"), g("w_sh_eg")], 1))], 1)
    d["vec2"] = np.concatenate([np.tile(np.concatenate([g("bq"), g("bk"), g("bv")]), (P, 1)), self_rope,
                                cols(g("w_ln1")), cols(g("w_ln2"))], 1)
    wide_e = lambda w: w.transpose(1, 0, 2).reshape(D, -1)
    up, down = chunk_layout(wide_e(g("w_gate_e")), wide_e(g("w_up_e")), g("w_down_e").reshape(-1, D), 352, 352)
    su, sd = chunk_layout(g("w_sh_gate"), g("w_sh_up"), g("w_sh_down"), 352, 352)
    d["up2"], d["down2"] = np.stack(up + su), np.stack(down + sd)
    g = lambda name: a[f"L3_ffn_{name}"]
    up, down = chunk_layout(wide_e(g("w1_routed")), wide_e(g("w3_routed")), g("w2_routed").reshape(-1, D), 352, 352)
    su, sd = chunk_layout(g("w1_shared"), g("w3_shared"), g("w2_shared"), 176, 352)
    d["up3"], d["down3"] = np.stack(up + su), np.stack(down + sd)
    d["router3"] = np.concatenate([rows_on_partitions(g("gate_w").T), np.tile(g("gate_b"), (P, 1))], 1)
    return {k: np.ascontiguousarray(v) for k, v in d.items()}


def kernel(**inputs):
    import concourse.bacc as bacc
    from concourse.bass_utils import run_bass_kernel_spmd

    arrays = layouts({k: np.asarray(v) for k, v in inputs.items()})
    nc = bacc.Bacc("TRN2", target_bir_lowering=False, num_devices=1)
    d = {k: nc.dram_tensor(f"in_{k}", v.shape, mybir.dt.from_np(v.dtype), kind="ExternalInput").ap() for k, v in arrays.items()}
    out = nc.dram_tensor("out", (NT, P, D), F32, kind="ExternalOutput").ap()
    build(nc, d, out)
    r = run_bass_kernel_spmd(nc, [{f"in_{k}": v for k, v in arrays.items()}], core_ids=[0])
    return r.results[0]["out"].reshape(B, S, D)
```
